# Optimizing a Trainium2 kernel written in Bass

```python
import numpy as np
import jax
import jax.numpy as jnp

def _softmax(x, axis=-1):
    return jax.nn.softmax(x, axis=axis)

def _gelu(x):
    return jax.nn.gelu(x, approximate=True)

def _silu(x):
    return jax.nn.silu(x)

def _sigmoid(x):
    return jax.nn.sigmoid(x)

def _layernorm(x, axis=-1, eps=1e-05):
    m = jnp.mean(x, axis=axis, keepdims=True)
    v = jnp.var(x, axis=axis, keepdims=True)
    return (x - m) / jnp.sqrt(v + eps)

def _scatter_add(tgt, idx, src, axis=0):
    return tgt.at[idx].add(src)

def _segment_sum(src, seg, n):
    return jax.ops.segment_sum(src, seg, n)
kernel_name = 'mk_gnn_preln_d2_gnn_r64_d24205'

def setup_inputs(seed: int=0):
    np.random.seed(seed)
    _w = jnp.asarray

    def _rec_inputs():
        import jax
        import jax.numpy as jnp
        _gk = jax.random.key(seed)
        x = -0.000202 + 1 * jax.random.normal(jax.random.fold_in(_gk, 1), (50000, 64), jnp.float32)
        src = jax.random.randint(jax.random.fold_in(_gk, 2), (25000,), 0, 50000, jnp.int32)
        dst = jnp.minimum((50000 * jax.random.uniform(jax.random.fold_in(_gk, 3), (25000,)) ** 2.0).astype(jnp.int32), 49999)
        _o = jnp.argsort(dst, stable=True)
        src = src[_o]
        dst = dst[_o]
        edge_attr_64 = 4.59472e-05 + 1.00006 * jax.random.normal(jax.random.fold_in(_gk, 12), (25000, 64), jnp.float32)
        return (x, src, dst, edge_attr_64)
    x, src, dst, edge_attr_64 = _rec_inputs()

    def _L0_gnn_setup():
        import jax, jax.numpy as jnp
        import numpy as np
        N, E, B = (100000, 1250000, 16)
        D_NODE, D_EDGE, D_COND, D_HID, D_OUT = (64, 64, 16, 256, 64)
        key = jax.random.key(seed)
        ks = jax.random.split(key, 8)
        x = jax.random.normal(ks[0], (N, D_NODE), dtype=jnp.float32)
        edge_index = jax.random.randint(ks[1], (2, E), 0, N, dtype=jnp.int32)
        edge_attr = jax.random.normal(ks[2], (E, D_EDGE), dtype=jnp.float32)
        u = jax.random.normal(ks[3], (B, D_COND), dtype=jnp.float32)
        batch = jnp.sort(jax.random.randint(ks[4], (N,), 0, B, dtype=jnp.int32))
        d_in = D_NODE + D_EDGE + D_COND
        W1 = jax.random.normal(ks[5], (d_in, D_HID), dtype=jnp.float32) / np.sqrt(d_in)
        b1 = jnp.zeros((D_HID,), dtype=jnp.float32)
        W2 = jax.random.normal(ks[6], (D_HID, D_OUT), dtype=jnp.float32) / np.sqrt(D_HID)
        b2 = jnp.zeros((D_OUT,), dtype=jnp.float32)
        return {'x': x, 'edge_index': edge_index, 'edge_attr': edge_attr, 'u': u, 'batch': batch, 'W1': W1, 'b1': b1, 'W2': W2, 'b2': b2}
    _L0_gnn_all = _L0_gnn_setup()
    _L0_gnn_in = {k: v for k, v in _L0_gnn_all.items() if k in ('u', 'W1', 'b1', 'W2', 'b2')}
    del _L0_gnn_all

    def _L1_gnn_setup():
        import jax, jax.numpy as jnp
        import numpy as np
        NEG_SLOPE = 0.2

        def _gat_layer(x, src, dst, n_nodes, W, a_src, a_dst, b):
            h = x @ W
            alpha_s = h @ a_src
            alpha_d = h @ a_dst
            e = jax.nn.leaky_relu(alpha_s[src] + alpha_d[dst], NEG_SLOPE)
            m = jax.ops.segment_max(e, dst, num_segments=n_nodes)
            w = jnp.exp(e - m[dst])
            z = jax.ops.segment_sum(w, dst, num_segments=n_nodes)
            alpha = w / (z[dst] + 1e-16)
            out = jax.ops.segment_sum(alpha[:, None] * h[src], dst, num_segments=n_nodes)
            return out + b
        key = jax.random.key(seed)
        N, E, D_IN, D_H, D_OUT = (50000, 12500, 64, 64, 64)
        ks = jax.random.split(key, 12)
        x = jax.random.normal(ks[0], (N, D_IN), dtype=jnp.float32)
        edge_index = jax.random.randint(ks[1], (2, E), 0, N, dtype=jnp.int64)
        s = 1.0 / np.sqrt(D_IN)
        W1 = jax.random.normal(ks[2], (D_IN, D_H), dtype=jnp.float32) * s
        a_src1 = jax.random.normal(ks[3], (D_H,), dtype=jnp.float32) * s
        a_dst1 = jax.random.normal(ks[4], (D_H,), dtype=jnp.float32) * s
        b1 = jnp.zeros((D_H,), dtype=jnp.float32)
        s2 = 1.0 / np.sqrt(D_H)
        W2 = jax.random.normal(ks[5], (D_H, D_OUT), dtype=jnp.float32) * s2
        a_src2 = jax.random.normal(ks[6], (D_OUT,), dtype=jnp.float32) * s2
        a_dst2 = jax.random.normal(ks[7], (D_OUT,), dtype=jnp.float32) * s2
        b2 = jnp.zeros((D_OUT,), dtype=jnp.float32)
        return {'x': x, 'edge_index': edge_index, 'W1': W1, 'a_src1': a_src1, 'a_dst1': a_dst1, 'b1': b1, 'W2': W2, 'a_src2': a_src2, 'a_dst2': a_dst2, 'b2': b2}
    _L1_gnn_all = _L1_gnn_setup()
    _L1_gnn_in = {k: v for k, v in _L1_gnn_all.items() if k in ('W1', 'a_src1', 'a_dst1', 'b1', 'W2', 'a_src2', 'a_dst2', 'b2')}
    del _L1_gnn_all
    return {'x': x, 'src': src, 'dst': dst, 'edge_attr_64': edge_attr_64, 'L0_gnn_u': _L0_gnn_in['u'], 'L0_gnn_W1': _L0_gnn_in['W1'], 'L0_gnn_b1': _L0_gnn_in['b1'], 'L0_gnn_W2': _L0_gnn_in['W2'], 'L0_gnn_b2': _L0_gnn_in['b2'], 'L1_gnn_W1': _L1_gnn_in['W1'], 'L1_gnn_a_src1': _L1_gnn_in['a_src1'], 'L1_gnn_a_dst1': _L1_gnn_in['a_dst1'], 'L1_gnn_b1': _L1_gnn_in['b1'], 'L1_gnn_W2': _L1_gnn_in['W2'], 'L1_gnn_a_src2': _L1_gnn_in['a_src2'], 'L1_gnn_a_dst2': _L1_gnn_in['a_dst2'], 'L1_gnn_b2': _L1_gnn_in['b2']}

def reference(x, src, dst, edge_attr_64, L0_gnn_u, L0_gnn_W1, L0_gnn_b1, L0_gnn_W2, L0_gnn_b2, L1_gnn_W1, L1_gnn_a_src1, L1_gnn_a_dst1, L1_gnn_b1, L1_gnn_W2, L1_gnn_a_src2, L1_gnn_a_dst2, L1_gnn_b2):
    import jax
    import jax.numpy as jnp

    def _L0_gnn_ref(x, edge_index, edge_attr, u, batch, W1, b1, W2, b2):
        import jax, jax.numpy as jnp
        import numpy as np
        N, E, B = (100000, 1250000, 16)
        D_NODE, D_EDGE, D_COND, D_HID, D_OUT = (64, 64, 16, 256, 64)
        row = edge_index[0]
        agg = jax.ops.segment_sum(edge_attr, row, num_segments=x.shape[0])
        h = jnp.concatenate([x, agg, u[batch]], axis=1)
        h = jax.nn.relu(h @ W1 + b1)
        return h @ W2 + b2

    def _L1_gnn_ref(x, edge_index, W1, a_src1, a_dst1, b1, W2, a_src2, a_dst2, b2):
        import jax, jax.numpy as jnp
        import numpy as np
        NEG_SLOPE = 0.2

        def _gat_layer(x, src, dst, n_nodes, W, a_src, a_dst, b):
            h = x @ W
            alpha_s = h @ a_src
            alpha_d = h @ a_dst
            e = jax.nn.leaky_relu(alpha_s[src] + alpha_d[dst], NEG_SLOPE)
            m = jax.ops.segment_max(e, dst, num_segments=n_nodes)
            w = jnp.exp(e - m[dst])
            z = jax.ops.segment_sum(w, dst, num_segments=n_nodes)
            alpha = w / (z[dst] + 1e-16)
            out = jax.ops.segment_sum(alpha[:, None] * h[src], dst, num_segments=n_nodes)
            return out + b
        n_nodes = x.shape[0]
        loops = jnp.arange(n_nodes, dtype=edge_index.dtype)
        src = jnp.concatenate([edge_index[0], loops])
        dst = jnp.concatenate([edge_index[1], loops])
        h = _gat_layer(x, src, dst, n_nodes, W1, a_src1, a_dst1, b1)
        h = jax.nn.relu(h)
        out = _gat_layer(h, src, dst, n_nodes, W2, a_src2, a_dst2, b2)
        return out
    edge_index = jnp.stack([src, dst])
    batch0 = jnp.zeros((50000,), jnp.int32)
    h = jnp.maximum(_layernorm(x, axis=-1), 0.0)
    x = x + _L0_gnn_ref(h, edge_index, edge_attr_64, L0_gnn_u, batch0, L0_gnn_W1, L0_gnn_b1, L0_gnn_W2, L0_gnn_b2)
    h = jnp.maximum(_layernorm(x, axis=-1), 0.0)
    x = x + _L1_gnn_ref(h, edge_index, L1_gnn_W1, L1_gnn_a_src1, L1_gnn_a_dst1, L1_gnn_b1, L1_gnn_W2, L1_gnn_a_src2, L1_gnn_a_dst2, L1_gnn_b2)
    return x

_drawn_inputs = setup_inputs


def setup_inputs(seed=0):
    import zlib

    import numpy as np

    out = dict(_drawn_inputs(seed))
    spreads = {'L0_gnn_b1': (0.0, 0.1),
     'L0_gnn_b2': (0.0, 0.1),
     'L1_gnn_b1': (0.0, 0.1),
     'L1_gnn_b2': (0.0, 0.1)}
    factors = {'L1_gnn_a_dst1': 8.0, 'L1_gnn_a_src2': 3.782, 'L1_gnn_a_dst2': 8.0}
    for name, (base, spread) in spreads.items():
        noise = np.random.default_rng([zlib.crc32(name.encode()), seed]).standard_normal(out[name].shape)
        drawn = base * np.exp(spread * noise) if base else spread * noise
        out[name] = jnp.asarray(drawn.astype(out[name].dtype))
    for name, factor in factors.items():
        out[name] = (out[name] * factor).astype(out[name].dtype)
    return out
```

```python
from contextlib import ExitStack

import concourse.bass as bass
from concourse import mybir
from concourse.alu_op_type import AluOpType as ALU

F32 = mybir.dt.float32
BF16 = mybir.dt.bfloat16
I32 = mybir.dt.int32
ACT = mybir.ActivationFunctionType
AX = mybir.AxisListType

P = 128
BIG = 1.0e30
EPS = 1e-5
SLOPE = 0.2

N = 50000
E = 25000
D = 64
HID = 256
ROW = D + 2

J = 8
CH = P * J
CHUNKS = -(-N // CH)
LAST = N - CH
SHIFT = (CHUNKS - 1) * CH - LAST

EC = -(-E // P)
EPARTS = 4
EW = EC // EPARTS
FULLP = E // EC
RESTC = E - FULLP * EC

GT = 4
GE = P * GT
GROUPS = -(-E // GE)
LASTE = E - (GROUPS - 1) * GE
PADROW = N + GE
ZERO_DMAS = 12
AGG_ROWS = -(-(PADROW + 1) // (P * ZERO_DMAS)) * P * ZERO_DMAS
SKIP = 1 << 16


def wait(eng, sem, value):
    if isinstance(value, int) and value <= 0:
        return
    eng.wait_ge(sem, value)


def steps(eng, count, lead, unroll, body, tail):
    trips = (count - 1) // unroll
    for t in range(lead):
        body(t, t)
    with eng.Fori(lead // unroll, trips) as r:
        for b in range(unroll):
            body(r * unroll + b, b)
    for t in range(trips * unroll, count + tail):
        body(t, t)


def chunk_base(t):
    return min(t * CH, LAST) if isinstance(t, int) else t * CH


def flat(dram, start, rows, width):
    f = dram.rearrange("n c -> (n c)")
    return f[bass.ds(start * width, P * rows * width)].rearrange("(p f) -> p f", p=P)


class Mem:

    def __init__(self, nc, ctx, tag):
        self.nc, self.ctx, self.tag = nc, ctx, tag

    def sb(self, name, shape, dt=F32):
        return self.ctx.enter_context(self.nc.sbuf_tensor(f"{name}_{self.tag}", shape, dt))

    def ps(self, name, shape):
        return self.ctx.enter_context(self.nc.psum_tensor(f"{name}_{self.tag}", shape, F32))

    def sem(self, name):
        return self.ctx.enter_context(self.nc.semaphore(f"{name}_{self.tag}"))


def setup(nc, mem, con, W):
    with ExitStack() as ctx:
        tmp = Mem(nc, ctx, "setup")
        io392 = tmp.sb("io392", [P, J * CHUNKS], I32)
        dumi = tmp.sb("dumi", [P, GROUPS, GT], I32)
        piota = tmp.sb("piota", [P, 1], I32)
        ones = tmp.sb("ones", [P, P])
        srcc = tmp.sb("srcc", [P, GROUPS * GT], I32)
        di = tmp.sb("di", [P, EC + 2], I32)
        u0 = tmp.sb("u0", [16, 1])
        w1u = tmp.sb("w1u", [16, HID])
        b1c = tmp.sb("b1c", [P, 2])
        wst = tmp.sb("wst", [P, 2, D])
        wT = tmp.sb("wT", [D, 2, P])
        av = tmp.sb("av", [D, 2, 2])
        q = tmp.sb("q", [P, 12, EC])
        qi = tmp.sb("qi", [P, 6, EC], I32)
        hib = tmp.sb("hib", [P, EC], BF16)
        identb = tmp.sb("identb", [P, P], BF16)
        nend = tmp.sb("nend", [P, 4])
        ps_u = tmp.ps("ps_u", [P, 512])
        ps_w = tmp.ps("ps_w", [P, 512])
        ps_a = tmp.ps("ps_a", [P, 512])
        ps_f = tmp.ps("ps_f", [P, 512])
        ps_h = tmp.ps("ps_h", [P, 4, 4, P])
        sem = tmp.sem
        pooled, loaded, filled = sem("pooled"), sem("loaded"), sem("filled")
        edge_loaded, table_zeroed = sem("edge_loaded"), con["agg_zeroed"]
        dve_step, pe_step, act_step, onehot_made = sem("dve_step"), sem("pe_step"), sem("act_step"), sem("onehot_made")
        hi_spread = sem("hi_spread")
        zero_ready, diff_done = sem("zero_ready"), sem("diff_done")
        LOADS = 0

        ctx.enter_context(nc.allow_non_contiguous_dma(reason="a few hundred single keys, vectors as columns"))
        block = ctx.enter_context(nc.Block())

        @block.gpsimd
        def _(pool):
            nc.gpsimd.memset(con["zero"][:], 0.0).then_inc(zero_ready, 1)
            nc.gpsimd.memset(ones[:], 1.0).then_inc(filled, 1)
            nc.gpsimd.memset(con["bd1"][:], 0.0).then_inc(filled, 1)
            nc.gpsimd.memset(con["bd2"][:], 0.0).then_inc(filled, 1)
            nc.gpsimd.memset(di[:], N).then_inc(filled, 1)
            nc.gpsimd.memset(con["srcg"][:], 0).then_inc(filled, 1)
            nc.gpsimd.memset(srcc[:], PADROW).then_inc(filled, 1)
            nc.gpsimd.iota(io392[:], pattern=[[1, J * CHUNKS]], base=0, channel_multiplier=0).then_inc(filled, 1)
            nc.gpsimd.iota(dumi[:], pattern=[[0, GROUPS], [P, GT]], base=N, channel_multiplier=1).then_inc(filled, 1)
            nc.gpsimd.iota(piota[:], pattern=[[0, 1]], base=0, channel_multiplier=1).then_inc(filled, 1)
            pool.wait_ge(filled, 9)
            nc.gpsimd.affine_select(out=con["ident"][:], in_=ones[:], compare_op=ALU.is_equal, fill=0.0, base=0,
                                    pattern=[[1, P]], channel_multiplier=-1).then_inc(pooled, 1)
            nc.gpsimd.affine_select(out=con["later"][:], in_=ones[:], compare_op=ALU.is_gt, fill=0.0, base=0,
                                    pattern=[[1, P]], channel_multiplier=-1).then_inc(pooled, 1)
            nc.gpsimd.affine_select(out=con["earlier"][:], in_=ones[:], compare_op=ALU.is_gt, fill=0.0, base=0,
                                    pattern=[[-1, P]], channel_multiplier=1).then_inc(pooled, 1)
            nc.gpsimd.tensor_copy(con["iota"][:], io392[:]).then_inc(pooled, 1)
            nc.gpsimd.tensor_copy(con["dummy"][:], dumi[:].rearrange("p g i -> p (g i)")).then_inc(pooled, 1)
            nc.gpsimd.tensor_copy(con["pidx"][:], piota[:]).then_inc(pooled, 1)
            nc.gpsimd.memset(con["nzrows"][:], 0.0).then_inc(pooled, 1)
            pool.wait_ge(pooled, 7)
            nc.gpsimd.memset(con["nzrows"][:, :, ROW - 1:ROW], -BIG).then_inc(pooled, 1)

        n_w = 0

        @block.sync
        def _(sp):
            nonlocal n_w
            def load(dst, src):
                nonlocal n_w
                sp.dma_start(dst, src).then_inc(loaded, 16)
                n_w += 1
            sp.wait_ge(filled, 6)
            main = (GROUPS - 1) * GE
            src_g = W["src"][0:main].rearrange("(g p i) -> p g i", p=P, i=GT)
            sp.dma_start(srcc[:, 0:(GROUPS - 1) * GT].rearrange("p (g i) -> p g i", i=GT), src_g).then_inc(edge_loaded, 16)
            sp.dma_start(srcc[0:LASTE // GT, (GROUPS - 1) * GT:],
                         W["src"][main:E].rearrange("(p i) -> p i", i=GT)).then_inc(edge_loaded, 16)
            sp.dma_start(di[0:FULLP, 1:EC + 1], W["dst"][0:FULLP * EC].rearrange("(p c) -> p c", c=EC)).then_inc(edge_loaded, 16)
            sp.dma_start(di[FULLP:FULLP + 1, 1:RESTC + 1],
                         W["dst"][FULLP * EC:E].rearrange("(p c) -> p c", p=1)).then_inc(edge_loaded, 16)
            sp.dma_start(di[1:FULLP + 1, 0:1], W["dst"][0:FULLP * EC].rearrange("(p c) -> p c", c=EC)[:, EC - 1:EC]).then_inc(edge_loaded, 16)
            sp.dma_start(di[0:FULLP - 1, EC + 1:EC + 2],
                         W["dst"][EC:FULLP * EC].rearrange("(p c) -> p c", c=EC)[:, 0:1]).then_inc(edge_loaded, 16)
            sp.dma_start(di[FULLP - 1:FULLP, EC + 1:EC + 2],
                         W["dst"][FULLP * EC:FULLP * EC + 1].rearrange("(p c) -> p c", p=1)).then_inc(edge_loaded, 16)
            sp.dma_start(con["srcg"][0:FULLP, :], W["src"][0:FULLP * EC].rearrange("(p c) -> p c", c=EC)).then_inc(edge_loaded, 16)
            sp.dma_start(con["srcg"][FULLP:FULLP + 1, 0:RESTC],
                         W["src"][FULLP * EC:E].rearrange("(p c) -> p c", p=1)).then_inc(edge_loaded, 16)
            load(con["w1"][:], W["W1"][0:P, :])
            load(w1u[:], W["W1"][P:P + 16, :])
            load(u0[:], W["u"][0:1, :].rearrange("a c -> c a"))
            load(b1c[:], W["b1"].rearrange("(m p) -> p m", p=P))
            load(con["w2"][:], W["W2"].rearrange("(m p) n -> p m n", p=P))
            load(con["b2row"][:], W["b2"].partition_broadcast(P))
            load(con["gb2row"][:], W["gb2"].partition_broadcast(P))
            for l, (w, bd) in enumerate((("gW1", "bd1"), ("gW2", "bd2"))):
                for h in range(2):
                    load(wst[D * h:D * h + D, l, :], W[w])
                    load(con[bd][D * h:D * h + D, ROW * h:ROW * h + D], W[w])
                load(av[:, l, 0:1], W[f"as{l + 1}"].rearrange("(n o) -> n o", o=1))
                load(av[:, l, 1:2], W[f"ad{l + 1}"].rearrange("(n o) -> n o", o=1))
            for h in range(2):
                load(con["gb1col"][D * h:D * h + D, :], W["gb1"].rearrange("(n o) -> n o", o=1))

        @block.scalar
        def _(act):
            act.wait_ge(zero_ready, 1)
            rows = AGG_ROWS // P // ZERO_DMAS
            for k in range(ZERO_DMAS):
                act.dma_start(flat(W["agg"], k * P * rows, rows, D), con["zero"][:]).then_inc(table_zeroed, 16)

        @block.tensor
        def _(pe):
            pe.wait_ge(loaded, 16 * 21)
            pe.wait_ge(pooled, 1)
            for m in range(2):
                mm = nc.tensor.matmul(ps_u[:, m:m + 1], w1u[:, m * P:m * P + P], u0[:, :], start=True, stop=True)
            mm.then_inc(pe_step, 1)
            for l in range(2):
                mm = nc.tensor.transpose(ps_w[0:D, l * P:l * P + P], wst[:, l, :], con["ident"][:])
            mm.then_inc(pe_step, 1)
            pe.wait_ge(act_step, 2)
            for l in range(2):
                mm = nc.tensor.matmul(ps_a[:, 2 * l:2 * l + 2], wT[:, l, :], av[:, l, :], start=True, stop=True)
            mm.then_inc(pe_step, 1)
            pe.wait_ge(dve_step, 2)
            nc.tensor.matmul(ps_f[:, 0:P], q[:, 0, 0:1].to_broadcast([P, P]), con["ident"][:], start=True, stop=True)
            nc.tensor.matmul(ps_f[:, P:2 * P], q[:, 0, EC - 1:EC].to_broadcast([P, P]), con["ident"][:],
                             start=True, stop=True).then_inc(pe_step, 1)
            pe.wait_ge(onehot_made, 1)
            for c in range(0, EC, 4):
                if c >= 16:
                    pe.wait_ge(onehot_made, 1 + (c - 16) // 4 + 1)
                for k in range(4):
                    mm = nc.tensor.matmul(ps_h[:, c // 4 % 4, k, :], hib[:, c + k:c + k + 1].to_broadcast([P, P]), identb[:],
                                          start=True, stop=True)
                mm.then_inc(hi_spread, 1)

        @block.scalar
        def _(act):
            act.wait_ge(pe_step, 1)
            act.wait_ge(loaded, 16 * 21)
            for m in range(2):
                ins = nc.scalar.activation(con["hbias"][:, m:m + 1], ps_u[:, m:m + 1], ACT.Identity, bias=b1c[:, m:m + 1])
            ins.then_inc(act_step, 1)
            act.wait_ge(pe_step, 2)
            nc.scalar.copy(wT[:].rearrange("p l k -> p (l k)"), ps_w[0:D, 0:2 * P]).then_inc(act_step, 1)
            act.wait_ge(pe_step, 3)
            for l, bd in enumerate(("bd1", "bd2")):
                for h in range(2):
                    ins = nc.scalar.copy(con[bd][D * h:D * h + D, ROW * h + D:ROW * h + ROW],
                                         ps_a[D * h:D * h + D, 2 * l:2 * l + 2])
            ins.then_inc(act_step, 1)

        @block.vector
        def _(dve):
            count = [0]

            def link(ins):
                count[0] += 1
                ins.then_inc(dve_step, 1)
                dve.wait_ge(dve_step, count[0])

            dve.wait_ge(edge_loaded, 16 * 9)
            dve.wait_ge(pooled, 8)
            d = di[:, 1:EC + 1]
            key, prv, nxt, t0, t1, same, endf, lead, t2 = (q[:, k, :] for k in range(9))
            link(nc.vector.tensor_copy(key, d))
            link(nc.vector.tensor_copy(con["lastkey"][:], key[:, EC - 1:EC]))
            link(nc.vector.tensor_copy(prv, di[:, 0:EC]))
            link(nc.vector.tensor_copy(nxt, di[:, 2:EC + 2]))
            link(nc.vector.tensor_tensor(same, key, prv, ALU.is_equal))
            link(nc.vector.tensor_tensor(endf, key, nxt, ALU.not_equal))
            link(nc.vector.memset(t0, 1.0))
            link(nc.vector.memset(t0[:, 0:1], 0.0))
            link(nc.vector.tensor_tensor(con["same"][:], same, t0, ALU.mult))
            link(nc.vector.tensor_scalar(con["cut"][:], con["same"][:], BIG, -BIG, ALU.mult, ALU.add))
            link(nc.vector.tensor_tensor(t1[:, 0:1], prv[:, 0:1], con["pidx"][:], ALU.add))
            link(nc.vector.tensor_scalar(t1[:, 1:2], con["pidx"][:], 0.5, None, ALU.is_ge))
            link(nc.vector.tensor_scalar(lead, key, prv[:, 0:1], t1[:, 1:2], ALU.is_equal, ALU.mult))
            link(nc.vector.tensor_tensor(con["leadend"][:], lead, endf, ALU.mult))
            link(nc.vector.tensor_tensor(t2, endf, con["leadend"][:], ALU.subtract))
            link(nc.vector.tensor_scalar(t0, t2, -float(SKIP), float(SKIP), ALU.mult, ALU.add))
            link(nc.vector.tensor_tensor(con["rowidx"][:], t0, key, ALU.add))
            link(nc.vector.tensor_reduce(nend[:, 0:1], con["leadend"][:], AX.X, ALU.add))
            link(nc.vector.tensor_scalar(nend[:, 1:2], nend[:, 0:1], -float(SKIP), float(SKIP), ALU.mult, ALU.add))
            link(nc.vector.tensor_tensor(con["leadidx"][:], nend[:, 1:2], key[:, 0:1], ALU.add))
            link(nc.vector.tensor_scalar(t0, key, float((CHUNKS - 1) * CH), float(SHIFT), ALU.is_ge, ALU.mult))
            link(nc.vector.tensor_tensor(qi[:, 0, :], t0, key, ALU.add))
            link(nc.vector.tensor_scalar(qi[:, 1, :], qi[:, 0, :], J.bit_length() - 1, P - 1,
                                         ALU.logical_shift_right, ALU.bitwise_and))
            link(nc.vector.tensor_scalar(qi[:, 2, :], qi[:, 0, :], CH.bit_length() - 1, J.bit_length() - 1,
                                         ALU.logical_shift_right, ALU.logical_shift_left))
            link(nc.vector.tensor_scalar(qi[:, 3, :], qi[:, 0, :], J - 1, None, ALU.bitwise_and))
            link(nc.vector.tensor_tensor(con["lo"][:], qi[:, 2, :], qi[:, 3, :], ALU.add))
            link(nc.vector.tensor_copy(identb[:], con["ident"][:]))
            nc.vector.tensor_copy(hib[:], qi[:, 1, :]).then_inc(onehot_made, 1)
            dve.wait_ge(pe_step, 4)
            link(nc.vector.tensor_scalar(con["joins"][:], ps_f[:, P:2 * P], key[:, 0:1], None, ALU.is_equal))
            link(nc.vector.tensor_tensor(con["joins"][:], con["joins"][:], con["earlier"][:], ALU.mult))
            link(nc.vector.tensor_scalar(con["nojoin"][:], con["joins"][:], BIG, -BIG, ALU.mult, ALU.add))
            link(nc.vector.tensor_copy(con["srckey"][:], srcc[:]))
            link(nc.vector.tensor_tensor(con["dumdiff"][:], con["dummy"][:], con["srckey"][:], ALU.subtract))
            for c in range(0, EC, 4):
                dve.wait_ge(hi_spread, c // 4 + 1)
                nc.vector.tensor_scalar(con["onehot"][:, c:c + 4, :], ps_h[:, c // 4 % 4], con["pidx"][:, 0:1], None,
                                        ALU.is_equal).then_inc(onehot_made, 1)


def sum_edges(nc, con, W):
    with ExitStack() as ctx:
        tmp = Mem(nc, ctx, "agg")
        krow = tmp.sb("krow", [P, 2, GE], I32)
        ea = tmp.sb("ea", [P, 2, GT, D])
        eq = tmp.sb("eq", [P, 2, GT, GT, P])
        diag = tmp.sb("diag", [P, 2, GT, P])
        onec = tmp.sb("onec", [P, 1])
        tot = tmp.sb("tot", [P, 2, GT, D])
        away = tmp.sb("away", [P, 2, GT])
        idx = tmp.sb("idx", [P, 2, GT], I32)
        ps_t = [tmp.ps(f"ps_t{b}", [P, GT, P]) for b in range(2)]
        ps_d = [tmp.ps(f"ps_d{b}", [P, 512]) for b in range(2)]
        sem = tmp.sem
        keys_in, attr_in = [sem("keys_in0"), sem("keys_in1")], [sem("attr_in0"), sem("attr_in1")]
        padded, eq_built, diag_built, ones_set = sem("padded"), sem("eq_built"), sem("diag_built"), sem("ones_set")
        summed, counted = sem("summed"), sem("counted")
        sums_out, away_out, idx_out = sem("sums_out"), sem("away_out"), sem("idx_out")
        added = sem("added")
        block = ctx.enter_context(nc.Block())
        attr = W["ea"].rearrange("n c -> (n c)")

        def groups(eng, body):
            steps(eng, GROUPS, 2, 2, body, 0)

        @block.sync
        def _(sp):
            def body(g, b):
                b %= 2
                wait(sp, diag_built, g - 1)
                if not isinstance(g, int) or g < GROUPS - 1:
                    sp.dma_start(krow[:, b], W["src"][bass.ds(g * GE, GE)].partition_broadcast(P)).then_inc(keys_in[b], 16)
                else:
                    wait(sp, padded, 2)
                    sp.dma_start(krow[:, b, 0:LASTE], W["src"][E - LASTE:E].partition_broadcast(P)).then_inc(keys_in[b], 16)
                wait(sp, summed, g - 1)
                if not isinstance(g, int) or g < GROUPS - 1:
                    sp.dma_start(ea[:, b].rearrange("p i c -> p (i c)"),
                                 attr[bass.ds(g * GE * D, GE * D)].rearrange("(p f) -> p f", p=P)).then_inc(attr_in[b], 16)
                else:
                    sp.dma_start(ea[0:LASTE // GT, b].rearrange("p i c -> p (i c)"),
                                 attr[(E - LASTE) * D:E * D].rearrange("(p f) -> p f", f=GT * D)).then_inc(attr_in[b], 16)
            groups(sp, body)

        @block.vector
        def _(dve):
            nc.vector.memset(onec[:], 1.0).then_inc(ones_set, 1)

            def indices(g, b):
                dve.wait_ge(counted, g + 1)
                wait(dve, idx_out, g - 1)
                nc.vector.scalar_tensor_tensor(out=away[:, b], in0=ps_d[b][:, 0:GT], scalar=0.5,
                                               in1=con["dumdiff"][:, bass.ds(g * GT, GT)], op0=ALU.is_ge,
                                               op1=ALU.mult).then_inc(away_out, 1)
                dve.wait_ge(away_out, g + 1)
                wait(dve, added, 16 * GT * (g - 1))
                nc.vector.tensor_tensor(idx[:, b], away[:, b], con["srckey"][:, bass.ds(g * GT, GT)],
                                        ALU.add).then_inc(idx_out, 1)

            def body(g, b):
                b %= 2
                if isinstance(g, int) and g == GROUPS - 1:
                    dve.wait_ge(diag_built, g - 1)
                    dve.wait_ge(summed, g - 1)
                    nc.vector.memset(krow[:, b], PADROW).then_inc(padded, 1)
                    nc.vector.memset(ea[:, b], 0.0).then_inc(padded, 1)
                if not isinstance(g, int) or g < GROUPS:
                    dve.wait_ge(keys_in[b], 16 * (g // 2 + 1) if isinstance(g, int) else 8 * (g - b) + 16)
                    wait(dve, counted, g - 1)
                    for j in range(GT):
                        nc.vector.tensor_scalar(eq[:, b, j], krow[:, b].rearrange("p (m i) -> p i m", i=GT),
                                                con["srckey"][:, bass.ds(g * GT + j, 1)], None,
                                                ALU.is_equal).then_inc(eq_built, 1)
                    dve.wait_ge(eq_built, GT * (g + 1))
                    nc.vector.tensor_tensor(diag[:, b], eq[:, b].rearrange("p j i m -> p (j i) m")[:, ::GT + 1, :],
                                            con["later"][:].unsqueeze(1).to_broadcast([P, GT, P]),
                                            ALU.mult).then_inc(diag_built, 1)
                if not isinstance(g, int) or g >= 1:
                    indices(g - 1, 1 - b)
            steps(dve, GROUPS, 2, 2, body, 1)

        @block.tensor
        def _(pe):
            pe.wait_ge(ones_set, 1)

            def body(g, b):
                b %= 2
                pe.wait_ge(attr_in[b], 16 * (g // 2 + 1) if isinstance(g, int) else 8 * (g - b) + 16)
                pe.wait_ge(diag_built, g + 1)
                wait(pe, sums_out, g - 1)
                for i in range(GT):
                    for j in range(GT):
                        mm = nc.tensor.matmul(ps_t[b][:, i, 0:D], eq[:, b, j, i], ea[:, b, j],
                                              start=(j == 0), stop=(j == GT - 1))
                mm.then_inc(summed, 1)
                wait(pe, away_out, g - 1)
                for i in range(GT):
                    for j in range(i + 1):
                        mm = nc.tensor.matmul(ps_d[b][:, i:i + 1], diag[:, b, i] if j == i else eq[:, b, j, i], onec[:],
                                              start=(j == 0), stop=(j == i))
                mm.then_inc(counted, 1)
            groups(pe, body)

        @block.scalar
        def _(act):
            def body(g, b):
                b %= 2
                act.wait_ge(summed, g + 1)
                wait(act, added, 16 * GT * (g - 1))
                nc.scalar.copy(tot[:, b], ps_t[b][:, :, 0:D]).then_inc(sums_out, 1)
            groups(act, body)

        @block.gpsimd
        def _(pool):
            pool.wait_ge(con["agg_zeroed"], 16 * ZERO_DMAS)

            def body(g, b):
                b %= 2
                pool.wait_ge(sums_out, g + 1)
                pool.wait_ge(idx_out, g + 1)
                wait(pool, added, 16 * GT * g)
                pool.nop(nofuse=True)
                for i in range(GT):
                    nc.gpsimd.indirect_dma_start(
                        out=W["agg"], out_offset=bass.IndirectOffsetOnAxis(ap=idx[:, b, i:i + 1], axis=0),
                        in_=tot[:, b, i], in_offset=None, compute_op=ALU.add).then_inc(added, 16)
            groups(pool, body)
            pool.wait_ge(added, 16 * GT * GROUPS)


def mlp(nc, con, W):
    with ExitStack() as ctx:
        tmp = Mem(nc, ctx, "mlp")
        NX = 4
        xt = tmp.sb("xt", [P, NX, J, D])
        xb = tmp.sb("xb", [P, NX, J, D])
        xc = tmp.sb("xc", [P, 2, J, D])
        sq = tmp.sb("sq", [P, J, D])
        hx = tmp.sb("hx", [P, 2, J, 2 * D])
        hxT = tmp.sb("hxT", [P, 2, CH])
        hid = tmp.sb("hid", [P, 2, 2, CH])
        x1 = tmp.sb("x1", [P, 2, J, D])
        x1o = tmp.sb("x1o", [P, 2, J, D])
        yc = tmp.sb("yc", [P, 2, J, D])
        sqy = tmp.sb("sqy", [P, J, D])
        h1 = tmp.sb("h1", [P, 2, J, D])
        h1T = tmp.sb("h1T", [P, CH // 2])
        tt = tmp.sb("tt", [P, 2, J, ROW])
        st = tmp.sb("st", [P, 2, 5, J])
        eps = tmp.sb("eps", [P, 1])
        invd = tmp.sb("invd", [P, J])
        ps_x = tmp.ps("ps_x", [P, J, P])
        ps_h = [tmp.ps(f"ps_h{m}", [P, 512]) for m in range(2)]
        ps_o = tmp.ps("ps_o", [P, J, D])
        ps_n = tmp.ps("ps_n", [P, 4, P])
        ps_t = tmp.ps("ps_t", [P, 4, 256])
        sem = tmp.sem
        x_in = [sem(f"x_in{k}") for k in range(NX)]
        agg_in = [sem(f"agg_in{k}") for k in range(2)]
        x1_saved = [sem(f"x1_saved{k}") for k in range(2)]
        t_saved = [sem(f"t_saved{k}") for k in range(2)]
        invd_set = sem("invd_set")
        (eps_set, x_sum, x_mean, x_centred, x_square, x_var, x_dev, x_inv, h_ready, xb_ready,
         hx_turned, hxT_out, hid_done, hid_out, mlp_done, x1_ready, x1o_ready,
         y_sum, y_mean, y_centred, y_square, y_var, y_dev, y_inv, y_ready,
         y_turned, yT_out, t_done, t_out, ad_out) = (sem(n) for n in (
            "eps_set", "x_sum", "x_mean", "x_centred", "x_square", "x_var", "x_dev", "x_inv", "h_ready", "xb_ready",
            "hx_turned", "hxT_out", "hid_done", "hid_out", "mlp_done", "x1_ready", "x1o_ready",
            "y_sum", "y_mean", "y_centred", "y_square", "y_var", "y_dev", "y_inv", "y_ready",
            "y_turned", "yT_out", "t_done", "t_out", "ad_out"))
        block = ctx.enter_context(nc.Block())

        def bc(v):
            return v.unsqueeze(2).to_broadcast([P, J, D])

        def within(t):
            return not isinstance(t, int) or 0 <= t < CHUNKS

        def run(eng, body):
            steps(eng, CHUNKS, 4, 4, body, 2)

        @block.sync
        def _(sp):
            def body(s, k):
                if within(s):
                    wait(sp, xb_ready, s - 3)
                    wait(sp, x_centred, s - 3)
                    sp.dma_start(xt[:, k % 4].rearrange("p j c -> p (j c)"),
                                 flat(W["x"], chunk_base(s), J, D)).then_inc(x_in[k % 4], 16)
                    wait(sp, hx_turned, 2 * (s - 1))
                    aggr = W["agg"].rearrange("n c -> (n c)")[bass.ds(chunk_base(s) * D, CH * D)]
                    sp.dma_start(hx[:, k % 2, :, D:2 * D],
                                 aggr.rearrange("(p j c) -> p j c", p=P, j=J)).then_inc(agg_in[k % 2], 16)
                t = s - 2
                if within(t):
                    if isinstance(t, int) and t == CHUNKS - 1:
                        sp.wait_ge(x1_saved[1 - t % 2], 16 * (CHUNKS // 2))
                        sp.wait_ge(t_saved[1 - t % 2], 16 * (CHUNKS // 2))
                    sp.wait_ge(x1o_ready, t + 1)
                    sp.dma_start(flat(W["x1"], chunk_base(t), J, D),
                                 x1o[:, k % 2].rearrange("p j c -> p (j c)")).then_inc(x1_saved[k % 2], 16)
                    sp.wait_ge(t_out, t + 1)
                    sp.dma_start(flat(W["tab"], chunk_base(t), J, ROW),
                                 tt[:, k % 2].rearrange("p j c -> p (j c)")).then_inc(t_saved[k % 2], 16)
            run(sp, body)
            for k in range(2):
                sp.wait_ge(x1_saved[k], 16 * ((CHUNKS + 1 - k) // 2))
                sp.wait_ge(t_saved[k], 16 * ((CHUNKS + 1 - k) // 2))

        def sems16(t, k, every):
            return 16 * (t // every + 1) if isinstance(t, int) else (16 // every) * (t - k % every) + 16

        @block.vector
        def _(dve):
            nc.vector.memset(eps[:], EPS).then_inc(eps_set, 1)

            def body(s, k):
                t = s - 2
                b, c = k % 2, k % 2
                if within(t):
                    dve.wait_ge(mlp_done, t + 1)
                    dve.wait_ge(xb_ready, t + 1)
                    wait(dve, y_centred, t - 1)
                    wait(dve, x1o_ready, t - 1)
                    nc.vector.tensor_tensor(x1[:, c], ps_o[:], xb[:, (k - 2) % 4], ALU.add).then_inc(x1_ready, 1)
                    dve.wait_ge(x1_ready, t + 1)
                    wait(dve, y_mean, t)
                    nc.vector.tensor_reduce(st[:, 1, 0], x1[:, c], AX.X, ALU.add).then_inc(y_sum, 1)
                if within(s):
                    dve.wait_ge(x_in[k % 4], sems16(s, k, 4))
                    wait(dve, x_mean, s)
                    nc.vector.tensor_reduce(st[:, 0, 0], xt[:, k % 4], AX.X, ALU.add).then_inc(x_sum, 1)
                if within(t):
                    dve.wait_ge(y_square, t + 1)
                    wait(dve, y_dev, t)
                    nc.vector.tensor_reduce(st[:, 1, 2], sqy[:], AX.X, ALU.add).then_inc(y_var, 1)
                if within(s):
                    dve.wait_ge(x_square, s + 1)
                    wait(dve, x_dev, s)
                    nc.vector.tensor_reduce(st[:, 0, 2], sq[:], AX.X, ALU.add).then_inc(x_var, 1)
                if within(t):
                    dve.wait_ge(y_dev, t + 1)
                    wait(dve, y_ready, t)
                    nc.vector.reciprocal(st[:, 1, 4], st[:, 1, 3]).then_inc(y_inv, 1)
                    dve.wait_ge(y_inv, t + 1)
                    wait(dve, y_turned, t - 1)
                    nc.vector.scalar_tensor_tensor(out=h1[:, c], in0=yc[:, c], scalar=0.0, in1=bc(st[:, 1, 4]),
                                                   op0=ALU.max, op1=ALU.mult).then_inc(y_ready, 1)
                if within(s):
                    dve.wait_ge(x_dev, s + 1)
                    wait(dve, h_ready, s)
                    nc.vector.reciprocal(st[:, 0, 4], st[:, 0, 3]).then_inc(x_inv, 1)
                    dve.wait_ge(x_inv, s + 1)
                    wait(dve, hx_turned, 2 * (s - 1))
                    nc.vector.scalar_tensor_tensor(out=hx[:, b, :, 0:D], in0=xc[:, b], scalar=0.0, in1=bc(st[:, 0, 4]),
                                                   op0=ALU.max, op1=ALU.mult).then_inc(h_ready, 1)
            run(dve, body)

        @block.gpsimd
        def _(pool):
            nc.gpsimd.memset(invd[:], 1.0 / D).then_inc(invd_set, 1)
            pool.wait_ge(invd_set, 1)

            def body(s, k):
                t = s - 2
                b = k % 2
                if within(t):
                    pool.wait_ge(y_sum, t + 1)
                    wait(pool, y_centred, t)
                    nc.gpsimd.tensor_tensor(st[:, 1, 1], st[:, 1, 0], invd[:], ALU.mult).then_inc(y_mean, 1)
                    pool.wait_ge(y_mean, t + 1)
                    wait(pool, y_ready, t - 1)
                    nc.gpsimd.tensor_tensor(yc[:, b], x1[:, b], bc(st[:, 1, 1]), ALU.subtract).then_inc(y_centred, 1)
                if within(s):
                    pool.wait_ge(x_sum, s + 1)
                    wait(pool, x_centred, s)
                    nc.gpsimd.tensor_tensor(st[:, 0, 1], st[:, 0, 0], invd[:], ALU.mult).then_inc(x_mean, 1)
                    pool.wait_ge(x_mean, s + 1)
                    wait(pool, h_ready, s - 1)
                    nc.gpsimd.tensor_tensor(xc[:, b], xt[:, k % 4], bc(st[:, 0, 1]), ALU.subtract).then_inc(x_centred, 1)
                    wait(pool, x1_ready, s - 3)
                    nc.gpsimd.tensor_tensor(xb[:, k % 4], xt[:, k % 4], con["b2row"][:].unsqueeze(1).to_broadcast([P, J, D]),
                                            ALU.add).then_inc(xb_ready, 1)
                if within(t):
                    wait(pool, x1_saved[b], 16 * (t // 2) if isinstance(t, int) else 8 * (t - b))
                    nc.gpsimd.tensor_tensor(x1o[:, b], x1[:, b], con["gb2row"][:].unsqueeze(1).to_broadcast([P, J, D]),
                                            ALU.add).then_inc(x1o_ready, 1)
            run(pool, body)

        @block.scalar
        def _(act):
            act.wait_ge(eps_set, 1)

            def body(s, k):
                r, t = s - 1, s - 2
                b = k % 2
                rb = (k - 1) % 2

                def relu(n, m):
                    act.wait_ge(hid_done, 4 * r + 2 * n + m + 1)
                    if (n, m) == (0, 0):
                        wait(act, mlp_done, r - 1)
                    nc.scalar.activation(hid[:, rb, m, n * 512:n * 512 + 512], ps_h[m][:], ACT.Relu,
                                         bias=con["hbias"][:, m:m + 1]).then_inc(hid_out, 1)

                if within(r):
                    for h in range(2):
                        act.wait_ge(hx_turned, 2 * r + h + 1)
                        wait(act, hid_done, 4 * (r - 1))
                        nc.scalar.copy(hxT[:, rb, h * 512:h * 512 + 512],
                                       ps_x[:, 4 * h:4 * h + 4]).then_inc(hxT_out, 1)
                if within(t):
                    act.wait_ge(y_centred, t + 1)
                    wait(act, y_var, t)
                    nc.scalar.activation(sqy[:], yc[:, b], ACT.Square).then_inc(y_square, 1)
                if within(r):
                    relu(0, 0)
                if within(s):
                    act.wait_ge(x_centred, s + 1)
                    wait(act, x_var, s)
                    nc.scalar.activation(sq[:], xc[:, b], ACT.Square).then_inc(x_square, 1)
                if within(r):
                    relu(0, 1)
                if within(t):
                    act.wait_ge(y_var, t + 1)
                    wait(act, y_inv, t)
                    nc.scalar.activation(st[:, 1, 3], st[:, 1, 2], ACT.Sqrt, scale=1.0 / D, bias=eps[:, 0:1]).then_inc(y_dev, 1)
                if within(r):
                    relu(1, 0)
                if within(s):
                    act.wait_ge(x_var, s + 1)
                    wait(act, x_inv, s)
                    nc.scalar.activation(st[:, 0, 3], st[:, 0, 2], ACT.Sqrt, scale=1.0 / D, bias=eps[:, 0:1]).then_inc(x_dev, 1)
                if within(r):
                    relu(1, 1)
                if within(t):
                    act.wait_ge(y_turned, t + 1)
                    wait(act, t_done, t)
                    nc.scalar.copy(h1T[:], ps_n[:]).then_inc(yT_out, 1)
                    act.wait_ge(t_done, t + 1)
                    wait(act, t_saved[b], 16 * (t // 2) if isinstance(t, int) else 8 * (t - b))
                    nc.scalar.copy(tt[:, b].rearrange("p (a v) c -> p a (v c)", v=2),
                                   ps_t[:, :, 0:2 * ROW]).then_inc(t_out, 1)
                    nc.scalar.copy(con["ad"][:, bass.ds(t * J, J)].rearrange("p (a v) -> p a v", v=2),
                                   ps_t[:, :, D + 1:2 * ROW:ROW]).then_inc(ad_out, 1)
            run(act, body)

        @block.tensor
        def _(pe):
            def body(s, k):
                r, t = s - 1, s - 2
                b = k % 2
                rb = (k - 1) % 2
                if within(r):
                    pe.wait_ge(h_ready, r + 1)
                    pe.wait_ge(agg_in[rb], sems16(r, k - 1, 2))
                    for j in range(J):
                        if j % 4 == 0:
                            wait(pe, hxT_out, 2 * (r - 1) + j // 4 + 1)
                        mm = nc.tensor.transpose(ps_x[:, j, :], hx[:, rb, j, :], con["ident"][:])
                        if j % 4 == 3:
                            mm.then_inc(hx_turned, 1)
                    for n in range(2):
                        pe.wait_ge(hxT_out, 2 * r + n + 1)
                        for m in range(2):
                            wait(pe, hid_out, 4 * r + 2 * n + m - 1)
                            nc.tensor.matmul(ps_h[m][:], con["w1"][:, m * P:m * P + P],
                                             hxT[:, rb, n * 512:n * 512 + 512], start=True, stop=True).then_inc(hid_done, 1)
                    for j in range(J):
                        if j == 0:
                            wait(pe, x1_ready, r)
                        if j % 4 == 0:
                            pe.wait_ge(hid_out, 4 * r + j // 4 * 2 + 2)
                        for m in range(2):
                            mm = nc.tensor.matmul(ps_o[:, j, :], hid[:, rb, m, j * P:j * P + P], con["w2"][:, m, :],
                                                  start=(m == 0), stop=(m == 1))
                    mm.then_inc(mlp_done, 1)
                if within(t):
                    pe.wait_ge(y_ready, t + 1)
                    wait(pe, yT_out, t)
                    for a in range(4):
                        mm = nc.tensor.transpose(ps_n[:, a, :], h1[:, b, 2 * a:2 * a + 2].rearrange("p j c -> p (j c)"),
                                                 con["ident"][:])
                    mm.then_inc(y_turned, 1)
                    pe.wait_ge(yT_out, t + 1)
                    wait(pe, ad_out, t)
                    for a in range(4):
                        mm = nc.tensor.matmul(ps_t[:, a, 0:2 * ROW], h1T[:, a * P:a * P + P], con["bd1"][:],
                                              start=True, stop=True)
                    mm.then_inc(t_done, 1)
            run(pe, body)


def edge_attention(nc, con, W, tag):
    with ExitStack() as ctx:
        tmp = Mem(nc, ctx, tag)
        F = tmp.sb("F", [P, EC, ROW])
        parts = tmp.sb("parts", [P, 3, J * CHUNKS], BF16)
        rest = tmp.sb("rest", [P, 2, J * CHUNKS])
        pick = tmp.sb("pick", [P, J * CHUNKS])
        ade = tmp.sb("ade", [P, EC])
        sc = tmp.sb("sc", [P, 6, EW])
        m = tmp.sb("m", [P, EC + 1])
        prod = tmp.sb("prod", [P, EW, ROW])
        selp = tmp.sb("selp", [P, EPARTS, ROW])
        sel = tmp.sb("sel", [P, ROW])
        val = tmp.sb("val", [P, 2, P])
        wT = tmp.sb("wT", [P, P])
        sm = tmp.sb("sm", [P, 8])
        car = tmp.sb("car", [P, ROW])
        orow = tmp.sb("orow", [P, ROW])
        NB = 4
        ps_g = [tmp.ps(f"ps_g{k}", [P, 512]) for k in range(NB)]
        ps_m, ps_w, ps_c = (tmp.ps(n, [P, 512]) for n in ("ps_m", "ps_w", "ps_c"))
        sem = tmp.sem
        split, fetched, picked = sem("split"), sem("fetched"), sem("picked")
        gathered = [sem(f"gathered{k}") for k in range(EPARTS)]
        nz_set, scored, maxed, differ, powers, rows_done = (sem(n) for n in (
            "nz_set", "scored", "maxed", "differ", "powers", "rows_done"))
        dve_step, scattered, joined = sem("dve_step"), sem("scattered"), sem("joined")
        join_pe, join_act, lead_ready, lead_saved = sem("join_pe"), sem("join_act"), sem("lead_ready"), sem("lead_saved")
        block = ctx.enter_context(nc.Block())
        NZ_DMAS = 14
        nz_rows = CHUNKS * J // NZ_DMAS

        @block.sync
        def _(sp):
            for k in range(NZ_DMAS):
                sp.dma_start(flat(W["nz"], k * P * nz_rows, nz_rows, ROW),
                             con["nzrows"][:].rearrange("p r c -> p (r c)")).then_inc(nz_set, 16)

        @block.gpsimd
        def _(pool):
            for c in range(EC):
                nc.gpsimd.indirect_dma_start(
                    out=F[:, c, :], out_offset=None, in_=W["tab"],
                    in_offset=bass.IndirectOffsetOnAxis(ap=con["srcg"][:, c:c + 1], axis=0)).then_inc(gathered[c // EW], 16)
            pool.wait_ge(nz_set, 16 * NZ_DMAS)
            for c in range(EC):
                if c % EW == 0:
                    pool.wait_ge(rows_done, c // EW + 1)
                nc.gpsimd.indirect_dma_start(
                    out=W["nz"], out_offset=bass.IndirectOffsetOnAxis(ap=con["rowidx"][:, c:c + 1], axis=0),
                    in_=F[:, c, :], in_offset=None, bounds_check=N - 1, oob_is_err=False).then_inc(scattered, 16)
            pool.wait_ge(lead_ready, 2)
            nc.gpsimd.indirect_dma_start(
                out=W["nz"], out_offset=bass.IndirectOffsetOnAxis(ap=con["leadidx"][:, 0:1], axis=0),
                in_=orow[:], in_offset=None, bounds_check=N - 1, oob_is_err=False).then_inc(lead_saved, 16)
            pool.wait_ge(scattered, 16 * EC)
            pool.wait_ge(lead_saved, 16)

        @block.tensor
        def _(pe):
            pe.wait_ge(split, 5)

            def body(i, k):
                for v in range(NB):
                    wait(pe, picked, NB * (i - 1) + v + 1)
                    for part in range(3):
                        mm = nc.tensor.matmul(ps_g[v][:, 0:J * CHUNKS],
                                              con["onehot"][:, bass.ds(i * NB + v, 1), :].rearrange("p a m -> p (a m)"),
                                              parts[:, part, :], start=(part == 0), stop=(part == 2))
                    mm.then_inc(fetched, 1)
            body(0, 0)
            with pe.Fori(1, EC // NB) as i:
                body(i, 0)
            pe.wait_ge(maxed, EPARTS)
            nc.tensor.matmul(ps_m[:, 0:P], m[:, EC:EC + 1].to_broadcast([P, P]), con["ident"][:],
                             start=True, stop=True).then_inc(join_pe, 1)
            pe.wait_ge(joined, 3)
            nc.tensor.transpose(ps_w[:, 0:P], val[:, 1, :], con["ident"][:]).then_inc(join_pe, 1)
            pe.wait_ge(join_act, 2)
            pe.wait_ge(rows_done, EPARTS)
            nc.tensor.matmul(ps_c[:, 0:ROW - 1], wT[:], F[:, EC - 1, 0:ROW - 1], start=True, stop=True).then_inc(join_pe, 1)

        @block.vector
        def _(dve):
            ad = con["ad"]
            nc.vector.tensor_copy(parts[:, 0, :], ad[:]).then_inc(split, 1)
            dve.wait_ge(split, 1)
            nc.vector.tensor_tensor(rest[:, 0], ad[:], parts[:, 0, :], ALU.subtract).then_inc(split, 1)
            dve.wait_ge(split, 2)
            nc.vector.tensor_copy(parts[:, 1, :], rest[:, 0]).then_inc(split, 1)
            dve.wait_ge(split, 3)
            nc.vector.tensor_tensor(rest[:, 1], rest[:, 0], parts[:, 1, :], ALU.subtract).then_inc(split, 1)
            dve.wait_ge(split, 4)
            nc.vector.tensor_copy(parts[:, 2, :], rest[:, 1]).then_inc(split, 1)

            def body(i):
                for v in range(NB):
                    dve.wait_ge(fetched, NB * i + v + 1)
                    wait(dve, picked, NB * i + v)
                    nc.vector.scalar_tensor_tensor(out=pick[:], in0=con["iota"][:],
                                                   scalar=con["lo"][:, bass.ds(i * NB + v, 1)],
                                                   in1=ps_g[v][:, 0:J * CHUNKS], op0=ALU.is_equal, op1=ALU.mult,
                                                   accum_out=ade[:, bass.ds(i * NB + v, 1)]).then_inc(picked, 1)
            body(0)
            with dve.Fori(1, EC // NB) as i:
                body(i)
            count = [0]

            def link(ins, wait_for_it=True):
                count[0] += 1
                ins.then_inc(dve_step, 1)
                if wait_for_it:
                    dve.wait_ge(dve_step, count[0])

            dve.wait_ge(picked, EC)
            link(nc.vector.memset(m[:, 0:1], -BIG))
            for k in range(EPARTS):
                cols = slice(k * EW, k * EW + EW)
                mk, mprev = m[:, k * EW + 1:k * EW + EW + 1], m[:, k * EW:k * EW + EW]
                dve.wait_ge(gathered[k], 16 * EW)
                link(nc.vector.tensor_tensor(sc[:, 0], F[:, cols, D], ade[:, cols], ALU.add))
                link(nc.vector.scalar_tensor_tensor(out=sc[:, 1], in0=sc[:, 0], scalar=SLOPE, in1=sc[:, 0],
                                                    op0=ALU.mult, op1=ALU.max))
                link(nc.vector.tensor_copy(sm[:, 7:8], m[:, k * EW:k * EW + 1]))
                nc.vector.tensor_tensor_scan(mk, con["cut"][:, cols], sc[:, 1], sm[:, 7:8], ALU.add,
                                             ALU.max).then_inc(maxed, 1)
                dve.wait_ge(maxed, k + 1)
                link(nc.vector.tensor_tensor(sc[:, 2], sc[:, 1], mk, ALU.subtract))
                link(nc.vector.tensor_tensor(sc[:, 3], mprev, mk, ALU.subtract))
                nc.vector.tensor_scalar(sc[:, 3], sc[:, 3], 0.0, None, ALU.min).then_inc(differ, 1)
                dve.wait_ge(powers, k + 1)
                link(nc.vector.tensor_tensor(sc[:, 5], sc[:, 5], con["same"][:, cols], ALU.mult))
                link(nc.vector.tensor_tensor(F[:, cols, 0:D], F[:, cols, 0:D],
                                             sc[:, 4].unsqueeze(2).to_broadcast([P, EW, D]), ALU.mult))
                link(nc.vector.tensor_copy(F[:, cols, D], sc[:, 4]))
                link(nc.vector.tensor_copy(F[:, cols, D + 1], mk))
                for f in range(D + 1):
                    ins = nc.vector.tensor_tensor_scan(
                        F[:, cols, f], sc[:, 5], F[:, cols, f],
                        F[:, k * EW - 1, f:f + 1] if k else 0.0, ALU.mult, ALU.add)
                ins.then_inc(rows_done, 1)
                dve.wait_ge(rows_done, k + 1)
                if k:
                    dve.wait_ge(dve_step, count[0])
                link(nc.vector.tensor_tensor(prod[:], F[:, cols, :],
                                             con["leadend"][:, cols].unsqueeze(2).to_broadcast([P, EW, ROW]), ALU.mult))
                link(nc.vector.tensor_reduce(selp[:, k], prod[:].rearrange("p c f -> p f c"), AX.X, ALU.add))
            link(nc.vector.tensor_reduce(sel[:], selp[:].rearrange("p k f -> p f k"), AX.X, ALU.add))
            dve.wait_ge(join_pe, 1)
            link(nc.vector.tensor_tensor(val[:, 0], ps_m[:, 0:P], con["joins"][:], ALU.mult))
            link(nc.vector.tensor_tensor(val[:, 0], val[:, 0], con["nojoin"][:], ALU.add))
            link(nc.vector.tensor_reduce(sm[:, 0:1], val[:, 0], AX.X, ALU.max))
            nc.vector.tensor_scalar(val[:, 0], val[:, 0], sm[:, 0:1], None, ALU.subtract).then_inc(joined, 1)
            nc.vector.tensor_tensor(sm[:, 1:2], sm[:, 0:1], sel[:, ROW - 1:ROW], ALU.max).then_inc(joined, 1)
            dve.wait_ge(join_act, 1)
            nc.vector.tensor_tensor(val[:, 1], val[:, 1], con["joins"][:], ALU.mult).then_inc(joined, 1)
            dve.wait_ge(joined, 3)
            link(nc.vector.tensor_tensor(sm[:, 2:3], sel[:, ROW - 1:ROW], sm[:, 1:2], ALU.subtract))
            nc.vector.tensor_tensor(sm[:, 3:4], sm[:, 0:1], sm[:, 1:2], ALU.subtract).then_inc(joined, 1)
            dve.wait_ge(join_act, 3)
            dve.wait_ge(join_pe, 3)
            link(nc.vector.tensor_scalar(car[:, 0:ROW - 1], ps_c[:, 0:ROW - 1], sm[:, 5:6], None, ALU.mult))
            nc.vector.tensor_copy(orow[:, ROW - 1:ROW], sm[:, 1:2]).then_inc(lead_ready, 1)
            nc.vector.scalar_tensor_tensor(out=orow[:, 0:ROW - 1], in0=sel[:, 0:ROW - 1], scalar=sm[:, 4:5],
                                           in1=car[:, 0:ROW - 1], op0=ALU.mult, op1=ALU.add).then_inc(lead_ready, 1)

        @block.scalar
        def _(act):
            for k in range(EPARTS):
                act.wait_ge(differ, k + 1)
                nc.scalar.activation(sc[:, 4:6], sc[:, 2:4], ACT.Exp).then_inc(powers, 1)
            act.wait_ge(joined, 1)
            nc.scalar.activation(val[:, 1], val[:, 0], ACT.Exp).then_inc(join_act, 1)
            act.wait_ge(join_pe, 2)
            nc.scalar.copy(wT[:], ps_w[:, 0:P]).then_inc(join_act, 1)
            act.wait_ge(joined, 4)
            nc.scalar.activation(sm[:, 4:6], sm[:, 2:4], ACT.Exp).then_inc(join_act, 1)


def merge(nc, con, W, tag, last):
    with ExitStack() as ctx:
        tmp = Mem(nc, ctx, tag)
        tr = tmp.sb("tr", [P, 2, J, ROW])
        nz = tmp.sb("nz", [P, 2, J, ROW])
        xr = tmp.sb("xr", [P, 2, J, D])
        sc = tmp.sb("sc", [P, 2, 12, J])
        pa = tmp.sb("pa", [P, 2, J, D])
        pb = tmp.sb("pb", [P, 2, J, D])
        g = tmp.sb("g", [P, 2, J, D])
        gT = tmp.sb("gT", [P, 2, CH // 2])
        out = tmp.sb("out", [P, 2, J, ROW])
        ps_n = [tmp.ps(f"ps_n{k}", [P, 4, P]) for k in range(2)]
        ps_t = [tmp.ps(f"ps_t{k}", [P, 4, 256]) for k in range(2)]
        sem = tmp.sem
        tab_in, nz_in, x_in, saved = ([sem(f"{n}{k}") for k in range(2)] for n in ("tab_in", "nz_in", "x_in", "saved"))
        (self_sum, self_score, top, edge_off, self_off, powers, edge_z, den, inv, edge_w, self_w, edge_part, self_part, x_part,
         merged, turned, gT_out, t_done, t_out, ad_out) = (sem(n) for n in (
            "self_sum", "self_score", "top", "edge_off", "self_off", "powers", "edge_z", "den", "inv", "edge_w", "self_w",
            "edge_part", "self_part", "x_part", "merged", "turned", "gT_out", "t_done", "t_out", "ad_out"))
        block = ctx.enter_context(nc.Block())
        table = W["tab"]
        new_table = W["tab2"]

        def within(t):
            return not isinstance(t, int) or 0 <= t < CHUNKS

        def sems16(t, k):
            return 16 * (t // 2 + 1) if isinstance(t, int) else 8 * (t - k % 2) + 16

        def bc(v):
            return v.unsqueeze(2).to_broadcast([P, J, D])

        def run(eng, body):
            steps(eng, CHUNKS, 2, 2, body, 1)

        @block.sync
        def _(sp):
            def body(s, k):
                b = k % 2
                if within(s):
                    wait(sp, self_part, s - 1)
                    wait(sp, edge_part, s - 1)
                    sp.dma_start(tr[:, b].rearrange("p j c -> p (j c)"),
                                 flat(table, chunk_base(s), J, ROW)).then_inc(tab_in[b], 16)
                    sp.dma_start(nz[:, b].rearrange("p j c -> p (j c)"),
                                 flat(W["nz"], chunk_base(s), J, ROW)).then_inc(nz_in[b], 16)
                    if last:
                        wait(sp, merged, s - 1)
                        sp.dma_start(xr[:, b].rearrange("p j c -> p (j c)"),
                                     flat(W["x1"], chunk_base(s), J, D)).then_inc(x_in[b], 16)
                t = s - 1
                if within(t):
                    if isinstance(t, int) and t == CHUNKS - 1:
                        sp.wait_ge(saved[1 - t % 2], 16 * (CHUNKS // 2))
                    sp.wait_ge(merged if last else t_out, t + 1)
                    if last:
                        sp.dma_start(flat(W["out"], chunk_base(t), J, D),
                                     g[:, 1 - b].rearrange("p j c -> p (j c)")).then_inc(saved[1 - b], 16)
                    else:
                        sp.dma_start(flat(new_table, chunk_base(t), J, ROW),
                                     out[:, 1 - b].rearrange("p j c -> p (j c)")).then_inc(saved[1 - b], 16)
            run(sp, body)
            for k in range(2):
                sp.wait_ge(saved[k], 16 * ((CHUNKS + 1 - k) // 2))

        @block.vector
        def _(dve):
            def body(s, k):
                b = k % 2
                v = [sc[:, b, i] for i in range(12)]
                if within(s):
                    dve.wait_ge(tab_in[b], sems16(s, k))
                    dve.wait_ge(nz_in[b], sems16(s, k))
                    wait(dve, powers, s - 1)
                    wait(dve, self_part, s - 1)
                    nc.vector.tensor_tensor(v[0], tr[:, b, :, D], tr[:, b, :, D + 1], ALU.add).then_inc(self_sum, 1)
                    dve.wait_ge(self_sum, s + 1)
                    nc.vector.scalar_tensor_tensor(out=v[1], in0=v[0], scalar=SLOPE, in1=v[0], op0=ALU.mult,
                                                   op1=ALU.max).then_inc(self_score, 1)
                    dve.wait_ge(self_score, s + 1)
                    nc.vector.tensor_tensor(v[2], v[1], nz[:, b, :, D + 1], ALU.max).then_inc(top, 1)
                    dve.wait_ge(top, s + 1)
                    nc.vector.tensor_tensor(v[4], nz[:, b, :, D + 1], v[2], ALU.subtract).then_inc(edge_off, 1)
                    nc.vector.tensor_tensor(v[5], v[1], v[2], ALU.subtract).then_inc(self_off, 1)
                t = s - 1
                if within(t):
                    c = 1 - b
                    w = [sc[:, c, i] for i in range(12)]
                    dve.wait_ge(powers, t + 1)
                    nc.vector.tensor_tensor(w[8], w[6], nz[:, c, :, D], ALU.mult).then_inc(edge_z, 1)
                    dve.wait_ge(edge_z, t + 1)
                    nc.vector.scalar_tensor_tensor(out=w[9], in0=w[7], scalar=1e-16, in1=w[8], op0=ALU.add,
                                                   op1=ALU.add).then_inc(den, 1)
                    dve.wait_ge(den, t + 1)
                    nc.vector.reciprocal(w[10], w[9]).then_inc(inv, 1)
                    dve.wait_ge(inv, t + 1)
                    nc.vector.tensor_tensor(w[3], w[7], w[10], ALU.mult).then_inc(self_w, 1)
                    nc.vector.tensor_tensor(w[11], w[6], w[10], ALU.mult).then_inc(edge_w, 1)
                    dve.wait_ge(edge_w, t + 1)
                    wait(dve, merged, t - 1)
                    nc.vector.tensor_tensor(pa[:, c], nz[:, c, :, 0:D], bc(w[11]), ALU.mult).then_inc(edge_part, 1)
                    dve.wait_ge(edge_part, t + 1)
                    if last:
                        dve.wait_ge(x_in[c], sems16(t, k - 1))
                        nc.vector.tensor_tensor(pa[:, c], pa[:, c], xr[:, c], ALU.add).then_inc(x_part, 1)
                        dve.wait_ge(x_part, t + 1)
                        wait(dve, saved[c], 16 * (t // 2) if isinstance(t, int) else 8 * (t - c))
                    else:
                        wait(dve, turned, t - 1)
                    dve.wait_ge(self_part, t + 1)
                    nc.vector.tensor_tensor(g[:, c], pa[:, c], pb[:, c], ALU.add).then_inc(merged, 1)
            run(dve, body)

        @block.gpsimd
        def _(pool):
            def body(s, k):
                c = (k - 1) % 2
                t = s - 1
                if within(t):
                    pool.wait_ge(self_w, t + 1)
                    pool.wait_ge(tab_in[c], sems16(t, k - 1))
                    wait(pool, merged, t - 1)
                    nc.gpsimd.tensor_tensor(pb[:, c], tr[:, c, :, 0:D], bc(sc[:, c, 3]), ALU.mult).then_inc(self_part, 1)
            run(pool, body)

        @block.scalar
        def _(act):
            def body(s, k):
                b = k % 2
                if within(s):
                    act.wait_ge(edge_off, s + 1)
                    act.wait_ge(self_off, s + 1)
                    wait(act, edge_w, s - 1)
                    nc.scalar.activation(sc[:, b, 6:8], sc[:, b, 4:6], ACT.Exp).then_inc(powers, 1)
                t = s - 1
                if within(t) and not last:
                    c = 1 - b
                    act.wait_ge(turned, t + 1)
                    wait(act, t_done, t - 1)
                    nc.scalar.activation(gT[:, c], ps_n[c][:], ACT.Relu, bias=con["gb1col"][:, 0:1]).then_inc(gT_out, 1)
                    act.wait_ge(t_done, t + 1)
                    wait(act, saved[c], 16 * (t // 2) if isinstance(t, int) else 8 * (t - c))
                    nc.scalar.copy(out[:, c].rearrange("p (a v) c -> p a (v c)", v=2),
                                   ps_t[c][:, :, 0:2 * ROW]).then_inc(t_out, 1)
                    nc.scalar.copy(con["ad"][:, bass.ds(t * J, J)].rearrange("p (a v) -> p a v", v=2),
                                   ps_t[c][:, :, D + 1:2 * ROW:ROW]).then_inc(ad_out, 1)
            run(act, body)

        if not last:
            @block.tensor
            def _(pe):
                def body(s, k):
                    c = (k - 1) % 2
                    t = s - 1
                    if within(t):
                        pe.wait_ge(merged, t + 1)
                        wait(pe, gT_out, t - 1)
                        for a in range(4):
                            mm = nc.tensor.transpose(ps_n[c][:, a, :], g[:, c, 2 * a:2 * a + 2].rearrange("p j c -> p (j c)"),
                                                     con["ident"][:])
                        mm.then_inc(turned, 1)
                        pe.wait_ge(gT_out, t + 1)
                        wait(pe, ad_out, t - 1)
                        for a in range(4):
                            mm = nc.tensor.matmul(ps_t[c][:, a, 0:2 * ROW], gT[:, c, a * P:a * P + P], con["bd2"][:],
                                                  start=True, stop=True)
                        mm.then_inc(t_done, 1)
                run(pe, body)


def graph_kernel(nc, W):
    with ExitStack() as ctx:
        mem = Mem(nc, ctx, "all")
        shapes = dict(zero=[P, AGG_ROWS // P // ZERO_DMAS * D], ident=[P, P], later=[P, P], earlier=[P, P],
                      iota=[P, J * CHUNKS], dummy=[P, GROUPS * GT], pidx=[P, 1], nzrows=[P, CHUNKS * J // 14, ROW],
                      bd1=[P, 2 * ROW], bd2=[P, 2 * ROW], w1=[P, HID], w2=[P, 2, D], hbias=[P, 2], b2row=[P, D],
                      gb2row=[P, D], gb1col=[P, 1], lastkey=[P, 1], same=[P, EC], cut=[P, EC], leadend=[P, EC],
                      lo=[P, EC], joins=[P, P], nojoin=[P, P], srckey=[P, GROUPS * GT], dumdiff=[P, GROUPS * GT],
                      ad=[P, J * CHUNKS])
        con = {n: mem.sb(n, s) for n, s in shapes.items()}
        con.update(onehot=mem.sb("onehot", [P, EC, P], BF16), srcg=mem.sb("srcg", [P, EC], I32),
                   rowidx=mem.sb("rowidx", [P, EC], I32), leadidx=mem.sb("leadidx", [P, 1], I32),
                   agg_zeroed=mem.sem("agg_zeroed"))
        W["agg"] = nc.dram_tensor("agg_table", (AGG_ROWS, D), F32).ap()
        W["x1"] = nc.dram_tensor("x1_table", (N, D), F32).ap()
        W["tab"] = nc.dram_tensor("att_table1", (N, ROW), F32).ap()
        W["nz"] = nc.dram_tensor("nz_table", (CHUNKS * CH, ROW), F32).ap()
        tab2 = nc.dram_tensor("att_table2", (N, ROW), F32).ap()
        W["tab2"] = tab2
        setup(nc, mem, con, W)
        sum_edges(nc, con, W)
        mlp(nc, con, W)
        edge_attention(nc, con, W, "att1")
        merge(nc, con, W, "merge1", False)
        W["tab"] = tab2
        edge_attention(nc, con, W, "att2")
        merge(nc, con, W, "merge2", True)


_INS = {'x': 'x', 'src': 'src', 'dst': 'dst', 'edge_attr_64': 'ea', 'L0_gnn_u': 'u', 'L0_gnn_W1': 'W1', 'L0_gnn_b1': 'b1',
        'L0_gnn_W2': 'W2', 'L0_gnn_b2': 'b2', 'L1_gnn_W1': 'gW1', 'L1_gnn_a_src1': 'as1', 'L1_gnn_a_dst1': 'ad1',
        'L1_gnn_b1': 'gb1', 'L1_gnn_W2': 'gW2', 'L1_gnn_a_src2': 'as2', 'L1_gnn_a_dst2': 'ad2', 'L1_gnn_b2': 'gb2'}


def kernel(**inputs):
    import numpy as _np
    import concourse.bacc as _bacc
    from concourse import mybir as _mybir
    from concourse.bass_utils import run_bass_kernel_spmd as _run

    nc = _bacc.Bacc("TRN2", target_bir_lowering=False, num_devices=1)
    arrays, args = {}, {}
    for name, short in _INS.items():
        a = _np.ascontiguousarray(inputs[name])
        arrays[f"in_{name}_dram"] = a
        args[short] = nc.dram_tensor(f"in_{name}_dram", a.shape, _mybir.dt.from_np(a.dtype), kind="ExternalInput").ap()
    args["out"] = nc.dram_tensor("out_0_dram", (N, D), _mybir.dt.float32, kind="ExternalOutput").ap()
    graph_kernel(nc, args)
    r = _run(nc, [arrays], core_ids=[0])
    return r.results[0]["out_0_dram"]
```

```python
from contextlib import ExitStack

import concourse.bass as bass
from concourse import mybir
from concourse.alu_op_type import AluOpType as ALU

F32 = mybir.dt.float32
BF16 = mybir.dt.bfloat16
I32 = mybir.dt.int32
ACT = mybir.ActivationFunctionType
AX = mybir.AxisListType

P = 128
BIG = 1.0e30
EPS = 1e-5
SLOPE = 0.2

N = 50000
E = 25000
D = 64
HID = 256
ROW = D + 2

J = 8
CH = P * J
CHUNKS = -(-N // CH)
LAST = N - CH
SHIFT = (CHUNKS - 1) * CH - LAST

EC = -(-E // P)
EPARTS = 4
EW = EC // EPARTS
FULLP = E // EC
RESTC = E - FULLP * EC

GT = 4
GE = P * GT
GROUPS = -(-E // GE)
ALONE = 6
LASTE = E - (GROUPS - 1) * GE
PADROW = N + GE
ZERO_DMAS = 12
AGG_ROWS = -(-(PADROW + 1) // (P * ZERO_DMAS)) * P * ZERO_DMAS
ZERO_ROWS = AGG_ROWS // (P * ZERO_DMAS)
SKIP = 1 << 16


def wait(eng, sem, value):
    if isinstance(value, int) and value <= 0:
        return
    eng.wait_ge(sem, value)


def steps(eng, count, lead, unroll, body, tail, ahead=0):
    trips = (count - 1 - ahead) // unroll
    for t in range(lead):
        body(t, t)
    with eng.Fori(lead // unroll, trips) as r:
        for b in range(unroll):
            body(r * unroll + b, b)
    for t in range(trips * unroll, count + tail):
        body(t, t)


def chunk_base(t):
    return min(t * CH, LAST) if isinstance(t, int) else t * CH


def flat(dram, start, rows, width):
    f = dram.rearrange("n c -> (n c)")
    return f[bass.ds(start * width, P * rows * width)].rearrange("(p f) -> p f", p=P)


class Mem:

    def __init__(self, nc, ctx, tag):
        self.nc, self.ctx, self.tag = nc, ctx, tag
        self.sems = []

    def sb(self, name, shape, dt=F32):
        return self.ctx.enter_context(self.nc.sbuf_tensor(f"{name}_{self.tag}", shape, dt))

    def ps(self, name, shape):
        return self.ctx.enter_context(self.nc.psum_tensor(f"{name}_{self.tag}", shape, F32))

    def sem(self, name):
        self.sems.append(self.ctx.enter_context(self.nc.semaphore(f"{name}_{self.tag}")))
        return self.sems[-1]

    def block(self):
        numbers = sorted(s.num for s in self.sems)

        def clear():
            start = numbers[0]
            for a, b in zip(numbers, numbers[1:] + [None]):
                if b != a + 1:
                    self.nc.gpsimd.sem_clear(range(start, a + 1))
                    start = b
        self.ctx.callback(clear)
        return self.ctx.enter_context(self.nc.Block())


def setup(nc, mem, con, W):
    with ExitStack() as ctx:
        tmp = Mem(nc, ctx, "setup")
        io392 = tmp.sb("io392", [P, J * CHUNKS], I32)
        dumi = tmp.sb("dumi", [P, GROUPS, GT], I32)
        piota = tmp.sb("piota", [P, 1], I32)
        ones = tmp.sb("ones", [P, P])
        srcc = tmp.sb("srcc", [P, GROUPS * GT], I32)
        di = tmp.sb("di", [P, EC + 2], I32)
        u0 = tmp.sb("u0", [16, 1])
        w1u = tmp.sb("w1u", [16, HID])
        b1c = tmp.sb("b1c", [P, 2])
        wst = tmp.sb("wst", [P, 2, D])
        wT = tmp.sb("wT", [D, 2, P])
        av = tmp.sb("av", [D, 2, 2])
        q = tmp.sb("q", [P, 12, EC])
        qi = tmp.sb("qi", [P, 6, EC], I32)
        nend = tmp.sb("nend", [P, 4])
        ps_u = tmp.ps("ps_u", [P, 512])
        ps_w = tmp.ps("ps_w", [P, 512])
        ps_a = tmp.ps("ps_a", [P, 512])
        ps_f = tmp.ps("ps_f", [P, 512])
        sem = tmp.sem
        pooled, loaded, filled = sem("pooled"), sem("loaded"), sem("filled")
        edge_loaded, table_zeroed = sem("edge_loaded"), con["agg_zeroed"][0]
        dve_step, pe_step, act_step, zero_ready = sem("dve_step"), sem("pe_step"), sem("act_step"), sem("zero_ready")

        ctx.enter_context(nc.allow_non_contiguous_dma(reason="a few hundred single keys, vectors as columns"))
        block = tmp.block()

        @block.gpsimd
        def _(pool):
            nc.gpsimd.memset(con["zero"][:], 0.0).then_inc(zero_ready, 1)
            nc.gpsimd.memset(ones[:], 1.0).then_inc(filled, 1)
            nc.gpsimd.memset(con["bd1"][:], 0.0).then_inc(filled, 1)
            nc.gpsimd.memset(con["bd2"][:], 0.0).then_inc(filled, 1)
            nc.gpsimd.memset(di[:], N).then_inc(filled, 1)
            nc.gpsimd.memset(con["srcg"][:], 0).then_inc(filled, 1)
            nc.gpsimd.memset(srcc[:], PADROW).then_inc(filled, 1)
            nc.gpsimd.iota(io392[:], pattern=[[1, J * CHUNKS]], base=0, channel_multiplier=0).then_inc(filled, 1)
            nc.gpsimd.iota(dumi[:], pattern=[[0, GROUPS], [P, GT]], base=N, channel_multiplier=1).then_inc(filled, 1)
            nc.gpsimd.iota(piota[:], pattern=[[0, 1]], base=0, channel_multiplier=1).then_inc(filled, 1)
            pool.wait_ge(filled, 9)
            nc.gpsimd.affine_select(out=con["ident"][:], in_=ones[:], compare_op=ALU.is_equal, fill=0.0, base=0,
                                    pattern=[[1, P]], channel_multiplier=-1).then_inc(pooled, 1)
            nc.gpsimd.affine_select(out=con["later"][:], in_=ones[:], compare_op=ALU.is_gt, fill=0.0, base=0,
                                    pattern=[[1, P]], channel_multiplier=-1).then_inc(pooled, 1)
            nc.gpsimd.affine_select(out=con["earlier"][:], in_=ones[:], compare_op=ALU.is_gt, fill=0.0, base=0,
                                    pattern=[[-1, P]], channel_multiplier=1).then_inc(pooled, 1)
            nc.gpsimd.tensor_copy(con["iota"][:], io392[:]).then_inc(pooled, 1)
            nc.gpsimd.tensor_copy(con["dummy"][:], dumi[:].rearrange("p g i -> p (g i)")).then_inc(pooled, 1)
            nc.gpsimd.tensor_copy(con["pidx"][:], piota[:]).then_inc(pooled, 1)
            nc.gpsimd.memset(con["nzrows"][:], 0.0).then_inc(pooled, 1)
            pool.wait_ge(pooled, 7)
            nc.gpsimd.memset(con["nzrows"][:, :, ROW - 1:ROW], -BIG).then_inc(pooled, 1)

        n_w = 0

        @block.sync
        def _(sp):
            nonlocal n_w
            def load(dst, src):
                nonlocal n_w
                sp.dma_start(dst, src).then_inc(loaded, 16)
                n_w += 1
            sp.wait_ge(filled, 6)
            main = (GROUPS - 1) * GE
            src_g = W["src"][0:main].rearrange("(g p i) -> p g i", p=P, i=GT)
            sp.dma_start(srcc[:, 0:(GROUPS - 1) * GT].rearrange("p (g i) -> p g i", i=GT), src_g).then_inc(edge_loaded, 16)
            sp.dma_start(srcc[0:LASTE // GT, (GROUPS - 1) * GT:],
                         W["src"][main:E].rearrange("(p i) -> p i", i=GT)).then_inc(edge_loaded, 16)
            sp.dma_start(di[0:FULLP, 1:EC + 1], W["dst"][0:FULLP * EC].rearrange("(p c) -> p c", c=EC)).then_inc(edge_loaded, 16)
            sp.dma_start(di[FULLP:FULLP + 1, 1:RESTC + 1],
                         W["dst"][FULLP * EC:E].rearrange("(p c) -> p c", p=1)).then_inc(edge_loaded, 16)
            sp.dma_start(di[1:FULLP + 1, 0:1], W["dst"][0:FULLP * EC].rearrange("(p c) -> p c", c=EC)[:, EC - 1:EC]).then_inc(edge_loaded, 16)
            sp.dma_start(di[0:FULLP - 1, EC + 1:EC + 2],
                         W["dst"][EC:FULLP * EC].rearrange("(p c) -> p c", c=EC)[:, 0:1]).then_inc(edge_loaded, 16)
            sp.dma_start(di[FULLP - 1:FULLP, EC + 1:EC + 2],
                         W["dst"][FULLP * EC:FULLP * EC + 1].rearrange("(p c) -> p c", p=1)).then_inc(edge_loaded, 16)
            sp.dma_start(con["srcg"][0:FULLP, :], W["src"][0:FULLP * EC].rearrange("(p c) -> p c", c=EC)).then_inc(edge_loaded, 16)
            sp.dma_start(con["srcg"][FULLP:FULLP + 1, 0:RESTC],
                         W["src"][FULLP * EC:E].rearrange("(p c) -> p c", p=1)).then_inc(edge_loaded, 16)
            load(con["w1"][:], W["W1"][0:P, :])
            load(w1u[:], W["W1"][P:P + 16, :])
            load(u0[:], W["u"][0:1, :].rearrange("a c -> c a"))
            load(b1c[:], W["b1"].rearrange("(m p) -> p m", p=P))
            load(con["w2"][:], W["W2"].rearrange("(m p) n -> p m n", p=P))
            load(con["b2row"][:], W["b2"].partition_broadcast(P))
            load(con["gb2row"][:], W["gb2"].partition_broadcast(P))
            for l, (w, bd) in enumerate((("gW1", "bd1"), ("gW2", "bd2"))):
                for h in range(2):
                    load(wst[D * h:D * h + D, l, :], W[w])
                    load(con[bd][D * h:D * h + D, ROW * h:ROW * h + D], W[w])
                load(av[:, l, 0:1], W[f"as{l + 1}"].rearrange("(n o) -> n o", o=1))
                load(av[:, l, 1:2], W[f"ad{l + 1}"].rearrange("(n o) -> n o", o=1))
            for h in range(2):
                load(con["gb1col"][D * h:D * h + D, :], W["gb1"].rearrange("(n o) -> n o", o=1))

        @block.scalar
        def _(act):
            act.wait_ge(zero_ready, 1)
            for k in range(ZERO_DMAS):
                act.dma_start(flat(W["agg"][0], k * P * ZERO_ROWS, ZERO_ROWS, D), con["zero"][:]).then_inc(table_zeroed, 16)

        @block.tensor
        def _(pe):
            pe.wait_ge(loaded, 16 * 21)
            pe.wait_ge(pooled, 1)
            for m in range(2):
                mm = nc.tensor.matmul(ps_u[:, m:m + 1], w1u[:, m * P:m * P + P], u0[:, :], start=True, stop=True)
            mm.then_inc(pe_step, 1)
            for l in range(2):
                mm = nc.tensor.transpose(ps_w[0:D, l * P:l * P + P], wst[:, l, :], con["ident"][:])
            mm.then_inc(pe_step, 1)
            pe.wait_ge(act_step, 2)
            for l in range(2):
                mm = nc.tensor.matmul(ps_a[:, 2 * l:2 * l + 2], wT[:, l, :], av[:, l, :], start=True, stop=True)
            mm.then_inc(pe_step, 1)
            pe.wait_ge(dve_step, 2)
            nc.tensor.matmul(ps_f[:, 0:P], q[:, 0, 0:1].to_broadcast([P, P]), con["ident"][:], start=True, stop=True)
            nc.tensor.matmul(ps_f[:, P:2 * P], q[:, 0, EC - 1:EC].to_broadcast([P, P]), con["ident"][:],
                             start=True, stop=True).then_inc(pe_step, 1)

        @block.scalar
        def _(act):
            act.wait_ge(pe_step, 1)
            act.wait_ge(loaded, 16 * 21)
            for m in range(2):
                ins = nc.scalar.activation(con["hbias"][:, m:m + 1], ps_u[:, m:m + 1], ACT.Identity, bias=b1c[:, m:m + 1])
            ins.then_inc(act_step, 1)
            act.wait_ge(pe_step, 2)
            nc.scalar.copy(wT[:].rearrange("p l k -> p (l k)"), ps_w[0:D, 0:2 * P]).then_inc(act_step, 1)
            act.wait_ge(pe_step, 3)
            for l, bd in enumerate(("bd1", "bd2")):
                for h in range(2):
                    ins = nc.scalar.copy(con[bd][D * h:D * h + D, ROW * h + D:ROW * h + ROW],
                                         ps_a[D * h:D * h + D, 2 * l:2 * l + 2])
            ins.then_inc(act_step, 1)

        @block.vector
        def _(dve):
            count = [0]

            def link(ins):
                count[0] += 1
                ins.then_inc(dve_step, 1)
                dve.wait_ge(dve_step, count[0])

            dve.wait_ge(edge_loaded, 16 * 9)
            dve.wait_ge(pooled, 8)
            d = di[:, 1:EC + 1]
            key, prv, nxt, t0, t1, same, endf, lead, t2 = (q[:, k, :] for k in range(9))
            link(nc.vector.tensor_copy(key, d))
            link(nc.vector.tensor_copy(con["lastkey"][:], key[:, EC - 1:EC]))
            link(nc.vector.tensor_copy(prv, di[:, 0:EC]))
            link(nc.vector.tensor_copy(nxt, di[:, 2:EC + 2]))
            link(nc.vector.tensor_tensor(same, key, prv, ALU.is_equal))
            link(nc.vector.tensor_tensor(endf, key, nxt, ALU.not_equal))
            link(nc.vector.memset(t0, 1.0))
            link(nc.vector.memset(t0[:, 0:1], 0.0))
            link(nc.vector.tensor_tensor(con["same"][:], same, t0, ALU.mult))
            link(nc.vector.tensor_scalar(con["cut"][:], con["same"][:], BIG, -BIG, ALU.mult, ALU.add))
            link(nc.vector.tensor_tensor(t1[:, 0:1], prv[:, 0:1], con["pidx"][:], ALU.add))
            link(nc.vector.tensor_scalar(t1[:, 1:2], con["pidx"][:], 0.5, None, ALU.is_ge))
            link(nc.vector.tensor_scalar(lead, key, prv[:, 0:1], t1[:, 1:2], ALU.is_equal, ALU.mult))
            link(nc.vector.tensor_tensor(con["leadend"][:], lead, endf, ALU.mult))
            link(nc.vector.tensor_tensor(t2, endf, con["leadend"][:], ALU.subtract))
            link(nc.vector.tensor_scalar(t0, t2, -float(SKIP), float(SKIP), ALU.mult, ALU.add))
            link(nc.vector.tensor_tensor(con["rowidx"][:], t0, key, ALU.add))
            link(nc.vector.tensor_reduce(nend[:, 0:1], con["leadend"][:], AX.X, ALU.add))
            link(nc.vector.tensor_scalar(nend[:, 1:2], nend[:, 0:1], -float(SKIP), float(SKIP), ALU.mult, ALU.add))
            link(nc.vector.tensor_tensor(con["leadidx"][:], nend[:, 1:2], key[:, 0:1], ALU.add))
            link(nc.vector.tensor_scalar(t0, key, float((CHUNKS - 1) * CH), float(SHIFT), ALU.is_ge, ALU.mult))
            link(nc.vector.tensor_tensor(qi[:, 0, :], t0, key, ALU.add))
            link(nc.vector.tensor_scalar(qi[:, 1, :], qi[:, 0, :], J.bit_length() - 1, P - 1,
                                         ALU.logical_shift_right, ALU.bitwise_and))
            link(nc.vector.tensor_scalar(qi[:, 2, :], qi[:, 0, :], CH.bit_length() - 1, J.bit_length() - 1,
                                         ALU.logical_shift_right, ALU.logical_shift_left))
            link(nc.vector.tensor_scalar(qi[:, 3, :], qi[:, 0, :], J - 1, None, ALU.bitwise_and))
            link(nc.vector.tensor_tensor(con["lo"][:], qi[:, 2, :], qi[:, 3, :], ALU.add))
            link(nc.vector.tensor_copy(con["identb"][:], con["ident"][:]))
            link(nc.vector.tensor_copy(con["high4"][:].rearrange("p k g -> p g k"), qi[:, 1, :].rearrange("p (g k) -> p g k", k=4)))
            link(nc.vector.tensor_copy(con["laterb"][:], con["later"][:]))
            dve.wait_ge(pe_step, 4)
            link(nc.vector.tensor_scalar(con["joins"][:], ps_f[:, P:2 * P], key[:, 0:1], None, ALU.is_equal))
            link(nc.vector.tensor_tensor(con["joins"][:], con["joins"][:], con["earlier"][:], ALU.mult))
            link(nc.vector.tensor_scalar(con["nojoin"][:], con["joins"][:], BIG, -BIG, ALU.mult, ALU.add))
            link(nc.vector.tensor_copy(con["srckey"][:], srcc[:]))
            link(nc.vector.tensor_tensor(con["dumdiff"][:], con["dummy"][:], con["srckey"][:], ALU.subtract))


def sum_edges(nc, con, W):
    with ExitStack() as ctx:
        tmp = Mem(nc, ctx, "agg")
        krow = tmp.sb("krow", [P, 2, GE], I32)
        ea = tmp.sb("ea", [P, 2, GT, D])
        rest = tmp.sb("rest", [P, 2, 2, GT, D])
        part = tmp.sb("part", [P, 2, 3, GT, D], BF16)
        eq = tmp.sb("eq", [P, 2, GT, GT, P], BF16)
        diag = tmp.sb("diag", [P, 2, GT, P], BF16)
        onec = tmp.sb("onec", [P, 1], BF16)
        tot = tmp.sb("tot", [P, 2, GT, D])
        away = tmp.sb("away", [P, 2, GT])
        idx = tmp.sb("idx", [P, 2, GT], I32)
        ps_t = [tmp.ps(f"ps_t{b}", [P, GT, P]) for b in range(2)]
        ps_d = [tmp.ps(f"ps_d{b}", [P, 512]) for b in range(2)]
        ps_h = [tmp.ps(f"ps_h{b}", [P, 4, P]) for b in range(2)]
        sem = tmp.sem
        keys_in, attr_in = [sem("keys_in0"), sem("keys_in1")], [sem("attr_in0"), sem("attr_in1")]
        padded, eq_built, diag_built, ones_set = sem("padded"), sem("eq_built"), sem("diag_built"), sem("ones_set")
        part0_out, part1_out, part2_out = sem("part0_out"), sem("part1_out"), sem("part2_out")
        rest1_out, rest2_out = sem("rest1_out"), sem("rest2_out")
        summed, counted = sem("summed"), sem("counted")
        sums_out, away_out, idx_out = sem("sums_out"), sem("away_out"), sem("idx_out")
        hi_spread, onehot_made = sem("hi_spread"), sem("onehot_made")
        added = con["added"]
        block = tmp.block()
        attr = W["ea"].rearrange("n c -> (n c)")

        def groups(eng, body):
            steps(eng, GROUPS, ALONE, 2, body, 0)

        def landed(g, b):
            return 16 * (g // 2 + 1) if isinstance(g, int) else 8 * (g - b) + 16

        def adds(g, b):
            return 16 * GT * (g // 2 + 1) if isinstance(g, int) else 8 * GT * (g - b) + 16 * GT

        @block.sync
        def _(sp):
            def body(g, b):
                b %= 2
                wait(sp, eq_built, GT * (g - 1))
                if not isinstance(g, int) or g < GROUPS - 1:
                    sp.dma_start(krow[:, b], W["src"][bass.ds(g * GE, GE)].partition_broadcast(P)).then_inc(keys_in[b], 16)
                else:
                    wait(sp, padded, 2)
                    sp.dma_start(krow[:, b, 0:LASTE], W["src"][E - LASTE:E].partition_broadcast(P)).then_inc(keys_in[b], 16)
                wait(sp, part0_out, g - 1)
                wait(sp, rest1_out, g - 1)
                if not isinstance(g, int) or g < GROUPS - 1:
                    sp.dma_start(ea[:, b].rearrange("p i c -> p (i c)"),
                                 attr[bass.ds(g * GE * D, GE * D)].rearrange("(p f) -> p f", p=P)).then_inc(attr_in[b], 16)
                else:
                    sp.dma_start(ea[0:LASTE // GT, b].rearrange("p i c -> p (i c)"),
                                 attr[(E - LASTE) * D:E * D].rearrange("(p f) -> p f", f=GT * D)).then_inc(attr_in[b], 16)
            groups(sp, body)

        @block.vector
        def _(dve):
            nc.vector.memset(onec[:], 1.0).then_inc(ones_set, 1)

            def indices(g, b):
                dve.wait_ge(counted, g + 1)
                wait(dve, idx_out, g - 1)
                nc.vector.scalar_tensor_tensor(out=away[:, b], in0=ps_d[b][:, 0:GT], scalar=0.5,
                                               in1=con["dumdiff"][:, bass.ds(g * GT, GT)], op0=ALU.is_ge,
                                               op1=ALU.mult).then_inc(away_out, 1)
                dve.wait_ge(away_out, g + 1)
                wait(dve, added[b], adds(g, b) - 16 * GT)
                nc.vector.tensor_tensor(idx[:, b], away[:, b], con["srckey"][:, bass.ds(g * GT, GT)],
                                        ALU.add).then_inc(idx_out, 1)

            def body(g, b):
                b %= 2
                if isinstance(g, int) and g == GROUPS - 1:
                    dve.wait_ge(eq_built, GT * (g - 1))
                    dve.wait_ge(part0_out, g - 1)
                    dve.wait_ge(rest1_out, g - 1)
                    nc.vector.memset(krow[:, b], PADROW).then_inc(padded, 1)
                    nc.vector.memset(ea[:, b], 0.0).then_inc(padded, 1)
                if not isinstance(g, int) or g < GROUPS:
                    dve.wait_ge(keys_in[b], landed(g, b))
                    wait(dve, summed, g - 1)
                    for j in range(GT):
                        nc.vector.tensor_scalar(eq[:, b, j], krow[:, b].rearrange("p (m i) -> p i m", i=GT),
                                                con["srckey"][:, bass.ds(g * GT + j, 1)], None,
                                                ALU.is_equal).then_inc(eq_built, 1)
                        if j == 1:
                            dve.wait_ge(part0_out, g + 1)
                            dve.wait_ge(attr_in[b], landed(g, b))
                            wait(dve, rest2_out, g - 1)
                            nc.vector.tensor_tensor(rest[:, b, 0], ea[:, b], part[:, b, 0],
                                                    ALU.subtract).then_inc(rest1_out, 1)
                    dve.wait_ge(part1_out, g + 1)
                    dve.wait_ge(rest1_out, g + 1)
                    wait(dve, part2_out, g - 1)
                    nc.vector.tensor_tensor(rest[:, b, 1], rest[:, b, 0], part[:, b, 1],
                                            ALU.subtract).then_inc(rest2_out, 1)
                    dve.wait_ge(eq_built, GT * (g + 1))
                    nc.vector.tensor_tensor(diag[:, b], eq[:, b].rearrange("p j i m -> p (j i) m")[:, ::GT + 1, :],
                                            con["laterb"][:].unsqueeze(1).to_broadcast([P, GT, P]),
                                            ALU.mult).then_inc(diag_built, 1)
                    dve.wait_ge(hi_spread, g + 1)
                    nc.vector.tensor_scalar(con["onehot"][:, bass.ds(g * 4, 4), :], ps_h[b][:], con["pidx"][:, 0:1], None,
                                            ALU.is_equal).then_inc(onehot_made, 1)
                if not isinstance(g, int) or g >= 1:
                    indices(g - 1, 1 - b)
            steps(dve, GROUPS, ALONE, 2, body, 1)

        @block.tensor
        def _(pe):
            pe.wait_ge(ones_set, 1)

            def body(g, b):
                b %= 2
                wait(pe, onehot_made, g - 1)
                for k in range(4):
                    mm = nc.tensor.matmul(ps_h[b][:, k, :], con["high4"][:, k, bass.ds(g, 1)].to_broadcast([P, P]),
                                          con["identb"][:], start=True, stop=True)
                mm.then_inc(hi_spread, 1)
                pe.wait_ge(diag_built, g + 1)
                wait(pe, away_out, g - 1)
                for i in range(GT):
                    for j in range(i + 1):
                        mm = nc.tensor.matmul(ps_d[b][:, i:i + 1], diag[:, b, i] if j == i else eq[:, b, j, i], onec[:],
                                              start=(j == 0), stop=(j == i))
                mm.then_inc(counted, 1)
                pe.wait_ge(part2_out, g + 1)
                wait(pe, sums_out, g - 1)
                for i in range(GT):
                    for j in range(GT):
                        for v in range(3):
                            mm = nc.tensor.matmul(ps_t[b][:, i, 0:D], eq[:, b, j, i], part[:, b, v, j],
                                                  start=(j == 0 and v == 0), stop=(j == GT - 1 and v == 2))
                mm.then_inc(summed, 1)
            groups(pe, body)

        @block.scalar
        def _(act):
            def sums(g, b):
                act.wait_ge(summed, g + 1)
                wait(act, added[b], adds(g, b) - 16 * GT)
                nc.scalar.copy(tot[:, b], ps_t[b][:, :, 0:D]).then_inc(sums_out, 1)

            def body(g, b):
                b %= 2
                if not isinstance(g, int) or g < GROUPS:
                    act.wait_ge(attr_in[b], landed(g, b))
                    wait(act, summed, g - 1)
                    nc.scalar.copy(part[:, b, 0], ea[:, b]).then_inc(part0_out, 1)
                    act.wait_ge(rest1_out, g + 1)
                    nc.scalar.copy(part[:, b, 1], rest[:, b, 0]).then_inc(part1_out, 1)
                    act.wait_ge(rest2_out, g + 1)
                    nc.scalar.copy(part[:, b, 2], rest[:, b, 1]).then_inc(part2_out, 1)
                if isinstance(g, int) and g < ALONE:
                    for v in range(g * ZERO_DMAS // ALONE, (g + 1) * ZERO_DMAS // ALONE):
                        act.dma_start(flat(W["agg"][1], v * P * ZERO_ROWS, ZERO_ROWS, D),
                                      con["zero"][:]).then_inc(con["agg_zeroed"][1], 16)
                if not isinstance(g, int) or g >= 1:
                    sums(g - 1, 1 - b)
            steps(act, GROUPS, ALONE, 2, body, 1)

        @block.gpsimd
        def _(pool):
            def body(g, b):
                b %= 2
                alone = isinstance(g, int) and g < ALONE
                if isinstance(g, int) and g == 0:
                    pool.wait_ge(con["agg_zeroed"][0], 16 * ZERO_DMAS)
                pool.wait_ge(sums_out, g + 1)
                pool.wait_ge(idx_out, g + 1)
                wait(pool, added[b], adds(g, b) - 16 * GT)
                if alone and g > 0:
                    pool.wait_ge(added[1 - b], adds(g - 1, 1 - b))
                pool.nop(nofuse=True)
                for i in range(GT):
                    nc.gpsimd.indirect_dma_start(
                        out=W["agg"][0 if alone else b], out_offset=bass.IndirectOffsetOnAxis(ap=idx[:, b, i:i + 1], axis=0),
                        in_=tot[:, b, i], in_offset=None, compute_op=ALU.add).then_inc(added[b], 16)
                if isinstance(g, int) and g == ALONE - 1:
                    pool.wait_ge(con["agg_zeroed"][1], 16 * ZERO_DMAS)
                    pool.wait_ge(added[b], adds(g, b))
            groups(pool, body)
            for b in range(2):
                pool.wait_ge(added[b], 16 * GT * ((GROUPS + 1 - b) // 2))


def mlp(nc, con, W):
    with ExitStack() as ctx:
        tmp = Mem(nc, ctx, "mlp")
        NX = 4
        xt = tmp.sb("xt", [P, NX, J, D])
        xb = tmp.sb("xb", [P, NX, J, D])
        xc = tmp.sb("xc", [P, 2, J, D])
        sq = tmp.sb("sq", [P, J, D])
        hx = tmp.sb("hx", [P, 2, J, 2 * D])
        agg1 = tmp.sb("agg1", [P, 2, J, D])
        hxT = tmp.sb("hxT", [P, 2, CH])
        hid = tmp.sb("hid", [P, 2, 2, CH])
        x1 = tmp.sb("x1", [P, 2, J, D])
        x1o = tmp.sb("x1o", [P, 2, J, D])
        yc = tmp.sb("yc", [P, 2, J, D])
        sqy = tmp.sb("sqy", [P, J, D])
        h1 = tmp.sb("h1", [P, 2, J, D])
        h1T = tmp.sb("h1T", [P, CH // 2])
        tt = tmp.sb("tt", [P, 2, J, ROW])
        st = tmp.sb("st", [P, 2, 5, J])
        eps = tmp.sb("eps", [P, 1])
        invd = tmp.sb("invd", [P, J])
        ps_x = tmp.ps("ps_x", [P, J, P])
        ps_h = [tmp.ps(f"ps_h{m}", [P, 512]) for m in range(2)]
        ps_o = tmp.ps("ps_o", [P, J, D])
        ps_n = tmp.ps("ps_n", [P, 4, P])
        ps_t = tmp.ps("ps_t", [P, 4, 256])
        sem = tmp.sem
        x_in = [sem(f"x_in{k}") for k in range(NX)]
        agg_in = [sem(f"agg_in{k}") for k in range(2)]
        agg1_in = [sem(f"agg1_in{k}") for k in range(2)]
        agg_ready = sem("agg_ready")
        x1_saved = [sem(f"x1_saved{k}") for k in range(2)]
        t_saved = [sem(f"t_saved{k}") for k in range(2)]
        invd_set = sem("invd_set")
        (eps_set, x_sum, x_mean, x_centred, x_square, x_var, x_dev, x_inv, h_ready, xb_ready,
         hx_turned, hxT_out, hid_done, hid_out, mlp_done, x1_ready, x1o_ready,
         y_sum, y_mean, y_centred, y_square, y_var, y_dev, y_inv, y_ready,
         y_turned, yT_out, t_done, t_out, ad_out) = (sem(n) for n in (
            "eps_set", "x_sum", "x_mean", "x_centred", "x_square", "x_var", "x_dev", "x_inv", "h_ready", "xb_ready",
            "hx_turned", "hxT_out", "hid_done", "hid_out", "mlp_done", "x1_ready", "x1o_ready",
            "y_sum", "y_mean", "y_centred", "y_square", "y_var", "y_dev", "y_inv", "y_ready",
            "y_turned", "yT_out", "t_done", "t_out", "ad_out"))
        block = tmp.block()

        def bc(v):
            return v.unsqueeze(2).to_broadcast([P, J, D])

        def within(t):
            return not isinstance(t, int) or 0 <= t < CHUNKS

        def run(eng, body, ahead=0):
            steps(eng, CHUNKS, 8, 4, body, 3, ahead)

        def sems16(t, k, every):
            return 16 * (t // every + 1) if isinstance(t, int) else (16 // every) * (t - k % every) + 16

        @block.sync
        def _(sp):
            def load_x(s, k):
                wait(sp, xb_ready, s - 3)
                wait(sp, x_centred, s - 3)
                sp.dma_start(xt[:, k % 4].rearrange("p j c -> p (j c)"),
                             flat(W["x"], chunk_base(s), J, D)).then_inc(x_in[k % 4], 16)

            def body(s, k):
                if isinstance(s, int) and s == 0:
                    load_x(0, 0)
                if not isinstance(s, int) or s + 1 < CHUNKS:
                    load_x(s + 1, k + 1)
                if within(s):
                    wait(sp, hx_turned, 2 * (s - 1))
                    aggr = W["agg"][0].rearrange("n c -> (n c)")[bass.ds(chunk_base(s) * D, CH * D)]
                    sp.dma_start(hx[:, k % 2, :, D:2 * D],
                                 aggr.rearrange("(p j c) -> p j c", p=P, j=J)).then_inc(agg_in[k % 2], 16)
                    wait(sp, agg_ready, s - 1)
                    sp.dma_start(agg1[:, k % 2].rearrange("p j c -> p (j c)"),
                                 flat(W["agg"][1], chunk_base(s), J, D)).then_inc(agg1_in[k % 2], 16)
                t = s - 3
                if within(t - 1):
                    save_table(t - 1, k)
                if within(t):
                    tb = (k - 3) % 2
                    if isinstance(t, int) and t == CHUNKS - 1:
                        sp.wait_ge(x1_saved[1 - tb], 16 * (CHUNKS // 2))
                    sp.wait_ge(x1o_ready, t + 1)
                    sp.dma_start(flat(W["x1"], chunk_base(t), J, D),
                                 x1o[:, tb].rearrange("p j c -> p (j c)")).then_inc(x1_saved[tb], 16)

            def save_table(t, k):
                tb = k % 2
                if isinstance(t, int) and t == CHUNKS - 1:
                    sp.wait_ge(t_saved[1 - tb], 16 * (CHUNKS // 2))
                sp.wait_ge(t_out, t + 1)
                sp.dma_start(flat(W["tab"], chunk_base(t), J, ROW),
                             tt[:, tb].rearrange("p j c -> p (j c)")).then_inc(t_saved[tb], 16)
            run(sp, body, 1)
            save_table(CHUNKS - 1, CHUNKS - 1)
            for k in range(2):
                sp.wait_ge(x1_saved[k], 16 * ((CHUNKS + 1 - k) // 2))
                sp.wait_ge(t_saved[k], 16 * ((CHUNKS + 1 - k) // 2))

        @block.vector
        def _(dve):
            nc.vector.memset(eps[:], EPS).then_inc(eps_set, 1)

            def body(s, k):
                t = s - 3
                b, c = k % 2, (k - 3) % 2
                if within(t):
                    dve.wait_ge(mlp_done, t + 1)
                    dve.wait_ge(xb_ready, t + 1)
                    wait(dve, y_centred, t - 1)
                    wait(dve, x1o_ready, t - 1)
                    nc.vector.tensor_tensor(x1[:, c], ps_o[:], xb[:, (k - 3) % 4], ALU.add).then_inc(x1_ready, 1)
                    dve.wait_ge(x1_ready, t + 1)
                    wait(dve, y_mean, t)
                    nc.vector.tensor_reduce(st[:, 1, 0], x1[:, c], AX.X, ALU.add).then_inc(y_sum, 1)
                if within(s):
                    dve.wait_ge(x_in[k % 4], sems16(s, k, 4))
                    wait(dve, x_mean, s)
                    nc.vector.tensor_reduce(st[:, 0, 0], xt[:, k % 4], AX.X, ALU.add).then_inc(x_sum, 1)
                if within(t):
                    dve.wait_ge(y_square, t + 1)
                    wait(dve, y_dev, t)
                    nc.vector.tensor_reduce(st[:, 1, 2], sqy[:], AX.X, ALU.add).then_inc(y_var, 1)
                    dve.wait_ge(y_dev, t + 1)
                    wait(dve, y_ready, t)
                    nc.vector.reciprocal(st[:, 1, 4], st[:, 1, 3]).then_inc(y_inv, 1)
                    dve.wait_ge(y_inv, t + 1)
                    wait(dve, y_turned, t - 1)
                    nc.vector.scalar_tensor_tensor(out=h1[:, c], in0=yc[:, c], scalar=0.0, in1=bc(st[:, 1, 4]),
                                                   op0=ALU.max, op1=ALU.mult).then_inc(y_ready, 1)
                if within(s):
                    dve.wait_ge(x_square, s + 1)
                    wait(dve, x_dev, s)
                    nc.vector.tensor_reduce(st[:, 0, 2], sq[:], AX.X, ALU.add).then_inc(x_var, 1)
                    dve.wait_ge(x_dev, s + 1)
                    wait(dve, h_ready, s)
                    nc.vector.reciprocal(st[:, 0, 4], st[:, 0, 3]).then_inc(x_inv, 1)
                    dve.wait_ge(x_inv, s + 1)
                    wait(dve, hx_turned, 2 * (s - 1))
                    nc.vector.scalar_tensor_tensor(out=hx[:, b, :, 0:D], in0=xc[:, b], scalar=0.0, in1=bc(st[:, 0, 4]),
                                                   op0=ALU.max, op1=ALU.mult).then_inc(h_ready, 1)
            run(dve, body)

        @block.gpsimd
        def _(pool):
            nc.gpsimd.memset(invd[:], 1.0 / D).then_inc(invd_set, 1)
            pool.wait_ge(invd_set, 1)

            def body(s, k):
                t = s - 3
                b, c = k % 2, (k - 3) % 2
                if within(t):
                    pool.wait_ge(y_sum, t + 1)
                    wait(pool, y_centred, t)
                    nc.gpsimd.tensor_tensor(st[:, 1, 1], st[:, 1, 0], invd[:], ALU.mult).then_inc(y_mean, 1)
                    pool.wait_ge(y_mean, t + 1)
                    wait(pool, y_ready, t - 1)
                    nc.gpsimd.tensor_tensor(yc[:, c], x1[:, c], bc(st[:, 1, 1]), ALU.subtract).then_inc(y_centred, 1)
                if within(s):
                    pool.wait_ge(x_sum, s + 1)
                    wait(pool, x_centred, s)
                    nc.gpsimd.tensor_tensor(st[:, 0, 1], st[:, 0, 0], invd[:], ALU.mult).then_inc(x_mean, 1)
                    pool.wait_ge(x_mean, s + 1)
                    wait(pool, h_ready, s - 1)
                    nc.gpsimd.tensor_tensor(xc[:, b], xt[:, k % 4], bc(st[:, 0, 1]), ALU.subtract).then_inc(x_centred, 1)
                if within(t):
                    wait(pool, x1_saved[c], 16 * (t // 2) if isinstance(t, int) else 8 * (t - c))
                    nc.gpsimd.tensor_tensor(x1o[:, c], x1[:, c], con["gb2row"][:].unsqueeze(1).to_broadcast([P, J, D]),
                                            ALU.add).then_inc(x1o_ready, 1)
                if within(s):
                    wait(pool, x1_ready, s - 3)
                    nc.gpsimd.tensor_tensor(xb[:, k % 4], xt[:, k % 4], con["b2row"][:].unsqueeze(1).to_broadcast([P, J, D]),
                                            ALU.add).then_inc(xb_ready, 1)
                    pool.wait_ge(agg_in[b], sems16(s, k, 2))
                    pool.wait_ge(agg1_in[b], sems16(s, k, 2))
                    nc.gpsimd.tensor_tensor(hx[:, b, :, D:2 * D], hx[:, b, :, D:2 * D], agg1[:, b],
                                            ALU.add).then_inc(agg_ready, 1)
            run(pool, body)

        @block.scalar
        def _(act):
            act.wait_ge(eps_set, 1)

            def body(s, k):
                q, r, t = s - 1, s - 2, s - 3
                b, c = k % 2, (k - 3) % 2

                def relu(n, m):
                    act.wait_ge(hid_done, 4 * r + 2 * n + m + 1)
                    if (n, m) == (0, 0):
                        wait(act, mlp_done, r - 1)
                    nc.scalar.activation(hid[:, b, m, n * 512:n * 512 + 512], ps_h[m][:], ACT.Relu,
                                         bias=con["hbias"][:, m:m + 1]).then_inc(hid_out, 1)

                if within(r):
                    relu(0, 0)
                    relu(0, 1)
                if within(t):
                    act.wait_ge(y_centred, t + 1)
                    wait(act, y_var, t)
                    nc.scalar.activation(sqy[:], yc[:, c], ACT.Square).then_inc(y_square, 1)
                if within(r):
                    relu(1, 0)
                    relu(1, 1)
                if within(t):
                    act.wait_ge(y_var, t + 1)
                    wait(act, y_inv, t)
                    nc.scalar.activation(st[:, 1, 3], st[:, 1, 2], ACT.Sqrt, scale=1.0 / D, bias=eps[:, 0:1]).then_inc(y_dev, 1)
                if within(s):
                    act.wait_ge(x_centred, s + 1)
                    wait(act, x_var, s)
                    nc.scalar.activation(sq[:], xc[:, b], ACT.Square).then_inc(x_square, 1)
                if within(q):
                    for h in range(2):
                        act.wait_ge(hx_turned, 2 * q + h + 1)
                        wait(act, hid_done, 4 * (q - 1))
                        nc.scalar.copy(hxT[:, 1 - b, h * 512:h * 512 + 512],
                                       ps_x[:, 4 * h:4 * h + 4]).then_inc(hxT_out, 1)
                if within(s):
                    act.wait_ge(x_var, s + 1)
                    wait(act, x_inv, s)
                    nc.scalar.activation(st[:, 0, 3], st[:, 0, 2], ACT.Sqrt, scale=1.0 / D, bias=eps[:, 0:1]).then_inc(x_dev, 1)
                if within(t):
                    act.wait_ge(y_turned, t + 1)
                    wait(act, t_done, t)
                    nc.scalar.copy(h1T[:], ps_n[:]).then_inc(yT_out, 1)
                    act.wait_ge(t_done, t + 1)
                    wait(act, t_saved[c], 16 * (t // 2) if isinstance(t, int) else 8 * (t - c))
                    nc.scalar.copy(tt[:, c].rearrange("p (a v) c -> p a (v c)", v=2),
                                   ps_t[:, :, 0:2 * ROW]).then_inc(t_out, 1)
                    nc.scalar.copy(con["ad"][:, bass.ds(t * J, J)].rearrange("p (a v) -> p a v", v=2),
                                   ps_t[:, :, D + 1:2 * ROW:ROW]).then_inc(ad_out, 1)
            run(act, body)

        @block.tensor
        def _(pe):
            def turn_y(t, c):
                if within(t):
                    pe.wait_ge(y_ready, t + 1)
                    wait(pe, yT_out, t)
                    for a in range(4):
                        mm = nc.tensor.transpose(ps_n[:, a, :], h1[:, c, 2 * a:2 * a + 2].rearrange("p j c -> p (j c)"),
                                                 con["ident"][:])
                    mm.then_inc(y_turned, 1)

            def body(s, k):
                q, r, t = s - 1, s - 2, s - 3
                b, c = k % 2, (k - 3) % 2
                if within(r):
                    for n in range(2):
                        pe.wait_ge(hxT_out, 2 * r + n + 1)
                        for m in range(2):
                            wait(pe, hid_out, 4 * r + 2 * n + m - 1)
                            nc.tensor.matmul(ps_h[m][:], con["w1"][:, m * P:m * P + P],
                                             hxT[:, b, n * 512:n * 512 + 512], start=True, stop=True).then_inc(hid_done, 1)
                if within(q):
                    pe.wait_ge(h_ready, q + 1)
                    pe.wait_ge(agg_ready, q + 1)
                    for j in range(J):
                        if j % 4 == 0:
                            wait(pe, hxT_out, 2 * (q - 1) + j // 4 + 1)
                        mm = nc.tensor.transpose(ps_x[:, j, :], hx[:, 1 - b, j, :], con["ident"][:])
                        if j % 4 == 3:
                            mm.then_inc(hx_turned, 1)
                if within(r):
                    wait(pe, x1_ready, r)
                    for j in range(J):
                        if j % 4 == 0:
                            pe.wait_ge(hid_out, 4 * r + j // 4 * 2 + 2)
                        for m in range(2):
                            mm = nc.tensor.matmul(ps_o[:, j, :], hid[:, b, m, j * P:j * P + P], con["w2"][:, m, :],
                                                  start=(m == 0), stop=(m == 1))
                        if j == J // 2:
                            turn_y(t, c)
                    mm.then_inc(mlp_done, 1)
                elif within(t):
                    turn_y(t, c)
                if within(t):
                    pe.wait_ge(yT_out, t + 1)
                    wait(pe, ad_out, t)
                    for a in range(4):
                        mm = nc.tensor.matmul(ps_t[:, a, 0:2 * ROW], h1T[:, a * P:a * P + P], con["bd1"][:],
                                              start=True, stop=True)
                    mm.then_inc(t_done, 1)
            run(pe, body)


def edge_attention(nc, con, W, tag):
    with ExitStack() as ctx:
        tmp = Mem(nc, ctx, tag)
        F = tmp.sb("F", [P, EC, ROW])
        parts = tmp.sb("parts", [P, 3, J * CHUNKS], BF16)
        rest = tmp.sb("rest", [P, 2, J * CHUNKS])
        pick = tmp.sb("pick", [P, J * CHUNKS])
        ade = tmp.sb("ade", [P, EC])
        sc = tmp.sb("sc", [P, 6, EW])
        m = tmp.sb("m", [P, EC + 1])
        prod = tmp.sb("prod", [P, EW, ROW])
        selp = tmp.sb("selp", [P, EPARTS, ROW])
        sel = tmp.sb("sel", [P, ROW])
        val = tmp.sb("val", [P, 2, P])
        wT = tmp.sb("wT", [P, P])
        sm = tmp.sb("sm", [P, 8])
        car = tmp.sb("car", [P, ROW])
        orow = tmp.sb("orow", [P, ROW])
        NB = 4
        ps_g = [tmp.ps(f"ps_g{k}", [P, 512]) for k in range(NB)]
        ps_m, ps_w, ps_c = (tmp.ps(n, [P, 512]) for n in ("ps_m", "ps_w", "ps_c"))
        sem = tmp.sem
        split, fetched, picked = sem("split"), sem("fetched"), sem("picked")
        gathered, scattered, lead_saved = con["gathered"], con["scattered"], con["lead_saved"]
        nz_set, scored, maxed, differ, powers, rows_done = (sem(n) for n in (
            "nz_set", "scored", "maxed", "differ", "powers", "rows_done"))
        dve_step, joined = sem("dve_step"), sem("joined")
        join_pe, join_act, lead_ready = sem("join_pe"), sem("join_act"), sem("lead_ready")
        block = tmp.block()
        NZ_DMAS = 14
        nz_rows = CHUNKS * J // NZ_DMAS

        @block.sync
        def _(sp):
            for k in range(NZ_DMAS):
                sp.dma_start(flat(W["nz"], k * P * nz_rows, nz_rows, ROW),
                             con["nzrows"][:].rearrange("p r c -> p (r c)")).then_inc(nz_set, 16)

        @block.gpsimd
        def _(pool):
            for c in range(EC):
                nc.gpsimd.indirect_dma_start(
                    out=F[:, c, :], out_offset=None, in_=W["tab"],
                    in_offset=bass.IndirectOffsetOnAxis(ap=con["srcg"][:, c:c + 1], axis=0)).then_inc(gathered[c // EW], 16)
            pool.wait_ge(nz_set, 16 * NZ_DMAS)
            for c in range(EC):
                if c % EW == 0:
                    pool.wait_ge(rows_done, c // EW + 1)
                nc.gpsimd.indirect_dma_start(
                    out=W["nz"], out_offset=bass.IndirectOffsetOnAxis(ap=con["rowidx"][:, c:c + 1], axis=0),
                    in_=F[:, c, :], in_offset=None, bounds_check=N - 1, oob_is_err=False).then_inc(scattered, 16)
            pool.wait_ge(lead_ready, 2)
            nc.gpsimd.indirect_dma_start(
                out=W["nz"], out_offset=bass.IndirectOffsetOnAxis(ap=con["leadidx"][:, 0:1], axis=0),
                in_=orow[:], in_offset=None, bounds_check=N - 1, oob_is_err=False).then_inc(lead_saved, 16)
            pool.wait_ge(scattered, 16 * EC)
            pool.wait_ge(lead_saved, 16)

        @block.tensor
        def _(pe):
            pe.wait_ge(split, 5)

            def body(i, k):
                for v in range(NB):
                    wait(pe, picked, NB * (i - 1) + v + 1)
                    for part in range(3):
                        mm = nc.tensor.matmul(ps_g[v][:, 0:J * CHUNKS],
                                              con["onehot"][:, bass.ds(i * NB + v, 1), :].rearrange("p a m -> p (a m)"),
                                              parts[:, part, :], start=(part == 0), stop=(part == 2))
                    mm.then_inc(fetched, 1)
            body(0, 0)
            with pe.Fori(1, EC // NB) as i:
                body(i, 0)
            pe.wait_ge(maxed, EPARTS)
            nc.tensor.matmul(ps_m[:, 0:P], m[:, EC:EC + 1].to_broadcast([P, P]), con["ident"][:],
                             start=True, stop=True).then_inc(join_pe, 1)
            pe.wait_ge(joined, 3)
            nc.tensor.transpose(ps_w[:, 0:P], val[:, 1, :], con["ident"][:]).then_inc(join_pe, 1)
            pe.wait_ge(join_act, 2)
            pe.wait_ge(rows_done, EPARTS)
            nc.tensor.matmul(ps_c[:, 0:ROW - 1], wT[:], F[:, EC - 1, 0:ROW - 1], start=True, stop=True).then_inc(join_pe, 1)

        @block.vector
        def _(dve):
            ad = con["ad"]
            nc.vector.tensor_copy(parts[:, 0, :], ad[:]).then_inc(split, 1)
            dve.wait_ge(split, 1)
            nc.vector.tensor_tensor(rest[:, 0], ad[:], parts[:, 0, :], ALU.subtract).then_inc(split, 1)
            dve.wait_ge(split, 2)
            nc.vector.tensor_copy(parts[:, 1, :], rest[:, 0]).then_inc(split, 1)
            dve.wait_ge(split, 3)
            nc.vector.tensor_tensor(rest[:, 1], rest[:, 0], parts[:, 1, :], ALU.subtract).then_inc(split, 1)
            dve.wait_ge(split, 4)
            nc.vector.tensor_copy(parts[:, 2, :], rest[:, 1]).then_inc(split, 1)

            def body(i):
                for v in range(NB):
                    dve.wait_ge(fetched, NB * i + v + 1)
                    wait(dve, picked, NB * i + v)
                    nc.vector.scalar_tensor_tensor(out=pick[:], in0=con["iota"][:],
                                                   scalar=con["lo"][:, bass.ds(i * NB + v, 1)],
                                                   in1=ps_g[v][:, 0:J * CHUNKS], op0=ALU.is_equal, op1=ALU.mult,
                                                   accum_out=ade[:, bass.ds(i * NB + v, 1)]).then_inc(picked, 1)
            body(0)
            with dve.Fori(1, EC // NB) as i:
                body(i)
            count = [0]

            def link(ins, wait_for_it=True):
                count[0] += 1
                ins.then_inc(dve_step, 1)
                if wait_for_it:
                    dve.wait_ge(dve_step, count[0])

            dve.wait_ge(picked, EC)
            link(nc.vector.memset(m[:, 0:1], -BIG))
            for k in range(EPARTS):
                cols = slice(k * EW, k * EW + EW)
                mk, mprev = m[:, k * EW + 1:k * EW + EW + 1], m[:, k * EW:k * EW + EW]
                dve.wait_ge(gathered[k], 16 * EW)
                link(nc.vector.tensor_tensor(sc[:, 0], F[:, cols, D], ade[:, cols], ALU.add))
                link(nc.vector.scalar_tensor_tensor(out=sc[:, 1], in0=sc[:, 0], scalar=SLOPE, in1=sc[:, 0],
                                                    op0=ALU.mult, op1=ALU.max))
                link(nc.vector.tensor_copy(sm[:, 7:8], m[:, k * EW:k * EW + 1]))
                nc.vector.tensor_tensor_scan(mk, con["cut"][:, cols], sc[:, 1], sm[:, 7:8], ALU.add,
                                             ALU.max).then_inc(maxed, 1)
                dve.wait_ge(maxed, k + 1)
                link(nc.vector.tensor_tensor(sc[:, 2], sc[:, 1], mk, ALU.subtract))
                link(nc.vector.tensor_tensor(sc[:, 3], mprev, mk, ALU.subtract))
                nc.vector.tensor_scalar(sc[:, 3], sc[:, 3], 0.0, None, ALU.min).then_inc(differ, 1)
                dve.wait_ge(powers, k + 1)
                link(nc.vector.tensor_tensor(sc[:, 5], sc[:, 5], con["same"][:, cols], ALU.mult))
                link(nc.vector.tensor_tensor(F[:, cols, 0:D], F[:, cols, 0:D],
                                             sc[:, 4].unsqueeze(2).to_broadcast([P, EW, D]), ALU.mult))
                link(nc.vector.tensor_copy(F[:, cols, D], sc[:, 4]))
                link(nc.vector.tensor_copy(F[:, cols, D + 1], mk))
                for f in range(D + 1):
                    ins = nc.vector.tensor_tensor_scan(
                        F[:, cols, f], sc[:, 5], F[:, cols, f],
                        F[:, k * EW - 1, f:f + 1] if k else 0.0, ALU.mult, ALU.add)
                ins.then_inc(rows_done, 1)
                dve.wait_ge(rows_done, k + 1)
                if k:
                    dve.wait_ge(dve_step, count[0])
                link(nc.vector.tensor_tensor(prod[:], F[:, cols, :],
                                             con["leadend"][:, cols].unsqueeze(2).to_broadcast([P, EW, ROW]), ALU.mult))
                link(nc.vector.tensor_reduce(selp[:, k], prod[:].rearrange("p c f -> p f c"), AX.X, ALU.add))
            link(nc.vector.tensor_reduce(sel[:], selp[:].rearrange("p k f -> p f k"), AX.X, ALU.add))
            dve.wait_ge(join_pe, 1)
            link(nc.vector.tensor_tensor(val[:, 0], ps_m[:, 0:P], con["joins"][:], ALU.mult))
            link(nc.vector.tensor_tensor(val[:, 0], val[:, 0], con["nojoin"][:], ALU.add))
            link(nc.vector.tensor_reduce(sm[:, 0:1], val[:, 0], AX.X, ALU.max))
            nc.vector.tensor_scalar(val[:, 0], val[:, 0], sm[:, 0:1], None, ALU.subtract).then_inc(joined, 1)
            nc.vector.tensor_tensor(sm[:, 1:2], sm[:, 0:1], sel[:, ROW - 1:ROW], ALU.max).then_inc(joined, 1)
            dve.wait_ge(join_act, 1)
            nc.vector.tensor_tensor(val[:, 1], val[:, 1], con["joins"][:], ALU.mult).then_inc(joined, 1)
            dve.wait_ge(joined, 3)
            link(nc.vector.tensor_tensor(sm[:, 2:3], sel[:, ROW - 1:ROW], sm[:, 1:2], ALU.subtract))
            nc.vector.tensor_tensor(sm[:, 3:4], sm[:, 0:1], sm[:, 1:2], ALU.subtract).then_inc(joined, 1)
            dve.wait_ge(join_act, 3)
            dve.wait_ge(join_pe, 3)
            link(nc.vector.tensor_scalar(car[:, 0:ROW - 1], ps_c[:, 0:ROW - 1], sm[:, 5:6], None, ALU.mult))
            nc.vector.tensor_copy(orow[:, ROW - 1:ROW], sm[:, 1:2]).then_inc(lead_ready, 1)
            nc.vector.scalar_tensor_tensor(out=orow[:, 0:ROW - 1], in0=sel[:, 0:ROW - 1], scalar=sm[:, 4:5],
                                           in1=car[:, 0:ROW - 1], op0=ALU.mult, op1=ALU.add).then_inc(lead_ready, 1)

        @block.scalar
        def _(act):
            for k in range(EPARTS):
                act.wait_ge(differ, k + 1)
                nc.scalar.activation(sc[:, 4:6], sc[:, 2:4], ACT.Exp).then_inc(powers, 1)
            act.wait_ge(joined, 1)
            nc.scalar.activation(val[:, 1], val[:, 0], ACT.Exp).then_inc(join_act, 1)
            act.wait_ge(join_pe, 2)
            nc.scalar.copy(wT[:], ps_w[:, 0:P]).then_inc(join_act, 1)
            act.wait_ge(joined, 4)
            nc.scalar.activation(sm[:, 4:6], sm[:, 2:4], ACT.Exp).then_inc(join_act, 1)


def merge(nc, con, W, tag, last):
    with ExitStack() as ctx:
        tmp = Mem(nc, ctx, tag)
        NB = 3
        UC = 4
        UNITS = (CHUNKS - 1) // UC + 1
        assert (CHUNKS - 1) % UC == 0
        tr = tmp.sb("tr", [P, NB, UC * J, ROW])
        nz = tmp.sb("nz", [P, NB, UC * J, ROW])
        g = tmp.sb("g", [P, NB, UC * J, D])
        sc = tmp.sb("sc", [P, NB, 12, UC * J])
        if last:
            xr = tmp.sb("xr", [P, NB, UC * J, D])
        else:
            gT = tmp.sb("gT", [P, 2, CH // 2])
            out = tmp.sb("out", [P, NB, UC * J, ROW])
            ps_n = [tmp.ps(f"ps_n{k}", [P, 4, P]) for k in range(2)]
            ps_t = [tmp.ps(f"ps_t{k}", [P, 4, 256]) for k in range(2)]
        sem = tmp.sem
        tab_in, nz_in, x_in, saved = ([sem(f"{n}{k}") for k in range(NB)] for n in ("tab_in", "nz_in", "x_in", "saved"))
        (self_sum, self_score, top, edge_off, self_off, powers, edge_z, den, inv, edge_w, self_w, edge_part, self_part, x_part,
         merged, turned, gT_out, t_done, t_out, ad_out) = (sem(n) for n in (
            "self_sum", "self_score", "top", "edge_off", "self_off", "powers", "edge_z", "den", "inv", "edge_w", "self_w",
            "edge_part", "self_part", "x_part", "merged", "turned", "gT_out", "t_done", "t_out", "ad_out"))
        block = tmp.block()

        def within(t):
            return not isinstance(t, int) or 0 <= t < UNITS

        def chunks_of(t):
            return 1 if isinstance(t, int) and t == UNITS - 1 else UC

        def unit_dram(dram, t, width):
            n = chunks_of(t)
            start = LAST if isinstance(t, int) and t == UNITS - 1 else t * (UC * CH)
            f = dram.rearrange("n c -> (n c)")
            return f[bass.ds(start * width, n * CH * width)].rearrange("(c p f) -> p c f", c=n, p=P)

        def unit_tile(tile, t, k):
            n = chunks_of(t)
            return tile[:, k % NB, 0:n * J].rearrange("p (c j) f -> p c (j f)", c=n)

        def run(eng, body):
            trips = (UNITS - 1) // NB
            for t in range(2 * NB):
                body(t, t, t // NB)
            with eng.Fori(2, trips) as r:
                for b in range(NB):
                    body(r * NB + b, b, r)
            for t in range(trips * NB, UNITS + 1):
                body(t, t, t // NB)

        def before(r, k):
            return r - 1 if k % NB == 0 else r

        @block.sync
        def _(sp):
            def body(s, k, r):
                if within(s):
                    wait(sp, merged, s - NB + 1)
                    sp.dma_start(unit_tile(tr, s, k), unit_dram(W["tab"], s, ROW)).then_inc(tab_in[k % NB], 16)
                    sp.dma_start(unit_tile(nz, s, k), unit_dram(W["nz"], s, ROW)).then_inc(nz_in[k % NB], 16)
                    if last:
                        sp.dma_start(unit_tile(xr, s, k), unit_dram(W["x1"], s, D)).then_inc(x_in[k % NB], 16)
            run(sp, body)

        def save(act, t, c, dram, tile, width):
            if isinstance(t, int) and t == UNITS - 1:
                act.wait_ge(saved[(t - 1) % NB], 16 * ((t - 1) // NB + 1))
            act.dma_start(unit_dram(dram, t, width), unit_tile(tile, t, c)).then_inc(saved[c], 16)

        @block.vector
        def _(dve):
            def body(s, k, r):
                if within(s):
                    b = k % NB
                    n = chunks_of(s) * J
                    v = [sc[:, b, i, 0:n] for i in range(12)]
                    dve.wait_ge(tab_in[b], 16 * r + 16)
                    dve.wait_ge(nz_in[b], 16 * r + 16)
                    wait(dve, merged, s - NB + 1)
                    nc.vector.tensor_tensor(v[0], tr[:, b, 0:n, D], tr[:, b, 0:n, D + 1], ALU.add).then_inc(self_sum, 1)
                    dve.wait_ge(self_sum, s + 1)
                    nc.vector.scalar_tensor_tensor(out=v[1], in0=v[0], scalar=SLOPE, in1=v[0], op0=ALU.mult,
                                                   op1=ALU.max).then_inc(self_score, 1)
                    dve.wait_ge(self_score, s + 1)
                    nc.vector.tensor_tensor(v[2], v[1], nz[:, b, 0:n, D + 1], ALU.max).then_inc(top, 1)
                    dve.wait_ge(top, s + 1)
                    nc.vector.tensor_tensor(v[4], nz[:, b, 0:n, D + 1], v[2], ALU.subtract).then_inc(edge_off, 1)
                    nc.vector.tensor_tensor(v[5], v[1], v[2], ALU.subtract).then_inc(self_off, 1)
                t = s - 1
                if within(t):
                    c = (k - 1) % NB
                    n = chunks_of(t) * J
                    w = [sc[:, c, i, 0:n] for i in range(12)]
                    dve.wait_ge(powers, t + 1)
                    nc.vector.tensor_tensor(w[8], w[6], nz[:, c, 0:n, D], ALU.mult).then_inc(edge_z, 1)
                    dve.wait_ge(edge_z, t + 1)
                    nc.vector.scalar_tensor_tensor(out=w[9], in0=w[7], scalar=1e-16, in1=w[8], op0=ALU.add,
                                                   op1=ALU.add).then_inc(den, 1)
                    dve.wait_ge(den, t + 1)
                    nc.vector.reciprocal(w[10], w[9]).then_inc(inv, 1)
                    dve.wait_ge(inv, t + 1)
                    nc.vector.tensor_tensor(w[3], w[7], w[10], ALU.mult).then_inc(self_w, 1)
                    nc.vector.tensor_tensor(w[11], w[6], w[10], ALU.mult).then_inc(edge_w, 1)
                    dve.wait_ge(edge_w, t + 1)
                    rows = nz[:, c, 0:n, 0:D]
                    nc.vector.tensor_tensor(rows, rows, w[11].unsqueeze(2).to_broadcast([P, n, D]),
                                            ALU.mult).then_inc(edge_part, 1)
                    dve.wait_ge(edge_part, t + 1)
                    if last:
                        dve.wait_ge(x_in[c], 16 * before(r, k) + 16)
                        nc.vector.tensor_tensor(rows, rows, xr[:, c, 0:n], ALU.add).then_inc(x_part, 1)
                        dve.wait_ge(x_part, t + 1)
                        wait(dve, saved[c], 16 * before(r, k))
                    else:
                        wait(dve, turned, UC * (t - NB + 1))
                    dve.wait_ge(self_part, t + 1)
                    nc.vector.tensor_tensor(g[:, c, 0:n], rows, tr[:, c, 0:n, 0:D], ALU.add).then_inc(merged, 1)
            run(dve, body)

        @block.gpsimd
        def _(pool):
            def body(s, k, r):
                t = s - 1
                if within(t):
                    c = (k - 1) % NB
                    n = chunks_of(t) * J
                    pool.wait_ge(self_w, t + 1)
                    pool.wait_ge(tab_in[c], 16 * before(r, k) + 16)
                    rows = tr[:, c, 0:n, 0:D]
                    nc.gpsimd.tensor_tensor(rows, rows, sc[:, c, 3, 0:n].unsqueeze(2).to_broadcast([P, n, D]),
                                            ALU.mult).then_inc(self_part, 1)
            run(pool, body)

        @block.scalar
        def _(act):
            def body(s, k, r):
                if within(s):
                    b = k % NB
                    n = chunks_of(s) * J
                    act.wait_ge(edge_off, s + 1)
                    act.wait_ge(self_off, s + 1)
                    wait(act, edge_w, s - NB + 1)
                    nc.scalar.activation(sc[:, b, 6:8, 0:n], sc[:, b, 4:6, 0:n], ACT.Exp).then_inc(powers, 1)
                t = s - 1
                if within(t) and not last:
                    c = (k - 1) % NB
                    for i in range(chunks_of(t)):
                        m = UC * t + i
                        act.wait_ge(turned, m + 1)
                        wait(act, t_done, m - 1)
                        nc.scalar.activation(gT[:, i % 2], ps_n[i % 2][:], ACT.Relu,
                                             bias=con["gb1col"][:, 0:1]).then_inc(gT_out, 1)
                        act.wait_ge(t_done, m + 1)
                        if i == 0:
                            wait(act, saved[c], 16 * before(r, k))
                        nc.scalar.copy(out[:, c, i * J:i * J + J].rearrange("p (a v) c -> p a (v c)", v=2),
                                       ps_t[i % 2][:, :, 0:2 * ROW]).then_inc(t_out, 1)
                        nc.scalar.copy(con["ad"][:, bass.ds(m * J, J)].rearrange("p (a v) -> p a v", v=2),
                                       ps_t[i % 2][:, :, D + 1:2 * ROW:ROW]).then_inc(ad_out, 1)
                    act.wait_ge(t_out, UC * t + chunks_of(t))
                    save(act, t, c, W["tab2"], out, ROW)
                if within(t) and last:
                    act.wait_ge(merged, t + 1)
                    save(act, t, (k - 1) % NB, W["out"], g, D)
            run(act, body)
            for k in range(NB):
                act.wait_ge(saved[k], 16 * ((UNITS + NB - 1 - k) // NB))

        if not last:
            @block.tensor
            def _(pe):
                def turn(t, k, i):
                    c = (k - 1) % NB
                    m = UC * t + i
                    if i == 0:
                        pe.wait_ge(merged, t + 1)
                    wait(pe, gT_out, m - 1)
                    for a in range(4):
                        mm = nc.tensor.transpose(ps_n[i % 2][:, a, :],
                                                 g[:, c, i * J + 2 * a:i * J + 2 * a + 2].rearrange("p j c -> p (j c)"),
                                                 con["ident"][:])
                    mm.then_inc(turned, 1)

                def body(s, k, r):
                    t = s - 1
                    if within(t):
                        n = chunks_of(t)
                        turn(t, k, 0)
                        for i in range(n):
                            m = UC * t + i
                            if i + 1 < n:
                                turn(t, k, i + 1)
                            pe.wait_ge(gT_out, m + 1)
                            wait(pe, ad_out, m - 1)
                            for a in range(4):
                                mm = nc.tensor.matmul(ps_t[i % 2][:, a, 0:2 * ROW], gT[:, i % 2, a * P:a * P + P],
                                                      con["bd2"][:], start=True, stop=True)
                            mm.then_inc(t_done, 1)
                run(pe, body)


def graph_kernel(nc, W):
    with ExitStack() as ctx:
        mem = Mem(nc, ctx, "all")
        shapes = dict(zero=[P, AGG_ROWS // P // ZERO_DMAS * D], ident=[P, P], later=[P, P], earlier=[P, P],
                      iota=[P, J * CHUNKS], dummy=[P, GROUPS * GT], pidx=[P, 1], nzrows=[P, CHUNKS * J // 14, ROW],
                      bd1=[P, 2 * ROW], bd2=[P, 2 * ROW], w1=[P, HID], w2=[P, 2, D], hbias=[P, 2], b2row=[P, D],
                      gb2row=[P, D], gb1col=[P, 1], lastkey=[P, 1], same=[P, EC], cut=[P, EC], leadend=[P, EC],
                      lo=[P, EC], joins=[P, P], nojoin=[P, P], srckey=[P, GROUPS * GT], dumdiff=[P, GROUPS * GT],
                      ad=[P, J * CHUNKS])
        con = {n: mem.sb(n, s) for n, s in shapes.items()}
        con.update(onehot=mem.sb("onehot", [P, EC, P], BF16), identb=mem.sb("identb", [P, P], BF16),
                   high4=mem.sb("high4", [P, 4, EC // 4], BF16), laterb=mem.sb("laterb", [P, P], BF16), srcg=mem.sb("srcg", [P, EC], I32),
                   rowidx=mem.sb("rowidx", [P, EC], I32), leadidx=mem.sb("leadidx", [P, 1], I32),
                   agg_zeroed=[mem.sem(f"agg_zeroed{k}") for k in range(2)])
        con["added"] = [mem.sem(f"added{k}") for k in range(2)]
        swdge = [dict(gathered=[mem.sem(f"gathered{l}_{k}") for k in range(EPARTS)], scattered=mem.sem(f"scattered{l}"),
                      lead_saved=mem.sem(f"lead_saved{l}")) for l in range(2)]
        W["agg"] = [nc.dram_tensor(f"agg_table{k}", (AGG_ROWS, D), F32).ap() for k in range(2)]
        W["x1"] = nc.dram_tensor("x1_table", (N, D), F32).ap()
        W["tab"] = nc.dram_tensor("att_table1", (N, ROW), F32).ap()
        W["nz"] = nc.dram_tensor("nz_table", (CHUNKS * CH, ROW), F32).ap()
        tab2 = nc.dram_tensor("att_table2", (N, ROW), F32).ap()
        W["tab2"] = tab2
        setup(nc, mem, con, W)
        sum_edges(nc, con, W)
        mlp(nc, con, W)
        edge_attention(nc, con | swdge[0], W, "att1")
        merge(nc, con, W, "merge1", False)
        W["tab"] = tab2
        edge_attention(nc, con | swdge[1], W, "att2")
        merge(nc, con, W, "merge2", True)


_INS = {'x': 'x', 'src': 'src', 'dst': 'dst', 'edge_attr_64': 'ea', 'L0_gnn_u': 'u', 'L0_gnn_W1': 'W1', 'L0_gnn_b1': 'b1',
        'L0_gnn_W2': 'W2', 'L0_gnn_b2': 'b2', 'L1_gnn_W1': 'gW1', 'L1_gnn_a_src1': 'as1', 'L1_gnn_a_dst1': 'ad1',
        'L1_gnn_b1': 'gb1', 'L1_gnn_W2': 'gW2', 'L1_gnn_a_src2': 'as2', 'L1_gnn_a_dst2': 'ad2', 'L1_gnn_b2': 'gb2'}


def kernel(**inputs):
    import numpy as _np
    import concourse.bacc as _bacc
    from concourse import mybir as _mybir
    from concourse.bass_utils import run_bass_kernel_spmd as _run

    nc = _bacc.Bacc("TRN2", target_bir_lowering=False, num_devices=1)
    arrays, args = {}, {}
    for name, short in _INS.items():
        a = _np.ascontiguousarray(inputs[name])
        arrays[f"in_{name}_dram"] = a
        args[short] = nc.dram_tensor(f"in_{name}_dram", a.shape, _mybir.dt.from_np(a.dtype), kind="ExternalInput").ap()
    args["out"] = nc.dram_tensor("out_0_dram", (N, D), _mybir.dt.float32, kind="ExternalOutput").ap()
    graph_kernel(nc, args)
    r = _run(nc, [arrays], core_ids=[0])
    return r.results[0]["out_0_dram"]
```

```python
from contextlib import ExitStack

import concourse.bass as bass
from concourse import mybir
from concourse.alu_op_type import AluOpType as ALU

F32 = mybir.dt.float32
BF16 = mybir.dt.bfloat16
I32 = mybir.dt.int32
ACT = mybir.ActivationFunctionType
AX = mybir.AxisListType

P = 128
BIG = 1.0e30
EPS = 1e-5
SLOPE = 0.2

N = 50000
E = 25000
D = 64
HID = 256
ROW = D + 2

J = 8
CH = P * J
CHUNKS = -(-N // CH)
LAST = N - CH
SHIFT = (CHUNKS - 1) * CH - LAST

EC = -(-E // P)
EPARTS = 4
EW = EC // EPARTS
FULLP = E // EC
RESTC = E - FULLP * EC

GT = 4
GE = P * GT
GROUPS = -(-E // GE)
ALONE = 4
LASTE = E - (GROUPS - 1) * GE
PADROW = N + GE
ZERO_DMAS = 24
EARLY_ZEROS = 6
AGG_ROWS = -(-(PADROW + 1) // (P * ZERO_DMAS)) * P * ZERO_DMAS
ZERO_ROWS = AGG_ROWS // (P * ZERO_DMAS)
SKIP = 1 << 16


def wait(eng, sem, value):
    if isinstance(value, int) and value <= 0:
        return
    eng.wait_ge(sem, value)


def steps(eng, count, lead, unroll, body, tail, ahead=0):
    trips = (count - 1 - ahead) // unroll
    for t in range(lead):
        body(t, t)
    with eng.Fori(lead // unroll, trips) as r:
        for b in range(unroll):
            body(r * unroll + b, b)
    for t in range(trips * unroll, count + tail):
        body(t, t)


def chunk_base(t):
    return min(t * CH, LAST) if isinstance(t, int) else t * CH


def flat(dram, start, rows, width):
    f = dram.rearrange("n c -> (n c)")
    return f[bass.ds(start * width, P * rows * width)].rearrange("(p f) -> p f", p=P)


class Mem:

    def __init__(self, nc, ctx, tag):
        self.nc, self.ctx, self.tag = nc, ctx, tag
        self.sems = []

    def sb(self, name, shape, dt=F32):
        return self.ctx.enter_context(self.nc.sbuf_tensor(f"{name}_{self.tag}", shape, dt))

    def ps(self, name, shape):
        return self.ctx.enter_context(self.nc.psum_tensor(f"{name}_{self.tag}", shape, F32))

    def sem(self, name):
        self.sems.append(self.ctx.enter_context(self.nc.semaphore(f"{name}_{self.tag}")))
        return self.sems[-1]

    def block(self):
        numbers = sorted(s.num for s in self.sems)

        def clear():
            start = numbers[0]
            for a, b in zip(numbers, numbers[1:] + [None]):
                if b != a + 1:
                    self.nc.gpsimd.sem_clear(range(start, a + 1))
                    start = b
        self.ctx.callback(clear)
        return self.ctx.enter_context(self.nc.Block())


def order_edges(nc, con, W):
    with ExitStack() as ctx:
        tmp = Mem(nc, ctx, "order")
        QP = P // EPARTS
        key_i = tmp.sb("key_i", [P, EC + 1], I32)
        src_i = tmp.sb("src_i", [P, EC], I32)
        key = tmp.sb("key", [P, EC + 1])
        falls = tmp.sb("falls", [P, EC])
        anyfall = tmp.sb("anyfall", [P, 1])
        ones = tmp.sb("ones", [P, P])
        half = tmp.sb("half", [P, P])
        flag = tmp.sb("flag", [1, 1], I32)
        row_i = tmp.sb("row_i", [P, QP * EC], I32)
        row = tmp.sb("row", [P, QP * EC])
        junk = tmp.sb("junk", [P, QP * EC])
        seen = tmp.sb("seen", [P, EC])
        count = tmp.sb("count", [P, EPARTS + 1, EC])
        place = tmp.sb("place", [P, EC])
        place_i = tmp.sb("place_i", [P, EC], I32)
        ps_f = tmp.ps("ps_f", [P, 512])
        sem = tmp.sem
        filled, keys_in, srcs_in, copied = sem("filled"), sem("keys_in"), sem("srcs_in"), sem("copied")
        half_set, keyed, falls_found, falls_summed, flag_set = (sem(n) for n in (
            "half_set", "keyed", "falls_found", "falls_summed", "flag_set"))
        row_filled, row_in, row_ready, counted, tied, placed = (sem(n) for n in (
            "row_filled", "row_in", "row_ready", "counted", "tied", "placed"))
        zero_ready = sem("zero_ready")
        ctx.enter_context(nc.allow_non_contiguous_dma(reason="one key of each partition"))
        block = tmp.block()

        @block.sync
        def _(sp):
            sp.wait_ge(filled, 1)
            sp.dma_start(key_i[0:FULLP, 0:EC], W["dst"][0:FULLP * EC].rearrange("(p c) -> p c", c=EC)).then_inc(keys_in, 16)
            sp.dma_start(key_i[FULLP:FULLP + 1, 0:RESTC],
                         W["dst"][FULLP * EC:E].rearrange("(p c) -> p c", p=1)).then_inc(keys_in, 16)
            sp.dma_start(key_i[0:FULLP - 1, EC:EC + 1],
                         W["dst"][EC:FULLP * EC].rearrange("(p c) -> p c", c=EC)[:, 0:1]).then_inc(keys_in, 16)
            sp.dma_start(key_i[FULLP - 1:FULLP, EC:EC + 1],
                         W["dst"][FULLP * EC:FULLP * EC + 1].rearrange("(p c) -> p c", p=1)).then_inc(keys_in, 16)
            for name in ("dst", "src"):
                sp.dma_start(W[f"{name}_ordered"][0:FULLP * EC].rearrange("(p c) -> p c", c=EC),
                             W[name][0:FULLP * EC].rearrange("(p c) -> p c", c=EC)).then_inc(copied, 16)
                sp.dma_start(W[f"{name}_ordered"][FULLP * EC:E].rearrange("(p c) -> p c", p=1),
                             W[name][FULLP * EC:E].rearrange("(p c) -> p c", p=1)).then_inc(copied, 16)
            sp.wait_ge(copied, 16 * 4)
            sp.wait_ge(flag_set, 1)
            unordered = sp.value_load(flag[0:1, 0:1], min_val=0, max_val=P)
            with sp.If(unordered > 0):
                sp.dma_start(src_i[0:FULLP, :], W["src"][0:FULLP * EC].rearrange("(p c) -> p c", c=EC)).then_inc(srcs_in, 16)
                sp.dma_start(src_i[FULLP:FULLP + 1, 0:RESTC],
                             W["src"][FULLP * EC:E].rearrange("(p c) -> p c", p=1)).then_inc(srcs_in, 16)
                for part in range(EPARTS):
                    wait(sp, row_ready, 2 * part)
                    first, n = part * QP * EC, QP * EC
                    if part == EPARTS - 1:
                        sp.wait_ge(row_filled, 1)
                        n = E - first
                    sp.dma_start(row_i[:, 0:n], W["dst"][first:first + n].partition_broadcast(P)).then_inc(row_in, 16)

        @block.scalar
        def _(act):
            act.wait_ge(zero_ready, 1)
            act.wait_ge(keys_in, 16 * 4)
            for k in range(EARLY_ZEROS):
                act.dma_start(flat(W["agg"][0], k * P * ZERO_ROWS, ZERO_ROWS, D),
                              con["zero"][:]).then_inc(con["agg_zeroed"][0], 16)

        @block.tensor
        def _(pe):
            pe.wait_ge(filled, 3)
            pe.wait_ge(falls_found, 2)
            nc.tensor.matmul(ps_f[:, 0:1], ones[:], anyfall[:], start=True, stop=True).then_inc(falls_summed, 1)

        @block.vector
        def _(dve):
            dve.wait_ge(keys_in, 16 * 4)
            nc.vector.tensor_copy(key[:], key_i[:]).then_inc(keyed, 1)
            dve.wait_ge(keyed, 1)
            nc.vector.tensor_tensor(falls[:], key[:, 0:EC], key[:, 1:EC + 1], ALU.is_gt).then_inc(falls_found, 1)
            dve.wait_ge(falls_found, 1)
            nc.vector.tensor_reduce(anyfall[:], falls[:], AX.X, ALU.max).then_inc(falls_found, 1)
            dve.wait_ge(falls_summed, 1)
            nc.vector.tensor_copy(flag[:], ps_f[0:1, 0:1]).then_inc(flag_set, 1)
            dve.wait_ge(flag_set, 1)
            unordered = dve.value_load(flag[0:1, 0:1], min_val=0, max_val=P)
            with dve.If(unordered > 0):
                dve.wait_ge(half_set, 1)
                dve.wait_ge(filled, 3)
                for part in range(EPARTS):
                    dve.wait_ge(row_in, 16 * part + 16)
                    wait(dve, counted, EC * part)
                    nc.vector.tensor_copy(row[:], row_i[:]).then_inc(row_ready, 1)
                    dve.wait_ge(row_ready, 2 * part + 1)
                    view = row[:].rearrange("p (q c) -> p q c", c=EC)
                    nc.vector.tensor_tensor(view, view, half[:, part * QP:part * QP + QP].unsqueeze(2).to_broadcast([P, QP, EC]),
                                            ALU.subtract).then_inc(row_ready, 1)
                    dve.wait_ge(row_ready, 2 * part + 2)
                    if part == EPARTS - 2:
                        nc.vector.memset(row_i[:], N).then_inc(row_filled, 1)

                    def lower(c):
                        nc.vector.scalar_tensor_tensor(
                            out=junk[:], in0=row[:], scalar=key[:, bass.ds(c, 1)], in1=ones[:, 0:1].to_broadcast([P, QP * EC]),
                            op0=ALU.is_lt, op1=ALU.mult, accum_out=count[:, part, bass.ds(c, 1)]).then_inc(counted, 1)
                    wait(dve, counted, EC * part)
                    lower(0)
                    with dve.Fori(1, EC) as c:
                        dve.wait_ge(counted, c + EC * part)
                        lower(c)
                nc.vector.memset(seen[:], -1.0).then_inc(tied, 1)

                def ties(c):
                    dve.wait_ge(tied, c * 2 + 1)
                    wait(dve, counted, EC * EPARTS)
                    nc.vector.scalar_tensor_tensor(
                        out=junk[:, 0:EC], in0=seen[:], scalar=key[:, bass.ds(c, 1)], in1=ones[:, 0:1].to_broadcast([P, EC]),
                        op0=ALU.is_equal, op1=ALU.mult, accum_out=count[:, EPARTS, bass.ds(c, 1)]).then_inc(tied, 1)
                    dve.wait_ge(tied, c * 2 + 2)
                    nc.vector.tensor_copy(seen[:, bass.ds(c, 1)], key[:, bass.ds(c, 1)]).then_inc(tied, 1)
                ties(0)
                with dve.Fori(1, EC) as c:
                    ties(c)
                dve.wait_ge(tied, 2 * EC + 1)
                nc.vector.tensor_reduce(place[:], count[:].rearrange("p k c -> p c k"), AX.X, ALU.add).then_inc(placed, 1)
                dve.wait_ge(placed, 1)
                nc.vector.tensor_copy(place_i[:], place[:]).then_inc(placed, 1)

        @block.gpsimd
        def _(pool):
            nc.gpsimd.memset(key_i[:], N).then_inc(filled, 1)
            nc.gpsimd.memset(src_i[:], 0).then_inc(filled, 1)
            nc.gpsimd.memset(ones[:], 1.0).then_inc(filled, 1)
            nc.gpsimd.memset(half[:], 0.5).then_inc(filled, 1)
            nc.gpsimd.memset(con["zero"][:], 0.0).then_inc(zero_ready, 1)
            pool.wait_ge(filled, 4)
            nc.gpsimd.affine_select(out=half[:], in_=half[:], compare_op=ALU.is_gt, fill=0.0, base=0,
                                    pattern=[[-1, P]], channel_multiplier=1).then_inc(half_set, 1)
            pool.wait_ge(flag_set, 1)
            unordered = pool.value_load(flag[0:1, 0:1], min_val=0, max_val=P)
            with pool.If(unordered > 0):
                pool.wait_ge(copied, 16 * 4)
                pool.wait_ge(srcs_in, 16 * 2)
                pool.wait_ge(placed, 2)
                for name, tile in (("dst", key_i), ("src", src_i)):
                    for c in range(EC):
                        nc.gpsimd.indirect_dma_start(
                            out=W[f"{name}_ordered"].rearrange("(n o) -> n o", o=1),
                            out_offset=bass.IndirectOffsetOnAxis(ap=place_i[:, c:c + 1], axis=0),
                            in_=tile[:, c:c + 1], in_offset=None, bounds_check=E - 1,
                            oob_is_err=False).then_inc(con["reordered"], 16)
                pool.wait_ge(con["reordered"], 16 * 2 * EC)


def setup(nc, mem, con, W):
    with ExitStack() as ctx:
        tmp = Mem(nc, ctx, "setup")
        io392 = tmp.sb("io392", [P, J * CHUNKS], I32)
        dumi = tmp.sb("dumi", [P, GROUPS, GT], I32)
        piota = tmp.sb("piota", [P, 1], I32)
        ones = tmp.sb("ones", [P, P])
        srcc = tmp.sb("srcc", [P, GROUPS * GT], I32)
        di = tmp.sb("di", [P, EC + 2], I32)
        u0 = tmp.sb("u0", [16, 1])
        w1u = tmp.sb("w1u", [16, HID])
        b1c = tmp.sb("b1c", [P, 2])
        wst = tmp.sb("wst", [P, 2, D])
        wT = tmp.sb("wT", [D, 2, P])
        av = tmp.sb("av", [D, 2, 2])
        q = tmp.sb("q", [P, 12, EC])
        qi = tmp.sb("qi", [P, 6, EC], I32)
        nend = tmp.sb("nend", [P, 4])
        ps_u = tmp.ps("ps_u", [P, 512])
        ps_w = tmp.ps("ps_w", [P, 512])
        ps_a = tmp.ps("ps_a", [P, 512])
        ps_f = tmp.ps("ps_f", [P, 512])
        sem = tmp.sem
        pooled, loaded, filled = sem("pooled"), sem("loaded"), sem("filled")
        edge_loaded, table_zeroed = sem("edge_loaded"), con["agg_zeroed"][0]
        dve_step, pe_step, act_step = sem("dve_step"), sem("pe_step"), sem("act_step")

        ctx.enter_context(nc.allow_non_contiguous_dma(reason="a few hundred single keys, vectors as columns"))
        block = tmp.block()

        @block.gpsimd
        def _(pool):
            nc.gpsimd.memset(ones[:], 1.0).then_inc(filled, 1)
            nc.gpsimd.memset(con["bd1"][:], 0.0).then_inc(filled, 1)
            nc.gpsimd.memset(con["bd2"][:], 0.0).then_inc(filled, 1)
            nc.gpsimd.memset(di[:], N).then_inc(filled, 1)
            nc.gpsimd.memset(con["srcg"][:], 0).then_inc(filled, 1)
            nc.gpsimd.memset(srcc[:], PADROW).then_inc(filled, 1)
            nc.gpsimd.iota(io392[:], pattern=[[1, J * CHUNKS]], base=0, channel_multiplier=0).then_inc(filled, 1)
            nc.gpsimd.iota(dumi[:], pattern=[[0, GROUPS], [P, GT]], base=N, channel_multiplier=1).then_inc(filled, 1)
            nc.gpsimd.iota(piota[:], pattern=[[0, 1]], base=0, channel_multiplier=1).then_inc(filled, 1)
            pool.wait_ge(filled, 9)
            nc.gpsimd.affine_select(out=con["ident"][:], in_=ones[:], compare_op=ALU.is_equal, fill=0.0, base=0,
                                    pattern=[[1, P]], channel_multiplier=-1).then_inc(pooled, 1)
            nc.gpsimd.affine_select(out=con["later"][:], in_=ones[:], compare_op=ALU.is_gt, fill=0.0, base=0,
                                    pattern=[[1, P]], channel_multiplier=-1).then_inc(pooled, 1)
            nc.gpsimd.affine_select(out=con["earlier"][:], in_=ones[:], compare_op=ALU.is_gt, fill=0.0, base=0,
                                    pattern=[[-1, P]], channel_multiplier=1).then_inc(pooled, 1)
            nc.gpsimd.tensor_copy(con["iota"][:], io392[:]).then_inc(pooled, 1)
            nc.gpsimd.tensor_copy(con["dummy"][:], dumi[:].rearrange("p g i -> p (g i)")).then_inc(pooled, 1)
            nc.gpsimd.tensor_copy(con["pidx"][:], piota[:]).then_inc(pooled, 1)
            nc.gpsimd.memset(con["nzrows"][:], 0.0).then_inc(pooled, 1)
            pool.wait_ge(pooled, 7)
            nc.gpsimd.memset(con["nzrows"][:, :, ROW - 1:ROW], -BIG).then_inc(pooled, 1)

        @block.sync
        def _(sp):
            def load(dst, src):
                sp.dma_start(dst, src).then_inc(loaded, 16)

            sp.wait_ge(filled, 6)
            main = (GROUPS - 1) * GE
            src_g = W["src"][0:main].rearrange("(g p i) -> p g i", p=P, i=GT)
            sp.dma_start(srcc[:, 0:(GROUPS - 1) * GT].rearrange("p (g i) -> p g i", i=GT), src_g).then_inc(edge_loaded, 16)
            sp.dma_start(srcc[0:LASTE // GT, (GROUPS - 1) * GT:],
                         W["src"][main:E].rearrange("(p i) -> p i", i=GT)).then_inc(edge_loaded, 16)
            sp.dma_start(di[0:FULLP, 1:EC + 1], W["dst_ordered"][0:FULLP * EC].rearrange("(p c) -> p c", c=EC)).then_inc(edge_loaded, 16)
            sp.dma_start(di[FULLP:FULLP + 1, 1:RESTC + 1],
                         W["dst_ordered"][FULLP * EC:E].rearrange("(p c) -> p c", p=1)).then_inc(edge_loaded, 16)
            sp.dma_start(di[1:FULLP + 1, 0:1], W["dst_ordered"][0:FULLP * EC].rearrange("(p c) -> p c", c=EC)[:, EC - 1:EC]).then_inc(edge_loaded, 16)
            sp.dma_start(di[0:FULLP - 1, EC + 1:EC + 2],
                         W["dst_ordered"][EC:FULLP * EC].rearrange("(p c) -> p c", c=EC)[:, 0:1]).then_inc(edge_loaded, 16)
            sp.dma_start(di[FULLP - 1:FULLP, EC + 1:EC + 2],
                         W["dst_ordered"][FULLP * EC:FULLP * EC + 1].rearrange("(p c) -> p c", p=1)).then_inc(edge_loaded, 16)
            sp.dma_start(con["srcg"][0:FULLP, :], W["src_ordered"][0:FULLP * EC].rearrange("(p c) -> p c", c=EC)).then_inc(edge_loaded, 16)
            sp.dma_start(con["srcg"][FULLP:FULLP + 1, 0:RESTC],
                         W["src_ordered"][FULLP * EC:E].rearrange("(p c) -> p c", p=1)).then_inc(edge_loaded, 16)
            load(con["w1"][:], W["W1"][0:P, :])
            load(w1u[:], W["W1"][P:P + 16, :])
            load(u0[:], W["u"][0:1, :].rearrange("a c -> c a"))
            load(b1c[:], W["b1"].rearrange("(m p) -> p m", p=P))
            load(con["w2"][:], W["W2"].rearrange("(m p) n -> p m n", p=P))
            load(con["b2row"][:], W["b2"].partition_broadcast(P))
            load(con["gb2row"][:], W["gb2"].partition_broadcast(P))
            for l, (w, bd) in enumerate((("gW1", "bd1"), ("gW2", "bd2"))):
                for h in range(2):
                    load(wst[D * h:D * h + D, l, :], W[w])
                    load(con[bd][D * h:D * h + D, ROW * h:ROW * h + D], W[w])
                load(av[:, l, 0:1], W[f"as{l + 1}"].rearrange("(n o) -> n o", o=1))
                load(av[:, l, 1:2], W[f"ad{l + 1}"].rearrange("(n o) -> n o", o=1))
            for h in range(2):
                load(con["gb1col"][D * h:D * h + D, :], W["gb1"].rearrange("(n o) -> n o", o=1))

        @block.scalar
        def _(act):
            act.wait_ge(edge_loaded, 16 * 9)
            for k in range(EARLY_ZEROS, ZERO_DMAS):
                act.dma_start(flat(W["agg"][0], k * P * ZERO_ROWS, ZERO_ROWS, D), con["zero"][:]).then_inc(table_zeroed, 16)

        @block.tensor
        def _(pe):
            pe.wait_ge(loaded, 16 * 21)
            pe.wait_ge(pooled, 1)
            for m in range(2):
                mm = nc.tensor.matmul(ps_u[:, m:m + 1], w1u[:, m * P:m * P + P], u0[:, :], start=True, stop=True)
            mm.then_inc(pe_step, 1)
            for l in range(2):
                mm = nc.tensor.transpose(ps_w[0:D, l * P:l * P + P], wst[:, l, :], con["ident"][:])
            mm.then_inc(pe_step, 1)
            pe.wait_ge(act_step, 2)
            for l in range(2):
                mm = nc.tensor.matmul(ps_a[:, 2 * l:2 * l + 2], wT[:, l, :], av[:, l, :], start=True, stop=True)
            mm.then_inc(pe_step, 1)
            pe.wait_ge(dve_step, 1)
            nc.tensor.matmul(ps_f[:, 0:P], q[:, 0, EC - 1:EC].to_broadcast([P, P]), con["ident"][:],
                             start=True, stop=True).then_inc(pe_step, 1)

        @block.scalar
        def _(act):
            act.wait_ge(pe_step, 1)
            act.wait_ge(loaded, 16 * 21)
            for m in range(2):
                ins = nc.scalar.activation(con["hbias"][:, m:m + 1], ps_u[:, m:m + 1], ACT.Identity, bias=b1c[:, m:m + 1])
            ins.then_inc(act_step, 1)
            act.wait_ge(pe_step, 2)
            nc.scalar.copy(wT[:].rearrange("p l k -> p (l k)"), ps_w[0:D, 0:2 * P]).then_inc(act_step, 1)
            act.wait_ge(pe_step, 3)
            for l, bd in enumerate(("bd1", "bd2")):
                for h in range(2):
                    ins = nc.scalar.copy(con[bd][D * h:D * h + D, ROW * h + D:ROW * h + ROW],
                                         ps_a[D * h:D * h + D, 2 * l:2 * l + 2])
            ins.then_inc(act_step, 1)

        @block.vector
        def _(dve):
            count = [0]

            def link(ins):
                count[0] += 1
                ins.then_inc(dve_step, 1)
                dve.wait_ge(dve_step, count[0])

            dve.wait_ge(edge_loaded, 16 * 9)
            dve.wait_ge(pooled, 8)
            d = di[:, 1:EC + 1]
            key, prv, nxt, t0, t1, same, endf, lead, t2 = (q[:, k, :] for k in range(9))
            link(nc.vector.tensor_copy(key, d))
            link(nc.vector.tensor_copy(prv, di[:, 0:EC]))
            link(nc.vector.tensor_copy(nxt, di[:, 2:EC + 2]))
            link(nc.vector.tensor_tensor(same, key, prv, ALU.is_equal))
            link(nc.vector.tensor_tensor(endf, key, nxt, ALU.not_equal))
            link(nc.vector.memset(t0, 1.0))
            link(nc.vector.memset(t0[:, 0:1], 0.0))
            link(nc.vector.tensor_tensor(con["same"][:], same, t0, ALU.mult))
            link(nc.vector.tensor_scalar(con["cut"][:], con["same"][:], BIG, -BIG, ALU.mult, ALU.add))
            link(nc.vector.tensor_tensor(t1[:, 0:1], prv[:, 0:1], con["pidx"][:], ALU.add))
            link(nc.vector.tensor_scalar(t1[:, 1:2], con["pidx"][:], 0.5, None, ALU.is_ge))
            link(nc.vector.tensor_scalar(lead, key, prv[:, 0:1], t1[:, 1:2], ALU.is_equal, ALU.mult))
            link(nc.vector.tensor_tensor(con["leadend"][:], lead, endf, ALU.mult))
            link(nc.vector.tensor_tensor(t2, endf, con["leadend"][:], ALU.subtract))
            link(nc.vector.tensor_scalar(t0, t2, -float(SKIP), float(SKIP), ALU.mult, ALU.add))
            link(nc.vector.tensor_tensor(con["rowidx"][:], t0, key, ALU.add))
            link(nc.vector.tensor_reduce(nend[:, 0:1], con["leadend"][:], AX.X, ALU.add))
            link(nc.vector.tensor_scalar(nend[:, 1:2], nend[:, 0:1], -float(SKIP), float(SKIP), ALU.mult, ALU.add))
            link(nc.vector.tensor_tensor(con["leadidx"][:], nend[:, 1:2], key[:, 0:1], ALU.add))
            link(nc.vector.tensor_scalar(t0, key, float((CHUNKS - 1) * CH), float(SHIFT), ALU.is_ge, ALU.mult))
            link(nc.vector.tensor_tensor(qi[:, 0, :], t0, key, ALU.add))
            link(nc.vector.tensor_scalar(qi[:, 1, :], qi[:, 0, :], J.bit_length() - 1, P - 1,
                                         ALU.logical_shift_right, ALU.bitwise_and))
            link(nc.vector.tensor_scalar(qi[:, 2, :], qi[:, 0, :], CH.bit_length() - 1, J.bit_length() - 1,
                                         ALU.logical_shift_right, ALU.logical_shift_left))
            link(nc.vector.tensor_scalar(qi[:, 3, :], qi[:, 0, :], J - 1, None, ALU.bitwise_and))
            link(nc.vector.tensor_tensor(con["lo"][:], qi[:, 2, :], qi[:, 3, :], ALU.add))
            link(nc.vector.tensor_copy(con["identb"][:], con["ident"][:]))
            link(nc.vector.tensor_copy(con["high4"][:].rearrange("p k g -> p g k"), qi[:, 1, :].rearrange("p (g k) -> p g k", k=4)))
            link(nc.vector.tensor_copy(con["laterb"][:], con["later"][:]))
            dve.wait_ge(pe_step, 4)
            link(nc.vector.tensor_scalar(con["joins"][:], ps_f[:, 0:P], key[:, 0:1], None, ALU.is_equal))
            link(nc.vector.tensor_tensor(con["joins"][:], con["joins"][:], con["earlier"][:], ALU.mult))
            link(nc.vector.tensor_scalar(con["nojoin"][:], con["joins"][:], BIG, -BIG, ALU.mult, ALU.add))
            link(nc.vector.tensor_copy(con["srckey"][:], srcc[:]))
            link(nc.vector.tensor_tensor(con["dumdiff"][:], con["dummy"][:], con["srckey"][:], ALU.subtract))


def sum_edges(nc, con, W):
    with ExitStack() as ctx:
        tmp = Mem(nc, ctx, "agg")
        krow = tmp.sb("krow", [P, 2, GE], I32)
        ea = tmp.sb("ea", [P, 2, GT, D])
        rest = tmp.sb("rest", [P, 2, 2, GT, D])
        part = tmp.sb("part", [P, 2, 3, GT, D], BF16)
        eq = tmp.sb("eq", [P, 2, GT, GT, P], BF16)
        diag = tmp.sb("diag", [P, 2, GT, P], BF16)
        onec = tmp.sb("onec", [P, 1], BF16)
        tot = tmp.sb("tot", [P, 2, GT, D])
        away = tmp.sb("away", [P, 2, GT])
        idx = tmp.sb("idx", [P, 2, GT], I32)
        ps_t = [tmp.ps(f"ps_t{b}", [P, GT, P]) for b in range(2)]
        ps_d = [tmp.ps(f"ps_d{b}", [P, 512]) for b in range(2)]
        ps_h = [tmp.ps(f"ps_h{b}", [P, 4, P]) for b in range(2)]
        sem = tmp.sem
        keys_in, attr_in = [sem("keys_in0"), sem("keys_in1")], [sem("attr_in0"), sem("attr_in1")]
        padded, eq_built, diag_built, ones_set = sem("padded"), sem("eq_built"), sem("diag_built"), sem("ones_set")
        part0_out, part1_out, part2_out = sem("part0_out"), sem("part1_out"), sem("part2_out")
        rest1_out, rest2_out = sem("rest1_out"), sem("rest2_out")
        summed, counted = sem("summed"), sem("counted")
        sums_out, away_out, idx_out = sem("sums_out"), sem("away_out"), sem("idx_out")
        hi_spread, onehot_made = sem("hi_spread"), sem("onehot_made")
        added = con["added"]
        block = tmp.block()
        attr = W["ea"].rearrange("n c -> (n c)")

        def groups(eng, body):
            steps(eng, GROUPS, ALONE, 2, body, 0)

        def landed(g, b):
            return 16 * (g // 2 + 1) if isinstance(g, int) else 8 * (g - b) + 16

        def adds(g, b):
            return 16 * GT * (g // 2 + 1) if isinstance(g, int) else 8 * GT * (g - b) + 16 * GT

        @block.sync
        def _(sp):
            def body(g, b):
                b %= 2
                wait(sp, eq_built, GT * (g - 1))
                if not isinstance(g, int) or g < GROUPS - 1:
                    sp.dma_start(krow[:, b], W["src"][bass.ds(g * GE, GE)].partition_broadcast(P)).then_inc(keys_in[b], 16)
                else:
                    wait(sp, padded, 2)
                    sp.dma_start(krow[:, b, 0:LASTE], W["src"][E - LASTE:E].partition_broadcast(P)).then_inc(keys_in[b], 16)
                wait(sp, part0_out, g - 1)
                wait(sp, rest1_out, g - 1)
                if not isinstance(g, int) or g < GROUPS - 1:
                    sp.dma_start(ea[:, b].rearrange("p i c -> p (i c)"),
                                 attr[bass.ds(g * GE * D, GE * D)].rearrange("(p f) -> p f", p=P)).then_inc(attr_in[b], 16)
                else:
                    sp.dma_start(ea[0:LASTE // GT, b].rearrange("p i c -> p (i c)"),
                                 attr[(E - LASTE) * D:E * D].rearrange("(p f) -> p f", f=GT * D)).then_inc(attr_in[b], 16)
            groups(sp, body)

        @block.vector
        def _(dve):
            nc.vector.memset(onec[:], 1.0).then_inc(ones_set, 1)

            def indices(g, b):
                dve.wait_ge(counted, g + 1)
                wait(dve, idx_out, g - 1)
                nc.vector.scalar_tensor_tensor(out=away[:, b], in0=ps_d[b][:, 0:GT], scalar=0.5,
                                               in1=con["dumdiff"][:, bass.ds(g * GT, GT)], op0=ALU.is_ge,
                                               op1=ALU.mult).then_inc(away_out, 1)
                dve.wait_ge(away_out, g + 1)
                wait(dve, added[b], adds(g, b) - 16 * GT)
                nc.vector.tensor_tensor(idx[:, b], away[:, b], con["srckey"][:, bass.ds(g * GT, GT)],
                                        ALU.add).then_inc(idx_out, 1)

            def body(g, b):
                b %= 2
                if isinstance(g, int) and g == GROUPS - 1:
                    dve.wait_ge(eq_built, GT * (g - 1))
                    dve.wait_ge(part0_out, g - 1)
                    dve.wait_ge(rest1_out, g - 1)
                    nc.vector.memset(krow[:, b], PADROW).then_inc(padded, 1)
                    nc.vector.memset(ea[:, b], 0.0).then_inc(padded, 1)
                if not isinstance(g, int) or g < GROUPS:
                    dve.wait_ge(keys_in[b], landed(g, b))
                    wait(dve, summed, g - 1)
                    for j in range(GT):
                        nc.vector.tensor_scalar(eq[:, b, j], krow[:, b].rearrange("p (m i) -> p i m", i=GT),
                                                con["srckey"][:, bass.ds(g * GT + j, 1)], None,
                                                ALU.is_equal).then_inc(eq_built, 1)
                        if j == 1:
                            dve.wait_ge(part0_out, g + 1)
                            dve.wait_ge(attr_in[b], landed(g, b))
                            wait(dve, rest2_out, g - 1)
                            nc.vector.tensor_tensor(rest[:, b, 0], ea[:, b], part[:, b, 0],
                                                    ALU.subtract).then_inc(rest1_out, 1)
                    dve.wait_ge(part1_out, g + 1)
                    dve.wait_ge(rest1_out, g + 1)
                    wait(dve, part2_out, g - 1)
                    nc.vector.tensor_tensor(rest[:, b, 1], rest[:, b, 0], part[:, b, 1],
                                            ALU.subtract).then_inc(rest2_out, 1)
                    dve.wait_ge(eq_built, GT * (g + 1))
                    nc.vector.tensor_tensor(diag[:, b], eq[:, b].rearrange("p j i m -> p (j i) m")[:, ::GT + 1, :],
                                            con["laterb"][:].unsqueeze(1).to_broadcast([P, GT, P]),
                                            ALU.mult).then_inc(diag_built, 1)
                    dve.wait_ge(hi_spread, g + 1)
                    nc.vector.tensor_scalar(con["onehot"][:, bass.ds(g * 4, 4), :], ps_h[b][:], con["pidx"][:, 0:1], None,
                                            ALU.is_equal).then_inc(onehot_made, 1)
                if not isinstance(g, int) or g >= 1:
                    indices(g - 1, 1 - b)
            steps(dve, GROUPS, ALONE, 2, body, 1)

        @block.tensor
        def _(pe):
            pe.wait_ge(ones_set, 1)

            def body(g, b):
                b %= 2
                wait(pe, onehot_made, g - 1)
                for k in range(4):
                    mm = nc.tensor.matmul(ps_h[b][:, k, :], con["high4"][:, k, bass.ds(g, 1)].to_broadcast([P, P]),
                                          con["identb"][:], start=True, stop=True)
                mm.then_inc(hi_spread, 1)
                pe.wait_ge(diag_built, g + 1)
                wait(pe, away_out, g - 1)
                for i in range(GT):
                    for j in range(i + 1):
                        mm = nc.tensor.matmul(ps_d[b][:, i:i + 1], diag[:, b, i] if j == i else eq[:, b, j, i], onec[:],
                                              start=(j == 0), stop=(j == i))
                mm.then_inc(counted, 1)
                pe.wait_ge(part2_out, g + 1)
                wait(pe, sums_out, g - 1)
                for i in range(GT):
                    for j in range(GT):
                        for v in range(3):
                            mm = nc.tensor.matmul(ps_t[b][:, i, 0:D], eq[:, b, j, i], part[:, b, v, j],
                                                  start=(j == 0 and v == 0), stop=(j == GT - 1 and v == 2))
                mm.then_inc(summed, 1)
            groups(pe, body)

        @block.scalar
        def _(act):
            def sums(g, b):
                act.wait_ge(summed, g + 1)
                wait(act, added[b], adds(g, b) - 16 * GT)
                nc.scalar.copy(tot[:, b], ps_t[b][:, :, 0:D]).then_inc(sums_out, 1)

            def body(g, b):
                b %= 2
                if not isinstance(g, int) or g < GROUPS:
                    act.wait_ge(attr_in[b], landed(g, b))
                    wait(act, summed, g - 1)
                    nc.scalar.copy(part[:, b, 0], ea[:, b]).then_inc(part0_out, 1)
                    if isinstance(g, int) and g < ALONE:
                        if g == 0:
                            act.wait_ge(attr_in[1], 16)
                        third = ZERO_DMAS // 3
                        for v in range(third + (ZERO_DMAS - third) * (g - 1) // (ALONE - 1) if g else 0,
                                       third + (ZERO_DMAS - third) * g // (ALONE - 1)):
                            act.dma_start(flat(W["agg"][1], v * P * ZERO_ROWS, ZERO_ROWS, D),
                                          con["zero"][:]).then_inc(con["agg_zeroed"][1], 16)
                    act.wait_ge(rest1_out, g + 1)
                    nc.scalar.copy(part[:, b, 1], rest[:, b, 0]).then_inc(part1_out, 1)
                    act.wait_ge(rest2_out, g + 1)
                    nc.scalar.copy(part[:, b, 2], rest[:, b, 1]).then_inc(part2_out, 1)
                if not isinstance(g, int) or g >= 1:
                    sums(g - 1, 1 - b)
            steps(act, GROUPS, ALONE, 2, body, 1)

        @block.gpsimd
        def _(pool):
            def body(g, b):
                b %= 2
                alone = isinstance(g, int) and g < ALONE
                if isinstance(g, int) and g == 0:
                    pool.wait_ge(con["agg_zeroed"][0], 16 * ZERO_DMAS)
                pool.wait_ge(sums_out, g + 1)
                pool.wait_ge(idx_out, g + 1)
                wait(pool, added[b], adds(g, b) - 16 * GT)
                if alone and g > 0:
                    pool.wait_ge(added[1 - b], adds(g - 1, 1 - b))
                pool.nop(nofuse=True)
                for i in range(GT):
                    nc.gpsimd.indirect_dma_start(
                        out=W["agg"][0 if alone else b], out_offset=bass.IndirectOffsetOnAxis(ap=idx[:, b, i:i + 1], axis=0),
                        in_=tot[:, b, i], in_offset=None, compute_op=ALU.add).then_inc(added[b], 16)
                if isinstance(g, int) and g == ALONE - 1:
                    pool.wait_ge(con["agg_zeroed"][1], 16 * ZERO_DMAS)
                    pool.wait_ge(added[b], adds(g, b))
            groups(pool, body)
            for b in range(2):
                pool.wait_ge(added[b], 16 * GT * ((GROUPS + 1 - b) // 2))


def mlp(nc, con, W):
    with ExitStack() as ctx:
        tmp = Mem(nc, ctx, "mlp")
        NX = 4
        xt = tmp.sb("xt", [P, NX, J, D])
        xb = tmp.sb("xb", [P, NX, J, D])
        xc = tmp.sb("xc", [P, 2, J, D])
        sq = tmp.sb("sq", [P, J, D])
        hx = tmp.sb("hx", [P, 2, J, 2 * D])
        agg1 = tmp.sb("agg1", [P, 2, J, D])
        hxT = tmp.sb("hxT", [P, 2, CH])
        hid = tmp.sb("hid", [P, 2, 2, CH])
        x1 = tmp.sb("x1", [P, 2, J, D])
        x1o = tmp.sb("x1o", [P, 2, J, D])
        yc = tmp.sb("yc", [P, 2, J, D])
        sqy = tmp.sb("sqy", [P, J, D])
        h1 = tmp.sb("h1", [P, 2, J, D])
        h1T = tmp.sb("h1T", [P, CH // 2])
        tt = tmp.sb("tt", [P, 2, J, ROW])
        st = tmp.sb("st", [P, 2, 5, J])
        eps = tmp.sb("eps", [P, 1])
        invd = tmp.sb("invd", [P, J])
        mlpT = tmp.sb("mlpT", [P, 4, P])
        ps_x = tmp.ps("ps_x", [P, 4, P])
        ps_h = [tmp.ps(f"ps_h{m}", [P, 512]) for m in range(2)]
        ps_y = tmp.ps("ps_y", [P, 512])
        ps_o = tmp.ps("ps_o", [P, 4, P])
        ps_n = tmp.ps("ps_n", [P, 4, P])
        ps_t = tmp.ps("ps_t", [P, 4, 256])
        sem = tmp.sem
        x_in = [sem(f"x_in{k}") for k in range(NX)]
        agg_in = [sem(f"agg_in{k}") for k in range(2)]
        agg1_in = [sem(f"agg1_in{k}") for k in range(2)]
        agg_ready = sem("agg_ready")
        x1_saved = [sem(f"x1_saved{k}") for k in range(2)]
        t_saved = [sem(f"t_saved{k}") for k in range(2)]
        invd_set = sem("invd_set")
        (eps_set, x_sum, x_mean, x_centred, x_square, x_var, x_dev, x_inv, h_ready, xb_ready,
         hx_turned, hxT_out, hid_done, hid_out, mlp_summed, mlp_copied, mlp_done, x1_ready, x1o_ready,
         y_sum, y_mean, y_centred, y_square, y_var, y_dev, y_inv, y_ready,
         y_turned, yT_out, t_done, t_out, ad_out) = (sem(n) for n in (
            "eps_set", "x_sum", "x_mean", "x_centred", "x_square", "x_var", "x_dev", "x_inv", "h_ready", "xb_ready",
            "hx_turned", "hxT_out", "hid_done", "hid_out", "mlp_summed", "mlp_copied", "mlp_done", "x1_ready", "x1o_ready",
            "y_sum", "y_mean", "y_centred", "y_square", "y_var", "y_dev", "y_inv", "y_ready",
            "y_turned", "yT_out", "t_done", "t_out", "ad_out"))
        block = tmp.block()

        def bc(v):
            return v.unsqueeze(2).to_broadcast([P, J, D])

        def halves(rows):
            return rows.rearrange("p (n a) c -> p n a c", n=2)

        def within(t):
            return not isinstance(t, int) or 0 <= t < CHUNKS

        def run(eng, body, ahead=0):
            steps(eng, CHUNKS, 8, 4, body, 3, ahead)

        def sems16(t, k, every):
            return 16 * (t // every + 1) if isinstance(t, int) else (16 // every) * (t - k % every) + 16

        @block.sync
        def _(sp):
            def load_x(s, k):
                wait(sp, xb_ready, s - 3)
                wait(sp, x_centred, s - 3)
                sp.dma_start(xt[:, k % 4].rearrange("p j c -> p (j c)"),
                             flat(W["x"], chunk_base(s), J, D)).then_inc(x_in[k % 4], 16)

            def body(s, k):
                if isinstance(s, int) and s == 0:
                    load_x(0, 0)
                if not isinstance(s, int) or s + 1 < CHUNKS:
                    load_x(s + 1, k + 1)
                if within(s):
                    wait(sp, hx_turned, 2 * (s - 1))
                    aggr = W["agg"][0].rearrange("n c -> (n c)")[bass.ds(chunk_base(s) * D, CH * D)]
                    sp.dma_start(hx[:, k % 2, :, D:2 * D],
                                 aggr.rearrange("(p j c) -> p j c", p=P, j=J)).then_inc(agg_in[k % 2], 16)
                    wait(sp, agg_ready, s - 1)
                    sp.dma_start(agg1[:, k % 2].rearrange("p j c -> p (j c)"),
                                 flat(W["agg"][1], chunk_base(s), J, D)).then_inc(agg1_in[k % 2], 16)
                t = s - 3
                if within(t - 1):
                    save_table(t - 1, k)
                if within(t):
                    tb = (k - 3) % 2
                    if isinstance(t, int) and t == CHUNKS - 1:
                        sp.wait_ge(x1_saved[1 - tb], 16 * (CHUNKS // 2))
                    sp.wait_ge(x1o_ready, t + 1)
                    sp.dma_start(flat(W["x1"], chunk_base(t), J, D),
                                 x1o[:, tb].rearrange("p j c -> p (j c)")).then_inc(x1_saved[tb], 16)

            def save_table(t, k):
                tb = k % 2
                if isinstance(t, int) and t == CHUNKS - 1:
                    sp.wait_ge(t_saved[1 - tb], 16 * (CHUNKS // 2))
                sp.wait_ge(t_out, t + 1)
                sp.dma_start(flat(W["tab"], chunk_base(t), J, ROW),
                             tt[:, tb].rearrange("p j c -> p (j c)")).then_inc(t_saved[tb], 16)
            run(sp, body, 1)
            save_table(CHUNKS - 1, CHUNKS - 1)
            for k in range(2):
                sp.wait_ge(x1_saved[k], 16 * ((CHUNKS + 1 - k) // 2))
                sp.wait_ge(t_saved[k], 16 * ((CHUNKS + 1 - k) // 2))

        @block.vector
        def _(dve):
            nc.vector.memset(eps[:], EPS).then_inc(eps_set, 1)

            def body(s, k):
                t = s - 3
                b, c = k % 2, (k - 3) % 2
                if within(t):
                    dve.wait_ge(mlp_done, t + 1)
                    dve.wait_ge(xb_ready, t + 1)
                    wait(dve, y_centred, t - 1)
                    wait(dve, x1o_ready, t - 1)
                    nc.vector.tensor_tensor(halves(x1[:, c]), ps_o[:].rearrange("p a (n c) -> p n a c", n=2),
                                            halves(xb[:, (k - 3) % 4]), ALU.add).then_inc(x1_ready, 1)
                    dve.wait_ge(x1_ready, t + 1)
                    wait(dve, y_mean, t)
                    nc.vector.tensor_reduce(st[:, 1, 0], x1[:, c], AX.X, ALU.add).then_inc(y_sum, 1)
                if within(s):
                    dve.wait_ge(x_in[k % 4], sems16(s, k, 4))
                    wait(dve, x_mean, s)
                    nc.vector.tensor_reduce(st[:, 0, 0], xt[:, k % 4], AX.X, ALU.add).then_inc(x_sum, 1)
                if within(t):
                    dve.wait_ge(y_square, t + 1)
                    wait(dve, y_dev, t)
                    nc.vector.tensor_reduce(st[:, 1, 2], sqy[:], AX.X, ALU.add).then_inc(y_var, 1)
                    dve.wait_ge(y_dev, t + 1)
                    wait(dve, y_ready, t)
                    nc.vector.reciprocal(st[:, 1, 4], st[:, 1, 3]).then_inc(y_inv, 1)
                    dve.wait_ge(y_inv, t + 1)
                    wait(dve, y_turned, t - 1)
                    nc.vector.scalar_tensor_tensor(out=h1[:, c], in0=yc[:, c], scalar=0.0, in1=bc(st[:, 1, 4]),
                                                   op0=ALU.max, op1=ALU.mult).then_inc(y_ready, 1)
                if within(s):
                    dve.wait_ge(x_square, s + 1)
                    wait(dve, x_dev, s)
                    nc.vector.tensor_reduce(st[:, 0, 2], sq[:], AX.X, ALU.add).then_inc(x_var, 1)
                    dve.wait_ge(x_dev, s + 1)
                    wait(dve, h_ready, s)
                    nc.vector.reciprocal(st[:, 0, 4], st[:, 0, 3]).then_inc(x_inv, 1)
                    dve.wait_ge(x_inv, s + 1)
                    wait(dve, hx_turned, 2 * (s - 1))
                    nc.vector.scalar_tensor_tensor(out=hx[:, b, :, 0:D], in0=xc[:, b], scalar=0.0, in1=bc(st[:, 0, 4]),
                                                   op0=ALU.max, op1=ALU.mult).then_inc(h_ready, 1)
            run(dve, body)

        @block.gpsimd
        def _(pool):
            nc.gpsimd.memset(invd[:], 1.0 / D).then_inc(invd_set, 1)
            pool.wait_ge(invd_set, 1)

            def body(s, k):
                t = s - 3
                b, c = k % 2, (k - 3) % 2
                if within(t):
                    pool.wait_ge(y_sum, t + 1)
                    wait(pool, y_centred, t)
                    nc.gpsimd.tensor_tensor(st[:, 1, 1], st[:, 1, 0], invd[:], ALU.mult).then_inc(y_mean, 1)
                    pool.wait_ge(y_mean, t + 1)
                    wait(pool, y_ready, t - 1)
                    nc.gpsimd.tensor_tensor(yc[:, c], x1[:, c], bc(st[:, 1, 1]), ALU.subtract).then_inc(y_centred, 1)
                if within(s):
                    pool.wait_ge(x_sum, s + 1)
                    wait(pool, x_centred, s)
                    nc.gpsimd.tensor_tensor(st[:, 0, 1], st[:, 0, 0], invd[:], ALU.mult).then_inc(x_mean, 1)
                    pool.wait_ge(x_mean, s + 1)
                    wait(pool, h_ready, s - 1)
                    nc.gpsimd.tensor_tensor(xc[:, b], xt[:, k % 4], bc(st[:, 0, 1]), ALU.subtract).then_inc(x_centred, 1)
                if within(t):
                    wait(pool, x1_saved[c], 16 * (t // 2) if isinstance(t, int) else 8 * (t - c))
                    nc.gpsimd.tensor_tensor(x1o[:, c], x1[:, c], con["gb2row"][:].unsqueeze(1).to_broadcast([P, J, D]),
                                            ALU.add).then_inc(x1o_ready, 1)
                if within(s):
                    wait(pool, x1_ready, s - 3)
                    nc.gpsimd.tensor_tensor(xb[:, k % 4], xt[:, k % 4], con["b2row"][:].unsqueeze(1).to_broadcast([P, J, D]),
                                            ALU.add).then_inc(xb_ready, 1)
                    pool.wait_ge(agg_in[b], sems16(s, k, 2))
                    pool.wait_ge(agg1_in[b], sems16(s, k, 2))
                    nc.gpsimd.tensor_tensor(hx[:, b, :, D:2 * D], hx[:, b, :, D:2 * D], agg1[:, b],
                                            ALU.add).then_inc(agg_ready, 1)
            run(pool, body)

        @block.scalar
        def _(act):
            act.wait_ge(eps_set, 1)

            def body(s, k):
                q, r, t = s - 1, s - 2, s - 3
                b, c = k % 2, (k - 3) % 2

                def relu(n, m):
                    act.wait_ge(hid_done, 4 * r + 2 * n + m + 1)
                    if (n, m) == (0, 0):
                        wait(act, mlp_summed, r - 1)
                    nc.scalar.activation(hid[:, b, m, n * 512:n * 512 + 512], ps_h[m][:], ACT.Relu,
                                         bias=con["hbias"][:, m:m + 1]).then_inc(hid_out, 1)

                def copy_turned(h):
                    act.wait_ge(hx_turned, 2 * q + h + 1)
                    wait(act, hid_done, 4 * (q - 1))
                    nc.scalar.copy(hxT[:, 1 - b, h * 512:h * 512 + 512], ps_x[:]).then_inc(hxT_out, 1)

                if within(r):
                    relu(0, 0)
                    relu(0, 1)
                if within(q):
                    copy_turned(0)
                if within(t):
                    act.wait_ge(y_centred, t + 1)
                    wait(act, y_var, t)
                    nc.scalar.activation(sqy[:], yc[:, c], ACT.Square).then_inc(y_square, 1)
                if within(r):
                    relu(1, 0)
                    relu(1, 1)
                if within(t):
                    act.wait_ge(y_var, t + 1)
                    wait(act, y_inv, t)
                    nc.scalar.activation(st[:, 1, 3], st[:, 1, 2], ACT.Sqrt, scale=1.0 / D, bias=eps[:, 0:1]).then_inc(y_dev, 1)
                if within(s):
                    act.wait_ge(x_centred, s + 1)
                    wait(act, x_var, s)
                    nc.scalar.activation(sq[:], xc[:, b], ACT.Square).then_inc(x_square, 1)
                if within(q):
                    copy_turned(1)
                if within(r):
                    act.wait_ge(mlp_summed, r + 1)
                    wait(act, mlp_done, r)
                    nc.scalar.copy(mlpT[:], ps_y[:]).then_inc(mlp_copied, 1)
                if within(s):
                    act.wait_ge(x_var, s + 1)
                    wait(act, x_inv, s)
                    nc.scalar.activation(st[:, 0, 3], st[:, 0, 2], ACT.Sqrt, scale=1.0 / D, bias=eps[:, 0:1]).then_inc(x_dev, 1)
                if within(t):
                    act.wait_ge(y_turned, t + 1)
                    wait(act, t_done, t)
                    nc.scalar.copy(h1T[:], ps_n[:]).then_inc(yT_out, 1)
                    act.wait_ge(t_done, t + 1)
                    wait(act, t_saved[c], 16 * (t // 2) if isinstance(t, int) else 8 * (t - c))
                    nc.scalar.copy(tt[:, c].rearrange("p (a v) c -> p a (v c)", v=2),
                                   ps_t[:, :, 0:2 * ROW]).then_inc(t_out, 1)
                    nc.scalar.copy(con["ad"][:, bass.ds(t * J, J)].rearrange("p (a v) -> p a v", v=2),
                                   ps_t[:, :, D + 1:2 * ROW:ROW]).then_inc(ad_out, 1)
            run(act, body)

        @block.tensor
        def _(pe):
            def turn_y(t, c):
                if within(t):
                    pe.wait_ge(y_ready, t + 1)
                    wait(pe, yT_out, t)
                    for a in range(4):
                        mm = nc.tensor.transpose(ps_n[:, a, :], h1[:, c, 2 * a:2 * a + 2].rearrange("p j c -> p (j c)"),
                                                 con["ident"][:])
                    mm.then_inc(y_turned, 1)

            def body(s, k):
                q, r, t = s - 1, s - 2, s - 3
                b, c = k % 2, (k - 3) % 2
                def hidden(n):
                    if within(r):
                        pe.wait_ge(hxT_out, 2 * r + n + 1)
                        for m in range(2):
                            wait(pe, hid_out, 4 * r + 2 * n + m - 1)
                            nc.tensor.matmul(ps_h[m][:], con["w1"][:, m * P:m * P + P],
                                             hxT[:, b, n * 512:n * 512 + 512], start=True, stop=True).then_inc(hid_done, 1)

                def turn_x(h):
                    if within(q):
                        if h == 0:
                            pe.wait_ge(h_ready, q + 1)
                            pe.wait_ge(agg_ready, q + 1)
                        wait(pe, hxT_out, 2 * q + h)
                        for a in range(4):
                            mm = nc.tensor.transpose(ps_x[:, a, :], hx[:, 1 - b, 4 * h + a, :], con["ident"][:])
                        mm.then_inc(hx_turned, 1)

                hidden(0)
                turn_x(0)
                hidden(1)
                turn_x(1)
                if within(r):
                    wait(pe, mlp_copied, r)
                    for m in range(2):
                        pe.wait_ge(hid_out, 4 * r + 3 + m)
                        for n in range(2):
                            mm = nc.tensor.matmul(ps_y[D * n:D * n + D, :], con["w2"][:, m, :],
                                                  hid[:, b, m, n * 512:n * 512 + 512], start=(m == 0), stop=(m == 1))
                    mm.then_inc(mlp_summed, 1)
                turn_y(t, c)
                if within(r):
                    pe.wait_ge(mlp_copied, r + 1)
                    wait(pe, x1_ready, r)
                    for a in range(4):
                        mm = nc.tensor.transpose(ps_o[:, a, :], mlpT[:, a, :], con["ident"][:])
                    mm.then_inc(mlp_done, 1)
                if within(t):
                    pe.wait_ge(yT_out, t + 1)
                    wait(pe, ad_out, t)
                    for a in range(4):
                        mm = nc.tensor.matmul(ps_t[:, a, 0:2 * ROW], h1T[:, a * P:a * P + P], con["bd1"][:],
                                              start=True, stop=True)
                    mm.then_inc(t_done, 1)
            run(pe, body)


def edge_attention(nc, con, W, tag, first):
    with ExitStack() as ctx:
        tmp = Mem(nc, ctx, tag)
        F = tmp.sb("F", [P, EC, ROW])
        parts = tmp.sb("parts", [P, 3, J * CHUNKS], BF16)
        rest = tmp.sb("rest", [P, 2, J * CHUNKS])
        pick = tmp.sb("pick", [P, J * CHUNKS])
        ade = tmp.sb("ade", [P, EC])
        sc = tmp.sb("sc", [P, 6, EW])
        m = tmp.sb("m", [P, EC + 1])
        prod = tmp.sb("prod", [P, EW, ROW])
        selp = tmp.sb("selp", [P, EPARTS, ROW])
        sel = tmp.sb("sel", [P, ROW])
        val = tmp.sb("val", [P, 2, P])
        wT = tmp.sb("wT", [P, P])
        sm = tmp.sb("sm", [P, 8])
        car = tmp.sb("car", [P, ROW])
        orow = tmp.sb("orow", [P, ROW])
        NB = 4
        ps_g = [tmp.ps(f"ps_g{k}", [P, 512]) for k in range(NB)]
        ps_m, ps_w, ps_c = (tmp.ps(n, [P, 512]) for n in ("ps_m", "ps_w", "ps_c"))
        sem = tmp.sem
        split, fetched, picked = sem("split"), sem("fetched"), sem("picked")
        gathered, scattered, lead_saved = con["gathered"], con["scattered"], con["lead_saved"]
        nz_set, maxed, differ, powers, rows_done = (sem(n) for n in (
            "nz_set", "maxed", "differ", "powers", "rows_done"))
        dve_step, joined = sem("dve_step"), sem("joined")
        join_pe, join_act, lead_ready = sem("join_pe"), sem("join_act"), sem("lead_ready")
        block = tmp.block()
        NZ_DMAS = 14
        nz_rows = CHUNKS * J // NZ_DMAS

        @block.sync
        def _(sp):
            if first:
                for k in range(NZ_DMAS):
                    sp.dma_start(flat(W["nz"], k * P * nz_rows, nz_rows, ROW),
                                 con["nzrows"][:].rearrange("p r c -> p (r c)")).then_inc(nz_set, 16)

        @block.gpsimd
        def _(pool):
            for c in range(EC):
                nc.gpsimd.indirect_dma_start(
                    out=F[:, c, :], out_offset=None, in_=W["tab"],
                    in_offset=bass.IndirectOffsetOnAxis(ap=con["srcg"][:, c:c + 1], axis=0)).then_inc(gathered[c // EW], 16)
            if first:
                pool.wait_ge(nz_set, 16 * NZ_DMAS)
            for c in range(EC):
                if c % EW == 0:
                    pool.wait_ge(rows_done, c // EW + 1)
                nc.gpsimd.indirect_dma_start(
                    out=W["nz"], out_offset=bass.IndirectOffsetOnAxis(ap=con["rowidx"][:, c:c + 1], axis=0),
                    in_=F[:, c, :], in_offset=None, bounds_check=N - 1, oob_is_err=False).then_inc(scattered, 16)
            pool.wait_ge(lead_ready, 2)
            nc.gpsimd.indirect_dma_start(
                out=W["nz"], out_offset=bass.IndirectOffsetOnAxis(ap=con["leadidx"][:, 0:1], axis=0),
                in_=orow[:], in_offset=None, bounds_check=N - 1, oob_is_err=False).then_inc(lead_saved, 16)
            pool.wait_ge(scattered, 16 * EC)
            pool.wait_ge(lead_saved, 16)

        @block.tensor
        def _(pe):
            pe.wait_ge(split, 5)

            def body(i, k):
                for v in range(NB):
                    wait(pe, picked, NB * (i - 1) + v + 1)
                    for part in range(3):
                        mm = nc.tensor.matmul(ps_g[v][:, 0:J * CHUNKS],
                                              con["onehot"][:, bass.ds(i * NB + v, 1), :].rearrange("p a m -> p (a m)"),
                                              parts[:, part, :], start=(part == 0), stop=(part == 2))
                    mm.then_inc(fetched, 1)
            body(0, 0)
            with pe.Fori(1, EC // NB) as i:
                body(i, 0)
            pe.wait_ge(maxed, EPARTS)
            nc.tensor.matmul(ps_m[:, 0:P], m[:, EC:EC + 1].to_broadcast([P, P]), con["ident"][:],
                             start=True, stop=True).then_inc(join_pe, 1)
            pe.wait_ge(joined, 3)
            nc.tensor.transpose(ps_w[:, 0:P], val[:, 1, :], con["ident"][:]).then_inc(join_pe, 1)
            pe.wait_ge(join_act, 2)
            pe.wait_ge(rows_done, EPARTS)
            nc.tensor.matmul(ps_c[:, 0:ROW - 1], wT[:], F[:, EC - 1, 0:ROW - 1], start=True, stop=True).then_inc(join_pe, 1)

        @block.vector
        def _(dve):
            ad = con["ad"]
            nc.vector.tensor_copy(parts[:, 0, :], ad[:]).then_inc(split, 1)
            dve.wait_ge(split, 1)
            nc.vector.tensor_tensor(rest[:, 0], ad[:], parts[:, 0, :], ALU.subtract).then_inc(split, 1)
            dve.wait_ge(split, 2)
            nc.vector.tensor_copy(parts[:, 1, :], rest[:, 0]).then_inc(split, 1)
            dve.wait_ge(split, 3)
            nc.vector.tensor_tensor(rest[:, 1], rest[:, 0], parts[:, 1, :], ALU.subtract).then_inc(split, 1)
            dve.wait_ge(split, 4)
            nc.vector.tensor_copy(parts[:, 2, :], rest[:, 1]).then_inc(split, 1)

            def body(i):
                for v in range(NB):
                    dve.wait_ge(fetched, NB * i + v + 1)
                    wait(dve, picked, NB * i + v)
                    nc.vector.scalar_tensor_tensor(out=pick[:], in0=con["iota"][:],
                                                   scalar=con["lo"][:, bass.ds(i * NB + v, 1)],
                                                   in1=ps_g[v][:, 0:J * CHUNKS], op0=ALU.is_equal, op1=ALU.mult,
                                                   accum_out=ade[:, bass.ds(i * NB + v, 1)]).then_inc(picked, 1)
            body(0)
            with dve.Fori(1, EC // NB) as i:
                body(i)
            count = [0]

            def link(ins, wait_for_it=True):
                count[0] += 1
                ins.then_inc(dve_step, 1)
                if wait_for_it:
                    dve.wait_ge(dve_step, count[0])

            dve.wait_ge(picked, EC)
            link(nc.vector.memset(m[:, 0:1], -BIG))
            for k in range(EPARTS):
                cols = slice(k * EW, k * EW + EW)
                mk, mprev = m[:, k * EW + 1:k * EW + EW + 1], m[:, k * EW:k * EW + EW]
                dve.wait_ge(gathered[k], 16 * EW)
                link(nc.vector.tensor_tensor(sc[:, 0], F[:, cols, D], ade[:, cols], ALU.add))
                link(nc.vector.scalar_tensor_tensor(out=sc[:, 1], in0=sc[:, 0], scalar=SLOPE, in1=sc[:, 0],
                                                    op0=ALU.mult, op1=ALU.max))
                link(nc.vector.tensor_copy(sm[:, 7:8], m[:, k * EW:k * EW + 1]))
                nc.vector.tensor_tensor_scan(mk, con["cut"][:, cols], sc[:, 1], sm[:, 7:8], ALU.add,
                                             ALU.max).then_inc(maxed, 1)
                dve.wait_ge(maxed, k + 1)
                link(nc.vector.tensor_tensor(sc[:, 2], sc[:, 1], mk, ALU.subtract))
                link(nc.vector.tensor_tensor(sc[:, 3], mprev, mk, ALU.subtract))
                nc.vector.tensor_scalar(sc[:, 3], sc[:, 3], 0.0, None, ALU.min).then_inc(differ, 1)
                dve.wait_ge(powers, k + 1)
                link(nc.vector.tensor_tensor(sc[:, 5], sc[:, 5], con["same"][:, cols], ALU.mult))
                link(nc.vector.tensor_tensor(F[:, cols, 0:D], F[:, cols, 0:D],
                                             sc[:, 4].unsqueeze(2).to_broadcast([P, EW, D]), ALU.mult))
                link(nc.vector.tensor_copy(F[:, cols, D], sc[:, 4]))
                link(nc.vector.tensor_copy(F[:, cols, D + 1], mk))
                for f in range(D + 1):
                    ins = nc.vector.tensor_tensor_scan(
                        F[:, cols, f], sc[:, 5], F[:, cols, f],
                        F[:, k * EW - 1, f:f + 1] if k else 0.0, ALU.mult, ALU.add)
                ins.then_inc(rows_done, 1)
                dve.wait_ge(rows_done, k + 1)
                if k:
                    dve.wait_ge(dve_step, count[0])
                link(nc.vector.tensor_tensor(prod[:], F[:, cols, :],
                                             con["leadend"][:, cols].unsqueeze(2).to_broadcast([P, EW, ROW]), ALU.mult))
                link(nc.vector.tensor_reduce(selp[:, k], prod[:].rearrange("p c f -> p f c"), AX.X, ALU.add))
            link(nc.vector.tensor_reduce(sel[:], selp[:].rearrange("p k f -> p f k"), AX.X, ALU.add))
            dve.wait_ge(join_pe, 1)
            link(nc.vector.tensor_tensor(val[:, 0], ps_m[:, 0:P], con["joins"][:], ALU.mult))
            link(nc.vector.tensor_tensor(val[:, 0], val[:, 0], con["nojoin"][:], ALU.add))
            link(nc.vector.tensor_reduce(sm[:, 0:1], val[:, 0], AX.X, ALU.max))
            nc.vector.tensor_scalar(val[:, 0], val[:, 0], sm[:, 0:1], None, ALU.subtract).then_inc(joined, 1)
            nc.vector.tensor_tensor(sm[:, 1:2], sm[:, 0:1], sel[:, ROW - 1:ROW], ALU.max).then_inc(joined, 1)
            dve.wait_ge(join_act, 1)
            nc.vector.tensor_tensor(val[:, 1], val[:, 1], con["joins"][:], ALU.mult).then_inc(joined, 1)
            dve.wait_ge(joined, 3)
            link(nc.vector.tensor_tensor(sm[:, 2:3], sel[:, ROW - 1:ROW], sm[:, 1:2], ALU.subtract))
            nc.vector.tensor_tensor(sm[:, 3:4], sm[:, 0:1], sm[:, 1:2], ALU.subtract).then_inc(joined, 1)
            dve.wait_ge(join_act, 3)
            dve.wait_ge(join_pe, 3)
            link(nc.vector.tensor_scalar(car[:, 0:ROW - 1], ps_c[:, 0:ROW - 1], sm[:, 5:6], None, ALU.mult))
            nc.vector.tensor_copy(orow[:, ROW - 1:ROW], sm[:, 1:2]).then_inc(lead_ready, 1)
            nc.vector.scalar_tensor_tensor(out=orow[:, 0:ROW - 1], in0=sel[:, 0:ROW - 1], scalar=sm[:, 4:5],
                                           in1=car[:, 0:ROW - 1], op0=ALU.mult, op1=ALU.add).then_inc(lead_ready, 1)

        @block.scalar
        def _(act):
            for k in range(EPARTS):
                act.wait_ge(differ, k + 1)
                nc.scalar.activation(sc[:, 4:6], sc[:, 2:4], ACT.Exp).then_inc(powers, 1)
            act.wait_ge(joined, 1)
            nc.scalar.activation(val[:, 1], val[:, 0], ACT.Exp).then_inc(join_act, 1)
            act.wait_ge(join_pe, 2)
            nc.scalar.copy(wT[:], ps_w[:, 0:P]).then_inc(join_act, 1)
            act.wait_ge(joined, 4)
            nc.scalar.activation(sm[:, 4:6], sm[:, 2:4], ACT.Exp).then_inc(join_act, 1)


def merge(nc, con, W, tag, last):
    with ExitStack() as ctx:
        tmp = Mem(nc, ctx, tag)
        NB = 3
        UC = 4
        UNITS = (CHUNKS - 1) // UC + 1
        assert (CHUNKS - 1) % UC == 0
        tr = tmp.sb("tr", [P, NB, UC * J, ROW])
        nz = tmp.sb("nz", [P, NB, UC * J, ROW])
        g = tmp.sb("g", [P, NB, UC * J, D])
        sc = tmp.sb("sc", [P, NB, 12, UC * J])
        if last:
            xr = tmp.sb("xr", [P, NB, UC * J, D])
        else:
            gT = tmp.sb("gT", [P, 2, CH // 2])
            out = tmp.sb("out", [P, NB, UC * J, ROW])
            ps_n = [tmp.ps(f"ps_n{k}", [P, 4, P]) for k in range(2)]
            ps_t = [tmp.ps(f"ps_t{k}", [P, 4, 256]) for k in range(2)]
        sem = tmp.sem
        tab_in, nz_in, x_in, saved = ([sem(f"{n}{k}") for k in range(NB)] for n in ("tab_in", "nz_in", "x_in", "saved"))
        (self_sum, self_score, top, edge_off, self_off, powers, edge_z, den, inv, edge_w, self_w, edge_part, self_part, x_part,
         merged, turned, gT_out, t_done, t_out, ad_out) = (sem(n) for n in (
            "self_sum", "self_score", "top", "edge_off", "self_off", "powers", "edge_z", "den", "inv", "edge_w", "self_w",
            "edge_part", "self_part", "x_part", "merged", "turned", "gT_out", "t_done", "t_out", "ad_out"))
        block = tmp.block()

        def within(t):
            return not isinstance(t, int) or 0 <= t < UNITS

        def chunks_of(t):
            return 1 if isinstance(t, int) and t == UNITS - 1 else UC

        def unit_dram(dram, t, width):
            n = chunks_of(t)
            start = LAST if isinstance(t, int) and t == UNITS - 1 else t * (UC * CH)
            f = dram.rearrange("n c -> (n c)")
            return f[bass.ds(start * width, n * CH * width)].rearrange("(c p f) -> p c f", c=n, p=P)

        def unit_tile(tile, t, k):
            n = chunks_of(t)
            return tile[:, k % NB, 0:n * J].rearrange("p (c j) f -> p c (j f)", c=n)

        def run(eng, body):
            trips = (UNITS - 1) // NB
            for t in range(2 * NB):
                body(t, t, t // NB)
            with eng.Fori(2, trips) as r:
                for b in range(NB):
                    body(r * NB + b, b, r)
            for t in range(trips * NB, UNITS + 1):
                body(t, t, t // NB)

        def before(r, k):
            return r - 1 if k % NB == 0 else r

        @block.sync
        def _(sp):
            def body(s, k, r):
                if within(s):
                    wait(sp, merged, s - NB + 1)
                    sp.dma_start(unit_tile(tr, s, k), unit_dram(W["tab"], s, ROW)).then_inc(tab_in[k % NB], 16)
                    sp.dma_start(unit_tile(nz, s, k), unit_dram(W["nz"], s, ROW)).then_inc(nz_in[k % NB], 16)
                    if last:
                        sp.dma_start(unit_tile(xr, s, k), unit_dram(W["x1"], s, D)).then_inc(x_in[k % NB], 16)
            run(sp, body)

        def save(act, t, c, dram, tile, width):
            if isinstance(t, int) and t == UNITS - 1:
                act.wait_ge(saved[(t - 1) % NB], 16 * ((t - 1) // NB + 1))
            act.dma_start(unit_dram(dram, t, width), unit_tile(tile, t, c)).then_inc(saved[c], 16)

        @block.vector
        def _(dve):
            def scores(s, k, r):
                if within(s):
                    b = k % NB
                    n = chunks_of(s) * J
                    v = [sc[:, b, i, 0:n] for i in range(12)]
                    dve.wait_ge(tab_in[b], 16 * r + 16)
                    dve.wait_ge(nz_in[b], 16 * r + 16)
                    wait(dve, merged, s - NB + 1)
                    nc.vector.tensor_tensor(v[0], tr[:, b, 0:n, D], tr[:, b, 0:n, D + 1], ALU.add).then_inc(self_sum, 1)
                    dve.wait_ge(self_sum, s + 1)
                    nc.vector.scalar_tensor_tensor(out=v[1], in0=v[0], scalar=SLOPE, in1=v[0], op0=ALU.mult,
                                                   op1=ALU.max).then_inc(self_score, 1)
                    dve.wait_ge(self_score, s + 1)
                    nc.vector.tensor_tensor(v[2], v[1], nz[:, b, 0:n, D + 1], ALU.max).then_inc(top, 1)
                    dve.wait_ge(top, s + 1)
                    nc.vector.tensor_tensor(v[4], nz[:, b, 0:n, D + 1], v[2], ALU.subtract).then_inc(edge_off, 1)
                    nc.vector.tensor_tensor(v[5], v[1], v[2], ALU.subtract).then_inc(self_off, 1)

            def body(s, k, r):
                t = s - 1
                if within(t):
                    c = (k - 1) % NB
                    n = chunks_of(t) * J
                    w = [sc[:, c, i, 0:n] for i in range(12)]
                    dve.wait_ge(powers, t + 1)
                    nc.vector.tensor_tensor(w[8], w[6], nz[:, c, 0:n, D], ALU.mult).then_inc(edge_z, 1)
                    dve.wait_ge(edge_z, t + 1)
                    nc.vector.scalar_tensor_tensor(out=w[9], in0=w[7], scalar=1e-16, in1=w[8], op0=ALU.add,
                                                   op1=ALU.add).then_inc(den, 1)
                    dve.wait_ge(den, t + 1)
                    nc.vector.reciprocal(w[10], w[9]).then_inc(inv, 1)
                    dve.wait_ge(inv, t + 1)
                    nc.vector.tensor_tensor(w[3], w[7], w[10], ALU.mult).then_inc(self_w, 1)
                    nc.vector.tensor_tensor(w[11], w[6], w[10], ALU.mult).then_inc(edge_w, 1)
                    dve.wait_ge(edge_w, t + 1)
                    rows = nz[:, c, 0:n, 0:D]
                    nc.vector.tensor_tensor(rows, rows, w[11].unsqueeze(2).to_broadcast([P, n, D]),
                                            ALU.mult).then_inc(edge_part, 1)
                    dve.wait_ge(edge_part, t + 1)
                    if last:
                        dve.wait_ge(x_in[c], 16 * before(r, k) + 16)
                        nc.vector.tensor_tensor(rows, rows, xr[:, c, 0:n], ALU.add).then_inc(x_part, 1)
                        dve.wait_ge(x_part, t + 1)
                        wait(dve, saved[c], 16 * before(r, k))
                    else:
                        wait(dve, turned, UC * (t - NB + 1))
                scores(s, k, r)
                if within(t):
                    dve.wait_ge(self_part, t + 1)
                    nc.vector.tensor_tensor(g[:, c, 0:n], rows, tr[:, c, 0:n, 0:D], ALU.add).then_inc(merged, 1)
            run(dve, body)

        @block.gpsimd
        def _(pool):
            def body(s, k, r):
                t = s - 1
                if within(t):
                    c = (k - 1) % NB
                    n = chunks_of(t) * J
                    pool.wait_ge(self_w, t + 1)
                    pool.wait_ge(tab_in[c], 16 * before(r, k) + 16)
                    rows = tr[:, c, 0:n, 0:D]
                    nc.gpsimd.tensor_tensor(rows, rows, sc[:, c, 3, 0:n].unsqueeze(2).to_broadcast([P, n, D]),
                                            ALU.mult).then_inc(self_part, 1)
            run(pool, body)

        @block.scalar
        def _(act):
            def relu(t, i):
                act.wait_ge(turned, UC * t + i + 1)
                wait(act, t_done, UC * t + i - 1)
                nc.scalar.activation(gT[:, i % 2], ps_n[i % 2][:], ACT.Relu, bias=con["gb1col"][:, 0:1]).then_inc(gT_out, 1)

            def body(s, k, r):
                if within(s):
                    b = k % NB
                    n = chunks_of(s) * J
                    act.wait_ge(edge_off, s + 1)
                    act.wait_ge(self_off, s + 1)
                    wait(act, edge_w, s - NB + 1)
                    nc.scalar.activation(sc[:, b, 6:8, 0:n], sc[:, b, 4:6, 0:n], ACT.Exp).then_inc(powers, 1)
                t = s - 1
                if within(t) and not last:
                    c = (k - 1) % NB
                    relu(t, 0)
                    for i in range(chunks_of(t)):
                        m = UC * t + i
                        if i + 1 < chunks_of(t):
                            relu(t, i + 1)
                        act.wait_ge(t_done, m + 1)
                        if i == 0:
                            wait(act, saved[c], 16 * before(r, k))
                        nc.scalar.copy(out[:, c, i * J:i * J + J].rearrange("p (a v) c -> p a (v c)", v=2),
                                       ps_t[i % 2][:, :, 0:2 * ROW]).then_inc(t_out, 1)
                        nc.scalar.copy(con["ad"][:, bass.ds(m * J, J)].rearrange("p (a v) -> p a v", v=2),
                                       ps_t[i % 2][:, :, D + 1:2 * ROW:ROW]).then_inc(ad_out, 1)
                    act.wait_ge(t_out, UC * t + chunks_of(t))
                    save(act, t, c, W["tab2"], out, ROW)
                if within(t) and last:
                    act.wait_ge(merged, t + 1)
                    save(act, t, (k - 1) % NB, W["out"], g, D)
            run(act, body)
            for k in range(NB):
                act.wait_ge(saved[k], 16 * ((UNITS + NB - 1 - k) // NB))

        if not last:
            @block.tensor
            def _(pe):
                def turn(t, k, i):
                    c = (k - 1) % NB
                    m = UC * t + i
                    if i == 0:
                        pe.wait_ge(merged, t + 1)
                    wait(pe, gT_out, m - 1)
                    for a in range(4):
                        mm = nc.tensor.transpose(ps_n[i % 2][:, a, :],
                                                 g[:, c, i * J + 2 * a:i * J + 2 * a + 2].rearrange("p j c -> p (j c)"),
                                                 con["ident"][:])
                    mm.then_inc(turned, 1)

                def body(s, k, r):
                    t = s - 1
                    if within(t):
                        n = chunks_of(t)
                        turn(t, k, 0)
                        for i in range(n):
                            m = UC * t + i
                            if i + 1 < n:
                                turn(t, k, i + 1)
                            pe.wait_ge(gT_out, m + 1)
                            wait(pe, ad_out, m - 1)
                            for a in range(4):
                                mm = nc.tensor.matmul(ps_t[i % 2][:, a, 0:2 * ROW], gT[:, i % 2, a * P:a * P + P],
                                                      con["bd2"][:], start=True, stop=True)
                            mm.then_inc(t_done, 1)
                run(pe, body)


def graph_kernel(nc, W):
    with ExitStack() as ctx:
        mem = Mem(nc, ctx, "all")
        shapes = dict(zero=[P, AGG_ROWS // P // ZERO_DMAS * D], ident=[P, P], later=[P, P], earlier=[P, P],
                      iota=[P, J * CHUNKS], dummy=[P, GROUPS * GT], pidx=[P, 1], nzrows=[P, CHUNKS * J // 14, ROW],
                      bd1=[P, 2 * ROW], bd2=[P, 2 * ROW], w1=[P, HID], w2=[P, 2, D], hbias=[P, 2], b2row=[P, D],
                      gb2row=[P, D], gb1col=[P, 1], same=[P, EC], cut=[P, EC], leadend=[P, EC],
                      lo=[P, EC], joins=[P, P], nojoin=[P, P], srckey=[P, GROUPS * GT], dumdiff=[P, GROUPS * GT],
                      ad=[P, J * CHUNKS])
        con = {n: mem.sb(n, s) for n, s in shapes.items()}
        con.update(onehot=mem.sb("onehot", [P, EC, P], BF16), identb=mem.sb("identb", [P, P], BF16),
                   high4=mem.sb("high4", [P, 4, EC // 4], BF16), laterb=mem.sb("laterb", [P, P], BF16), srcg=mem.sb("srcg", [P, EC], I32),
                   rowidx=mem.sb("rowidx", [P, EC], I32), leadidx=mem.sb("leadidx", [P, 1], I32),
                   agg_zeroed=[mem.sem(f"agg_zeroed{k}") for k in range(2)])
        con["reordered"] = mem.sem("reordered")
        con["added"] = [mem.sem(f"added{k}") for k in range(2)]
        swdge = [dict(gathered=[mem.sem(f"gathered{l}_{k}") for k in range(EPARTS)], scattered=mem.sem(f"scattered{l}"),
                      lead_saved=mem.sem(f"lead_saved{l}")) for l in range(2)]
        W["agg"] = [nc.dram_tensor(f"agg_table{k}", (AGG_ROWS, D), F32).ap() for k in range(2)]
        for name in ("src", "dst"):
            W[f"{name}_ordered"] = nc.dram_tensor(f"{name}_ordered", (E,), I32).ap()
        W["x1"] = nc.dram_tensor("x1_table", (N, D), F32).ap()
        W["tab"] = nc.dram_tensor("att_table1", (N, ROW), F32).ap()
        W["nz"] = nc.dram_tensor("nz_table", (CHUNKS * CH, ROW), F32).ap()
        tab2 = nc.dram_tensor("att_table2", (N, ROW), F32).ap()
        W["tab2"] = tab2
        order_edges(nc, con, W)
        setup(nc, mem, con, W)
        sum_edges(nc, con, W)
        mlp(nc, con, W)
        edge_attention(nc, con | swdge[0], W, "att1", True)
        merge(nc, con, W, "merge1", False)
        W["tab"] = tab2
        edge_attention(nc, con | swdge[1], W, "att2", False)
        merge(nc, con, W, "merge2", True)


_INS = {'x': 'x', 'src': 'src', 'dst': 'dst', 'edge_attr_64': 'ea', 'L0_gnn_u': 'u', 'L0_gnn_W1': 'W1', 'L0_gnn_b1': 'b1',
        'L0_gnn_W2': 'W2', 'L0_gnn_b2': 'b2', 'L1_gnn_W1': 'gW1', 'L1_gnn_a_src1': 'as1', 'L1_gnn_a_dst1': 'ad1',
        'L1_gnn_b1': 'gb1', 'L1_gnn_W2': 'gW2', 'L1_gnn_a_src2': 'as2', 'L1_gnn_a_dst2': 'ad2', 'L1_gnn_b2': 'gb2'}


def kernel(**inputs):
    import numpy as _np
    import concourse.bacc as _bacc
    from concourse import mybir as _mybir
    from concourse.bass_utils import run_bass_kernel_spmd as _run

    nc = _bacc.Bacc("TRN2", target_bir_lowering=False, num_devices=1)
    arrays, args = {}, {}
    for name, short in _INS.items():
        a = _np.ascontiguousarray(inputs[name])
        arrays[f"in_{name}_dram"] = a
        args[short] = nc.dram_tensor(f"in_{name}_dram", a.shape, _mybir.dt.from_np(a.dtype), kind="ExternalInput").ap()
    args["out"] = nc.dram_tensor("out_0_dram", (N, D), _mybir.dt.float32, kind="ExternalOutput").ap()
    graph_kernel(nc, args)
    r = _run(nc, [arrays], core_ids=[0])
    return r.results[0]["out_0_dram"]
```
